# Optimizing a Trainium2 kernel written in Bass

```python
import numpy as np
import jax
import jax.numpy as jnp

def _softmax(x, axis=-1):
    return jax.nn.softmax(x, axis=axis)

def _gelu(x):
    return jax.nn.gelu(x, approximate=True)

def _silu(x):
    return jax.nn.silu(x)

def _sigmoid(x):
    return jax.nn.sigmoid(x)

def _layernorm(x, axis=-1, eps=1e-05):
    m = jnp.mean(x, axis=axis, keepdims=True)
    v = jnp.var(x, axis=axis, keepdims=True)
    return (x - m) / jnp.sqrt(v + eps)

def _scatter_add(tgt, idx, src, axis=0):
    return tgt.at[idx].add(src)

def _segment_sum(src, seg, n):
    return jax.ops.segment_sum(src, seg, n)
kernel_name = 'mk_adaln_d2_jaxref_r4_bbb41d'

def setup_inputs(seed: int=0):
    np.random.seed(seed)
    _w = jnp.asarray

    def _L0_attn_setup():
        import math
        import jax, jax.numpy as jnp
        import numpy as np
        B, S, D, H = (2, 512, 256, 16)
        HD = D // H
        key = jax.random.key(seed)
        k1, k2, k3 = jax.random.split(key, 3)
        h = jax.random.normal(k1, (B, S, D), dtype=jnp.float32)
        Wqvk = jax.random.normal(k2, (D, 3 * D), dtype=jnp.float32) * (1.0 / math.sqrt(D))
        Wo = jax.random.normal(k3, (D, D), dtype=jnp.float32) * (1.0 / math.sqrt(D))
        return {'h': h, 'Wqvk': Wqvk, 'Wo': Wo}
    _L0_attn_in = _L0_attn_setup()

    def _L0_ffn_setup():
        import jax, jax.numpy as jnp
        import numpy as np
        D_MODEL = 256
        key = jax.random.key(seed)
        k_x, k_w, k_a1, k_a2 = jax.random.split(key, 4)
        x = jax.random.normal(k_x, (4, 512, D_MODEL), dtype=jnp.float32)
        weight = jax.random.normal(k_w, (D_MODEL, D_MODEL), dtype=jnp.float32) * 0.02
        aux_weight1 = jax.random.normal(k_a1, (D_MODEL, D_MODEL), dtype=jnp.float32) * 0.02
        aux_weight2 = jax.random.normal(k_a2, (D_MODEL, D_MODEL), dtype=jnp.float32) * 0.02
        bias = jnp.zeros((D_MODEL,), dtype=jnp.float32)
        return {'x': x, 'weight': weight, 'aux_weight1': aux_weight1, 'aux_weight2': aux_weight2, 'bias': bias}
    _L0_ffn_in = _L0_ffn_setup()
    _L0_c = _w((lambda *s: np.random.randn(*s).astype(np.float32) * 0.05)(8, 256))
    _L0_wmod = _w((lambda *s: np.random.randn(*s).astype(np.float32) * 0.05)(256, 6 * 256) * 256 ** (-0.5))

    def _L1_attn_setup():
        import jax, jax.numpy as jnp
        import numpy as np
        LN_EPS = 1e-05

        def _layernorm(x, g, b):
            m = jnp.mean(x, axis=-1, keepdims=True)
            v = jnp.mean((x - m) ** 2, axis=-1, keepdims=True)
            return (x - m) / jnp.sqrt(v + LN_EPS) * g + b

        def _eigenstate_fft(log_decay, frequency, beta_r, beta_i):
            B, T, K = beta_r.shape
            mag = jax.nn.sigmoid(log_decay)
            n = jnp.arange(T, dtype=beta_r.dtype)
            mag_pow = mag[None, :] ** n[:, None]
            phase = n[:, None] * frequency[None, :]
            kern = mag_pow * (jnp.cos(phase) + 1j * jnp.sin(phase))
            beta = beta_r + 1j * beta_i
            beta_p = jnp.pad(beta, ((0, 0), (0, T), (0, 0)))
            kern_p = jnp.pad(kern, ((0, T), (0, 0)))
            c = jnp.fft.ifft(jnp.fft.fft(beta_p, axis=1) * jnp.fft.fft(kern_p, axis=0)[None], axis=1)[:, :T, :]
            return (c.real.astype(beta_r.dtype), c.imag.astype(beta_r.dtype))

        def _reference_tuple_inner(x, in_proj_w, log_decay, frequency, coupling, out_proj_w, gate_w, gate_b, n1_g, n1_b, n2_g, n2_b, mlp_w1, mlp_b1, mlp_w2, mlp_b2):
            B, T, D = x.shape
            H, Kh, _ = coupling.shape
            K = H * Kh
            xn = _layernorm(x, n1_g, n1_b)
            beta = jnp.einsum('btd,kd->btk', xn, in_proj_w)
            br, bi = (beta[..., :K], beta[..., K:])
            cr, ci = _eigenstate_fft(log_decay, frequency, br, bi)
            cr_h = cr.reshape(B, T, H, Kh)
            ci_h = ci.reshape(B, T, H, Kh)
            cr = jnp.einsum('hjk,bthk->bthj', coupling, cr_h).reshape(B, T, K)
            ci = jnp.einsum('hjk,bthk->bthj', coupling, ci_h).reshape(B, T, K)
            eig = jnp.concatenate([cr, ci], axis=-1)
            out = jnp.einsum('btk,dk->btd', eig, out_proj_w)
            h = jax.nn.sigmoid(jnp.einsum('btd,ed->bte', xn, gate_w) + gate_b) * out
            x = x + h
            x2 = _layernorm(x, n2_g, n2_b)
            hid = jax.nn.silu(jnp.einsum('btd,md->btm', x2, mlp_w1) + mlp_b1)
            x = x + jnp.einsum('btm,dm->btd', hid, mlp_w2) + mlp_b2
            return (x, eig)
        key = jax.random.key(seed)
        ks = jax.random.split(key, 12)
        B, T, D, K, H = (4, 1024, 256, 64, 4)
        Kh = K // H
        M = 4 * D
        f32 = jnp.float32
        inp = {'x': jax.random.normal(ks[0], (B, T, D), f32), 'in_proj_w': jax.random.normal(ks[1], (2 * K, D), f32) / np.sqrt(D), 'log_decay': jax.random.uniform(ks[2], (K,), f32, -3.0, -0.1), 'frequency': jnp.linspace(0.0, 2 * np.pi * (1 - 1.0 / K), K, dtype=f32), 'coupling': jnp.eye(Kh, dtype=f32)[None] + 0.01 * jax.random.normal(ks[3], (H, Kh, Kh), f32) / np.sqrt(Kh), 'out_proj_w': jax.random.normal(ks[4], (D, 2 * K), f32) / np.sqrt(2 * K), 'gate_w': jax.random.normal(ks[5], (D, D), f32) / np.sqrt(D), 'gate_b': jnp.full((D,), -2.0, f32), 'n1_g': jnp.ones((D,), f32), 'n1_b': jnp.zeros((D,), f32), 'n2_g': jnp.ones((D,), f32), 'n2_b': jnp.zeros((D,), f32), 'mlp_w1': jax.random.normal(ks[6], (M, D), f32) / np.sqrt(D), 'mlp_b1': jnp.zeros((M,), f32), 'mlp_w2': jax.random.normal(ks[7], (D, M), f32) / np.sqrt(M), 'mlp_b2': jnp.zeros((D,), f32)}
        return inp
    _L1_attn_in = _L1_attn_setup()

    def _L1_ffn_setup():
        import jax, jax.numpy as jnp
        import numpy as np
        from jax import lax
        D = 256
        H = 1024
        E = 8
        TOPK = 2
        key = jax.random.key(seed)
        ks = jax.random.split(key, 7)
        s = 0.02
        return {'x': jax.random.normal(ks[0], (2, 512, D), dtype=jnp.float32), 'W1': jax.random.normal(ks[1], (E, D, H), dtype=jnp.float32) * s, 'b1': jnp.zeros((E, H), dtype=jnp.float32), 'W2': jax.random.normal(ks[2], (E, H, D), dtype=jnp.float32) * s, 'b2': jnp.zeros((E, D), dtype=jnp.float32), 'Wr': jax.random.normal(ks[3], (D, E), dtype=jnp.float32) * s, 'br': jnp.zeros((E,), dtype=jnp.float32)}
    _L1_ffn_in = _L1_ffn_setup()
    _L1_c = _w((lambda *s: np.random.randn(*s).astype(np.float32) * 0.05)(8, 256))
    _L1_wmod = _w((lambda *s: np.random.randn(*s).astype(np.float32) * 0.05)(256, 6 * 256) * 256 ** (-0.5))
    _d = {'L0_attn_h': _L0_attn_in['h'], 'L0_attn_Wqvk': _L0_attn_in['Wqvk'], 'L0_attn_Wo': _L0_attn_in['Wo'], 'L0_ffn_weight': _L0_ffn_in['weight'], 'L0_ffn_aux_weight1': _L0_ffn_in['aux_weight1'], 'L0_ffn_aux_weight2': _L0_ffn_in['aux_weight2'], 'L0_ffn_bias': _L0_ffn_in['bias'], 'L0_c': _L0_c, 'L0_wmod': _L0_wmod, 'L1_attn_in_proj_w': _L1_attn_in['in_proj_w'], 'L1_attn_log_decay': _L1_attn_in['log_decay'], 'L1_attn_frequency': _L1_attn_in['frequency'], 'L1_attn_coupling': _L1_attn_in['coupling'], 'L1_attn_out_proj_w': _L1_attn_in['out_proj_w'], 'L1_attn_gate_w': _L1_attn_in['gate_w'], 'L1_attn_gate_b': _L1_attn_in['gate_b'], 'L1_attn_n1_g': _L1_attn_in['n1_g'], 'L1_attn_n1_b': _L1_attn_in['n1_b'], 'L1_attn_n2_g': _L1_attn_in['n2_g'], 'L1_attn_n2_b': _L1_attn_in['n2_b'], 'L1_attn_mlp_w1': _L1_attn_in['mlp_w1'], 'L1_attn_mlp_b1': _L1_attn_in['mlp_b1'], 'L1_attn_mlp_w2': _L1_attn_in['mlp_w2'], 'L1_attn_mlp_b2': _L1_attn_in['mlp_b2'], 'L1_ffn_W1': _L1_ffn_in['W1'], 'L1_ffn_b1': _L1_ffn_in['b1'], 'L1_ffn_W2': _L1_ffn_in['W2'], 'L1_ffn_b2': _L1_ffn_in['b2'], 'L1_ffn_Wr': _L1_ffn_in['Wr'], 'L1_ffn_br': _L1_ffn_in['br'], 'L1_c': _L1_c, 'L1_wmod': _L1_wmod}
    _x0 = _d['L0_attn_h']
    _d['L0_attn_h'] = jax.random.normal(jax.random.fold_in(jax.random.key(seed), 1), (8, 512, 256), dtype=_x0.dtype)
    del _x0
    return _d

def reference(L0_attn_h, L0_attn_Wqvk, L0_attn_Wo, L0_ffn_weight, L0_ffn_aux_weight1, L0_ffn_aux_weight2, L0_ffn_bias, L0_c, L0_wmod, L1_attn_in_proj_w, L1_attn_log_decay, L1_attn_frequency, L1_attn_coupling, L1_attn_out_proj_w, L1_attn_gate_w, L1_attn_gate_b, L1_attn_n1_g, L1_attn_n1_b, L1_attn_n2_g, L1_attn_n2_b, L1_attn_mlp_w1, L1_attn_mlp_b1, L1_attn_mlp_w2, L1_attn_mlp_b2, L1_ffn_W1, L1_ffn_b1, L1_ffn_W2, L1_ffn_b2, L1_ffn_Wr, L1_ffn_br, L1_c, L1_wmod):

    def _L0_attn_ref(h, Wqvk, Wo):
        import math
        import jax, jax.numpy as jnp
        import numpy as np
        B, S, D, H = (2, 512, 256, 16)
        HD = D // H
        b, s, d = h.shape
        qvk = (h @ Wqvk).reshape(b, s, 3, H, HD)
        q, v, k = (qvk[:, :, 0], qvk[:, :, 1], qvk[:, :, 2])
        scores = jnp.einsum('bshi,bthi->bsth', q, k)
        mask = jnp.where(jnp.arange(s)[None, :] > jnp.arange(s)[:, None], jnp.float32(-jnp.inf), jnp.float32(0.0))
        scores = scores + mask[None, :, :, None]
        scores = scores / math.sqrt(d)
        weights = jax.nn.softmax(scores, axis=2)
        wv = jnp.einsum('bsth,bthi->bshi', weights, v).reshape(b, s, d)
        return wv @ Wo

    def _L0_ffn_ref(x, weight, aux_weight1, aux_weight2, bias):
        import jax, jax.numpy as jnp
        import numpy as np
        D_MODEL = 256
        h = jnp.einsum('btc,cd->btd', x, weight)
        h = jnp.einsum('btc,cd->btd', h, aux_weight1)
        h = jnp.einsum('btc,cd->btd', h, aux_weight2)
        return jnp.tanh(h + bias)

    def _L1_attn_ref(x, in_proj_w, log_decay, frequency, coupling, out_proj_w, gate_w, gate_b, n1_g, n1_b, n2_g, n2_b, mlp_w1, mlp_b1, mlp_w2, mlp_b2):
        import jax, jax.numpy as jnp
        import numpy as np
        LN_EPS = 1e-05

        def _layernorm(x, g, b):
            m = jnp.mean(x, axis=-1, keepdims=True)
            v = jnp.mean((x - m) ** 2, axis=-1, keepdims=True)
            return (x - m) / jnp.sqrt(v + LN_EPS) * g + b

        def _eigenstate_fft(log_decay, frequency, beta_r, beta_i):
            B, T, K = beta_r.shape
            mag = jax.nn.sigmoid(log_decay)
            n = jnp.arange(T, dtype=beta_r.dtype)
            mag_pow = mag[None, :] ** n[:, None]
            phase = n[:, None] * frequency[None, :]
            kern = mag_pow * (jnp.cos(phase) + 1j * jnp.sin(phase))
            beta = beta_r + 1j * beta_i
            beta_p = jnp.pad(beta, ((0, 0), (0, T), (0, 0)))
            kern_p = jnp.pad(kern, ((0, T), (0, 0)))
            c = jnp.fft.ifft(jnp.fft.fft(beta_p, axis=1) * jnp.fft.fft(kern_p, axis=0)[None], axis=1)[:, :T, :]
            return (c.real.astype(beta_r.dtype), c.imag.astype(beta_r.dtype))

        def _reference_tuple_inner(x, in_proj_w, log_decay, frequency, coupling, out_proj_w, gate_w, gate_b, n1_g, n1_b, n2_g, n2_b, mlp_w1, mlp_b1, mlp_w2, mlp_b2):
            B, T, D = x.shape
            H, Kh, _ = coupling.shape
            K = H * Kh
            xn = _layernorm(x, n1_g, n1_b)
            beta = jnp.einsum('btd,kd->btk', xn, in_proj_w)
            br, bi = (beta[..., :K], beta[..., K:])
            cr, ci = _eigenstate_fft(log_decay, frequency, br, bi)
            cr_h = cr.reshape(B, T, H, Kh)
            ci_h = ci.reshape(B, T, H, Kh)
            cr = jnp.einsum('hjk,bthk->bthj', coupling, cr_h).reshape(B, T, K)
            ci = jnp.einsum('hjk,bthk->bthj', coupling, ci_h).reshape(B, T, K)
            eig = jnp.concatenate([cr, ci], axis=-1)
            out = jnp.einsum('btk,dk->btd', eig, out_proj_w)
            h = jax.nn.sigmoid(jnp.einsum('btd,ed->bte', xn, gate_w) + gate_b) * out
            x = x + h
            x2 = _layernorm(x, n2_g, n2_b)
            hid = jax.nn.silu(jnp.einsum('btd,md->btm', x2, mlp_w1) + mlp_b1)
            x = x + jnp.einsum('btm,dm->btd', hid, mlp_w2) + mlp_b2
            return (x, eig)
        return _reference_tuple_inner(x, in_proj_w, log_decay, frequency, coupling, out_proj_w, gate_w, gate_b, n1_g, n1_b, n2_g, n2_b, mlp_w1, mlp_b1, mlp_w2, mlp_b2)[0]

    def _L1_ffn_ref(x, W1, b1, W2, b2, Wr, br):
        import jax, jax.numpy as jnp
        import numpy as np
        from jax import lax
        D = 256
        H = 1024
        E = 8
        TOPK = 2
        B, S, _ = x.shape
        xf = x.reshape(-1, D)
        logits = xf @ Wr + br
        topv, _ = lax.top_k(logits, TOPK)
        thresh = topv[:, TOPK - 1:TOPK]
        masked = jnp.where(logits >= thresh, logits, -jnp.inf)
        weights = jax.nn.softmax(masked, axis=-1)
        h = jax.nn.gelu(jnp.einsum('td,edh->eth', xf, W1) + b1[:, None, :], approximate=False)
        expert_out = jnp.einsum('eth,ehd->etd', h, W2) + b2[:, None, :]
        out = jnp.einsum('etd,te->td', expert_out, weights)
        return out.reshape(B, S, D)
    x = L0_attn_h
    mod = (_silu(L0_c) @ L0_wmod).reshape(L0_c.shape[0], 6, 1, -1)
    sa, ca, ga, sb, cb, gb = (mod[:, 0], mod[:, 1], mod[:, 2], mod[:, 3], mod[:, 4], mod[:, 5])
    ga = (2 * (ga >= 0) - 1) * jnp.maximum(jnp.abs(ga), 0.25)
    gb = (2 * (gb >= 0) - 1) * jnp.maximum(jnp.abs(gb), 0.25)
    h = _layernorm(x, axis=-1) * (1 + ca) + sa
    x = x + ga * _L0_attn_ref(h, L0_attn_Wqvk, L0_attn_Wo)
    h = _layernorm(x, axis=-1) * (1 + cb) + sb
    x = x + gb * _L0_ffn_ref(h, L0_ffn_weight, L0_ffn_aux_weight1, L0_ffn_aux_weight2, L0_ffn_bias)
    mod = (_silu(L1_c) @ L1_wmod).reshape(L1_c.shape[0], 6, 1, -1)
    sa, ca, ga, sb, cb, gb = (mod[:, 0], mod[:, 1], mod[:, 2], mod[:, 3], mod[:, 4], mod[:, 5])
    ga = (2 * (ga >= 0) - 1) * jnp.maximum(jnp.abs(ga), 0.25)
    gb = (2 * (gb >= 0) - 1) * jnp.maximum(jnp.abs(gb), 0.25)
    h = _layernorm(x, axis=-1) * (1 + ca) + sa
    x = x + ga * _L1_attn_ref(h, L1_attn_in_proj_w, L1_attn_log_decay, L1_attn_frequency, L1_attn_coupling, L1_attn_out_proj_w, L1_attn_gate_w, L1_attn_gate_b, L1_attn_n1_g, L1_attn_n1_b, L1_attn_n2_g, L1_attn_n2_b, L1_attn_mlp_w1, L1_attn_mlp_b1, L1_attn_mlp_w2, L1_attn_mlp_b2)
    h = _layernorm(x, axis=-1) * (1 + cb) + sb
    x = x + gb * _L1_ffn_ref(h, L1_ffn_W1, L1_ffn_b1, L1_ffn_W2, L1_ffn_b2, L1_ffn_Wr, L1_ffn_br)
    return x

_drawn_inputs = setup_inputs


def setup_inputs(seed=0):
    import zlib

    import numpy as np

    out = dict(_drawn_inputs(seed))
    spreads = {'L0_ffn_bias': (0.0, 0.306),
     'L1_attn_gate_b': (-2.0, 0.6),
     'L1_attn_n1_g': (1.0, 0.6),
     'L1_attn_n1_b': (0.0, 0.8),
     'L1_attn_n2_g': (1.0, 0.2),
     'L1_attn_n2_b': (0.0, 0.568),
     'L1_attn_mlp_b1': (0.0, 0.537),
     'L1_attn_mlp_b2': (0.0, 0.318),
     'L1_ffn_b1': (0.0, 0.8),
     'L1_ffn_b2': (0.0, 0.471),
     'L1_ffn_br': (0.0, 0.603)}
    factors = {'L0_ffn_weight': 6.82,
     'L0_ffn_aux_weight1': 6.845,
     'L0_ffn_aux_weight2': 6.881,
     'L1_attn_log_decay': 5.444,
     'L1_attn_frequency': 2.683,
     'L1_ffn_W1': 3.043,
     'L1_ffn_W2': 2.842}
    for name, (base, spread) in spreads.items():
        noise = np.random.default_rng([zlib.crc32(name.encode()), seed]).standard_normal(out[name].shape)
        drawn = base * np.exp(spread * noise) if base else spread * noise
        out[name] = jnp.asarray(drawn.astype(out[name].dtype))
    for name, factor in factors.items():
        out[name] = (out[name] * factor).astype(out[name].dtype)
    return out
```

```python
import numpy as np
import concourse.bass as bass
from concourse import mybir
from contextlib import ExitStack

F32 = mybir.dt.float32
F32R = mybir.dt.float32r
BF16 = mybir.dt.bfloat16
I32 = mybir.dt.int32
ACT = mybir.ActivationFunctionType
ALU = mybir.AluOpType
AX = mybir.AxisListType

B, S, D, H = 8, 512, 256, 16
HD = D // H
P = 128
NT = S // P
NC = D // P
T = B * NT
G = H // 4
TERMS = 6
Q_RUNS = (slice(0, 3), slice(0, 2), slice(0, 1))
K_RUNS = (slice(0, 2), slice(0, 2), slice(0, 3, 2))
LOADS = len(Q_RUNS) + len(K_RUNS)
KR = TERMS * HD
EPS = 1e-5
LOW = -3.0e38


def wait(eng, sem, value):
    if isinstance(value, int) and value <= 0:
        return
    eng.wait_ge(sem, value)


def hold(eng, K):
    eng.sem_inc(K["held"], 1)


def passes(eng, n, body, last_apart=False):
    body(0)
    with eng.Fori(1, n - 1 if last_apart else n) as i:
        body(i)
    if last_apart:
        body(n - 1)


def at(it, u, j=0, n=1):
    return it * (2 * n) + (2 * j + u + 1)


class Order:

    def __init__(self, eng, sem, per_pass):
        self.eng, self.sem, self.per_pass, self.n, self.base = eng, sem, per_pass, 0, 0

    def at(self, i):
        self.base, self.n = i * self.per_pass, 0

    def link(self, ins):
        self.n += 1
        ins.then_inc(self.sem, 1)
        self.eng.wait_ge(self.sem, self.base + self.n)

    def done(self):
        assert self.n == self.per_pass, (self.n, self.per_pass)


def setup_modulation(nc, K):
    with ExitStack() as ctx:
        sb = lambda name, shape, dt=F32: ctx.enter_context(nc.sbuf_tensor(name, shape, dt))
        wmod = sb("wmod", [P, 2, NC, 6 * D])
        ct = sb("ct", [P, 2, NC, B])
        silu = sb("silu", [P, 2, NC, B])
        rows = sb("rows", [B, 2, 6 * D])
        sign = sb("sign", [B, 2, 6, D])
        size = sb("size", [B, 2, 6, D])
        ps_col = [ctx.enter_context(nc.psum_tensor(f"ps_col{l}", [P, 512], F32)) for l in range(2)]
        ps_row = [ctx.enter_context(nc.psum_tensor(f"ps_row{j}", [P, 512], F32)) for j in range(6)]
        w_in = nc.alloc_semaphore("mod_w_in")
        x_in = nc.alloc_semaphore("mod_x_in")
        silu_ready = nc.alloc_semaphore("mod_silu_ready")
        cols_ready = nc.alloc_semaphore("mod_cols_ready")
        rows_ready = nc.alloc_semaphore("mod_rows_ready")
        fixed = nc.alloc_semaphore("mod_fixed")
        stored = nc.alloc_semaphore("mod_stored")
        squares = nc.alloc_semaphore("mod_squares")
        order = nc.alloc_semaphore("mod_dve_order")

        with nc.Block() as block:
            @block.sync
            def _(sp):
                for l in range(2):
                    sp.dma_start(ct[:, l], K[f"ct{l}"]).then_inc(w_in, 16)
                    sp.dma_start(wmod[:, l], K[f"wmod{l}"].rearrange("(c p) n -> p c n", p=P)).then_inc(w_in, 16)
                for b in range(B):
                    sp.dma_start(K["x_sb"][:, b * NT:(b + 1) * NT, :],
                                 K["x"][b].rearrange("(i p) d -> p i d", p=P)).then_inc(x_in, 16)
                sp.wait_ge(fixed, 2)
                sp.dma_start(K["mod_rows"].rearrange("l b n -> b l n"), rows[:]).then_inc(stored, 16)
                sp.wait_ge(stored, 16)
                sp.wait_ge(x_in, 16 * B)

            @block.scalar
            def _(act):
                act.wait_ge(w_in, 64)
                nc.scalar.activation(silu[:], ct[:], ACT.Silu).then_inc(silu_ready, 1)

            @block.tensor
            def _(pe):
                pe.wait_ge(silu_ready, 1)
                for l in range(2):
                    for m in range(12):
                        for c in range(NC):
                            last = nc.tensor.matmul(ps_col[l][:, m * B:(m + 1) * B], wmod[:, l, c, m * P:(m + 1) * P],
                                                    silu[:, l, c, :], start=(c == 0), stop=(c == NC - 1))
                    last.then_inc(cols_ready, 1)
                    for j in range(3):
                        for c in range(NC):
                            last = nc.tensor.matmul(ps_row[3 * l + j][0:B, :], silu[:, l, c, :],
                                                    wmod[:, l, c, 512 * j:512 * j + 512], start=(c == 0), stop=(c == NC - 1))
                    last.then_inc(rows_ready, 1)

            @block.vector
            def _(dve):
                ord_ = Order(dve, order, 0)
                for l in range(2):
                    dve.wait_ge(cols_ready, l + 1)
                    col = K["mod_cols"][:, l]
                    for j in range(6):
                        for c in range(NC):
                            m = j * NC + c
                            nc.vector.tensor_scalar(col[:, m, :], ps_col[l][:, m * B:(m + 1) * B],
                                                    1.0 if j in (1, 4) else 0.0, None, ALU.add)
                    dve.wait_ge(rows_ready, l + 1)
                    for j in range(3):
                        ord_.link(nc.vector.tensor_copy(rows[:, l, 512 * j:512 * j + 512], ps_row[3 * l + j][0:B, :]))
                    row = rows[:, l, :].rearrange("b (j d) -> b j d", d=D)
                    for j in (2, 5):
                        ord_.link(nc.vector.tensor_scalar(sign[:, l, j], row[:, j], 0.0, 2.0, ALU.is_ge, ALU.mult))
                        ord_.link(nc.vector.scalar_tensor_tensor(size[:, l, j], row[:, j], -1.0, row[:, j], ALU.mult, ALU.max))
                        ord_.link(nc.vector.tensor_scalar(size[:, l, j], size[:, l, j], 0.25, None, ALU.max))
                        ord_.link(nc.vector.scalar_tensor_tensor(row[:, j], sign[:, l, j], -1.0, size[:, l, j], ALU.add, ALU.mult))
                    ord_.link(nc.vector.tensor_scalar(row[:, 4], row[:, 4], 1.0, None, ALU.add))
                    nc.vector.tensor_scalar(row[:, 1], row[:, 1], 1.0, None, ALU.add).then_inc(fixed, 1)

            @block.gpsimd
            def _(pool):
                nc.gpsimd.memset(K["ident"][:], 0.0).then_inc(squares, 1)
                nc.gpsimd.memset(K["identb"][:], 0.0).then_inc(squares, 1)
                nc.gpsimd.memset(K["causal"][:], 0.0).then_inc(squares, 1)
                pool.wait_ge(squares, 3)
                for m in ("ident", "identb"):
                    nc.gpsimd.affine_select(out=K[m][:], in_=K[m][:], compare_op=ALU.not_equal, fill=1.0, base=0,
                                            pattern=[[-1, P]], channel_multiplier=1).then_inc(squares, 1)
                tri = K["causal"][:, S - P:S]
                nc.gpsimd.affine_select(out=tri, in_=tri, compare_op=ALU.is_ge, fill=LOW, base=0,
                                        pattern=[[-1, P]], channel_multiplier=1).then_inc(squares, 1)
                pool.wait_ge(squares, 6)


def layer_norm(nc, K, dve, link, src, stats, mv, root, dst, ready):
    n = 2 * NT
    v, y, t = root[:, 0], root[:, 1], root[:, 2]
    hold(dve, K)
    for i in range(n):
        last = nc.vector.bn_stats(stats[:, i, :], src[i])
    link(last)
    hold(dve, K)
    for i in range(n):
        last = nc.vector.bn_aggr(mv[:, i, :], stats[:, i, :])
    link(last)
    link(nc.vector.tensor_scalar(v, mv[:, :, 1], EPS, None, ALU.add))
    link(nc.vector.tensor_scalar(t.bitcast(I32), v.bitcast(I32), 1, None, ALU.logical_shift_right))
    link(nc.vector.tensor_scalar(y.bitcast(I32), t.bitcast(I32), -1.0, float(0x5F3759DF), ALU.mult, ALU.add))
    for _ in range(3):
        link(nc.vector.tensor_tensor(t, y, y, ALU.mult))
        link(nc.vector.scalar_tensor_tensor(t, t, -0.5, v, ALU.mult, ALU.mult))
        link(nc.vector.scalar_tensor_tensor(y, t, 1.5, y, ALU.add, ALU.mult))
    for i in range(n):
        last = nc.vector.tensor_scalar(dst[i], src[i], mv[:, i, 0:1], y[:, i:i + 1], ALU.subtract, ALU.mult)
        if i % NT == NT - 1:
            last.then_inc(ready, 1)


LN_LINKS = 2 + 3 + 9


def project_qkv(nc, K):
    with ExitStack() as ctx:
        sb = lambda name, shape, dt=F32: ctx.enter_context(nc.sbuf_tensor(name, shape, dt))
        w = sb("qkv_w", [P, NC, 3 * D])
        w_hi = sb("qkv_w_hi", [P, NC, 3 * D], F32R)
        w_lo = sb("qkv_w_lo", [P, NC, 3 * D], F32R)
        two = range(2)
        stats, mv, root = sb("q_stats", [P, 2 * NT, 6]), sb("q_mv", [P, 2 * NT, 2]), sb("q_root", [P, 3, 2 * NT])
        xn = [sb(f"q_xn{u}", [P, NT, D]) for u in two]
        mod = [sb(f"q_mod{u}", [P, 12, 1]) for u in two]
        h = [sb(f"q_h{u}", [P, NC, S]) for u in two]
        h_hi = [sb(f"q_h_hi{u}", [P, NC, S], F32R) for u in two]
        h_lo = [sb(f"q_h_lo{u}", [P, NC, S], F32R) for u in two]
        rest = [sb(f"q_rest{u}", [P, 4, S]) for u in two]
        parts = [sb(f"q_parts{u}", [P, 4, 3, S], BF16) for u in two]
        ps = [[ctx.enter_context(nc.psum_tensor(f"q_ps{u}{j}", [P, 512], F32)) for j in range(4)] for u in two]
        sem = nc.alloc_semaphore
        w_in, w_split, mod_ready = sem("q_w_in"), sem("q_w_split"), sem("q_mod_ready")
        xn_ready, xt_ready, h_ready, hlo_ready = sem("q_xn_ready"), sem("q_xt_ready"), sem("q_h_ready"), sem("q_hlo_ready")
        qk_ready, hi_ready, rest_ready, mid_ready, lo_ready = (sem("q_qk_ready"), sem("q_hi_ready"), sem("q_rest_ready"),
                                                               sem("q_mid_ready"), sem("q_lo_ready"))
        v_ready, v_kept = sem("q_v_ready"), sem("q_v_kept")
        parts_out = [sem(f"q_parts_out{u}") for u in two]
        order = sem("q_dve_order")
        COLS = (0, P, 2 * D, 2 * D + P)

        with nc.Block() as block:
            @block.sync
            def _(sp):
                sp.dma_start(w[:], K["wqkv"].rearrange("(c p) n -> p c n", p=P)).then_inc(w_in, 16)

                def body(it):
                    for m in range(4):
                        for u in two:
                            sp.wait_ge(lo_ready, at(it, u, m, 4))
                            for g in range(2):
                                for a in range(3):
                                    quad = (2 * it + u) * G + (m % 2) * 2 + g
                                    sp.dma_start(K["qk_parts"][bass.ds(quad * 2 + m // 2, 1), a].rearrange("o d h s -> (o h) d s"),
                                                 parts[u][64 * g:64 * g + 64, m, a]).then_inc(parts_out[u], 16)
                passes(sp, B // 2, body)
                for u in two:
                    sp.wait_ge(parts_out[u], 16 * 24 * (B // 2))

            @block.gpsimd
            def _(pool):
                def body(it):
                    for u in two:
                        wait(pool, h_ready, at(it - 1, u))
                        hold(pool, K)
                        nc.gpsimd.tensor_copy(mod[u][:], K["mod_cols"][:, 0, :, bass.ds(2 * it + u, 1)]).then_inc(mod_ready, 1)
                    for m in range(4):
                        for u in two:
                            wait(pool, parts_out[u], 384 * it)
                            pool.wait_ge(rest_ready, at(it, u, m, 4))
                            hold(pool, K)
                            nc.gpsimd.tensor_copy(parts[u][:, m, 1], rest[u][:, m]).then_inc(mid_ready, 1)
                passes(pool, B // 2, body)

            @block.scalar
            def _(act):
                def body(it):
                    for u in two:
                        act.wait_ge(xt_ready, at(it, u))
                        act.wait_ge(mod_ready, at(it, u))
                        wait(act, v_ready, at(it - 1, u, 1, 2))
                        for c in range(NC):
                            sc, sh = mod[u][:, 2 + c], mod[u][:, c]
                            nc.scalar.activation(h[u][:, c], ps[u][c][:], ACT.Identity, bias=sh, scale=sc)
                        for c in range(NC):
                            sc, sh = mod[u][:, 2 + c], mod[u][:, c]
                            last = nc.scalar.activation(h_hi[u][:, c], ps[u][c][:], ACT.Identity, bias=sh, scale=sc)
                        last.then_inc(h_ready, 1)
                    for m in range(4):
                        for u in two:
                            act.wait_ge(qk_ready, at(it, u, m, 4))
                            wait(act, parts_out[u], 384 * it)
                            nc.scalar.activation(parts[u][:, m, 0], ps[u][(m + 2) % 4][:], ACT.Copy).then_inc(hi_ready, 1)
                    for j in two:
                        for u in two:
                            act.wait_ge(v_ready, at(it, u, j, 2))
                            nc.scalar.activation(K["v"][:, bass.ds((2 * it + u) * NT + 2 * j, 2), :],
                                                 ps[u][2 + j][:].rearrange("p (i d) -> p i d", i=2), ACT.Copy).then_inc(v_kept, 1)
                passes(act, B // 2, body)

            @block.vector
            def _(dve):
                dve.wait_ge(w_in, 16)
                for c in range(NC):
                    nc.vector.tensor_copy(w_hi[:, c], w[:, c]).then_inc(w_split, 1)
                dve.wait_ge(w_split, 2)
                nc.vector.tensor_tensor(w_lo[:], w[:], w_hi[:].bitcast(F32), ALU.subtract).then_inc(w_split, 1)

                ord_ = Order(dve, order, LN_LINKS)
                def body(it):
                    ord_.at(it)
                    for u in two:
                        wait(dve, xt_ready, at(it - 1, u))
                    layer_norm(nc, K, dve, ord_.link, [K["x_sb"][:, bass.ds(2 * NT * it + i, 1), :] for i in range(2 * NT)], stats, mv, root,
                               [xn[u][:, i, :] for u in two for i in range(NT)], xn_ready)
                    for u in two:
                        dve.wait_ge(h_ready, at(it, u))
                        nc.vector.tensor_tensor(h_lo[u][:], h[u][:], h_hi[u][:].bitcast(F32), ALU.subtract).then_inc(hlo_ready, 1)
                    for m in range(5):
                        for u in two:
                            if m < 4:
                                dve.wait_ge(hi_ready, at(it, u, m, 4))
                                nc.vector.tensor_tensor(rest[u][:, m], ps[u][(m + 2) % 4][:], parts[u][:, m, 0],
                                                        ALU.subtract).then_inc(rest_ready, 1)
                        for u in two:
                            if m > 0:
                                dve.wait_ge(mid_ready, at(it, u, m - 1, 4))
                                nc.vector.tensor_tensor(parts[u][:, m - 1, 2], rest[u][:, m - 1], parts[u][:, m - 1, 1],
                                                        ALU.subtract).then_inc(lo_ready, 1)
                    ord_.done()
                passes(dve, B // 2, body)

            @block.tensor
            def _(pe):
                pe.wait_ge(w_split, 3)
                def body(it):
                    for u in two:
                        pe.wait_ge(xn_ready, at(it, u))
                        wait(pe, rest_ready, at(it - 1, u, 3, 4))
                        for c in range(NC):
                            for i in range(NT):
                                last = nc.tensor.transpose(ps[u][c][:, i * P:(i + 1) * P], xn[u][:, i, c * P:(c + 1) * P], K["ident"][:])
                        last.then_inc(xt_ready, 1)
                    for m in range(4):
                        for u in two:
                            pe.wait_ge(hlo_ready, at(it, u))
                            if m < 2:
                                wait(pe, v_kept, at(it - 1, u, m, 2))
                            bank, n = ps[u][(m + 2) % 4][:], 0
                            for c in range(NC):
                                for a, x in ((w_hi, h_hi), (w_hi, h_lo), (w_lo, h_hi)):
                                    last = nc.tensor.matmul(bank, a[:, c, COLS[m]:COLS[m] + P], x[u][:, c], start=(n == 0), stop=(n == 5))
                                    n += 1
                            last.then_inc(qk_ready, 1)
                    for j in two:
                        for u in two:
                            pe.wait_ge(rest_ready, at(it, u, j, 4))
                            for i in two:
                                n = 0
                                for c in range(NC):
                                    for x, a in ((h_hi, w_hi), (h_lo, w_hi), (h_hi, w_lo)):
                                        t = (2 * j + i) * P
                                        last = nc.tensor.matmul(ps[u][2 + j][:, i * D:(i + 1) * D], x[u][:, c, t:t + P],
                                                                a[:, c, D:2 * D], start=(n == 0), stop=(n == 5))
                                        n += 1
                            last.then_inc(v_ready, 1)
                passes(pe, B // 2, body)


EXP_JOBS = (((0, 0),), ((1, 0), (3, 384)), ((2, 0),))
MAX_JOBS = (((3, 0),), ((2, 0), (0, 384)), ((1, 0),))
EXP_AT = (0, 512, 1024, 896)
COLS = 1280


def attend(nc, K):
    with ExitStack() as ctx:
        sb = lambda name, shape, dt=F32: ctx.enter_context(nc.sbuf_tensor(name, shape, dt))
        ps = lambda name: ctx.enter_context(nc.psum_tensor(name, [P, 512], F32))
        sem = nc.alloc_semaphore
        NB = 4
        q_st = [sb(f"q_stack{g}", [KR + 3, 4, S], BF16) for g in range(NB)]
        k_st = [sb(f"k_stack{g}", [KR + 3, 4, S], BF16) for g in range(NB)]
        probs = [sb(f"probs{u}", [P, 4, COLS]) for u in range(2)]
        v1 = [sb(f"v_ones{u}", [P, NT, 4, HD + 1]) for u in range(2)]
        junk = sb("a_junk", [P, NT, S], BF16)
        mx = sb("a_mx", [P, NT, 4])
        mrest = sb("a_mrest", [P, 2, NT, 4])
        mparts = sb("a_mparts", [P, NT, 3, 4], BF16)
        mrow = sb("a_mrow", [12, S], BF16)
        ot = [sb(f"a_ot{u}", [P, S]) for u in range(2)]
        ps_max = [ps(f"a_ps_max{j}") for j in range(3)]
        ps_exp = [ps(f"a_ps_exp{j}") for j in range(3)]
        ps_out, ps_misc = ps("a_ps_out"), ps("a_ps_misc")
        ps_mt = ps_misc[:].bitcast(BF16)
        stack_in = [sem(f"a_stack_in{g}") for g in range(NB)]
        mrow_in = [sem(f"a_mrow_in{g}") for g in range(NB)]
        ot_out = [sem(f"a_ot_out{u}") for u in range(2)]
        ones_ready, v1_ready = sem("a_ones_ready"), sem("a_v1_ready")
        max_scores, max_read, mparts_ready, mt_ready, mrow_ready = (
            sem("a_max_scores"), sem("a_max_read"), sem("a_mparts_ready"), sem("a_mt_ready"), sem("a_mrow_ready"))
        exp_scores, exp_read, masked, pv_done = sem("a_exp_scores"), sem("a_exp_read"), sem("a_masked"), sem("a_pv_done")
        ot_ready = sem("a_ot_ready")
        order = sem("a_dve_order")

        with nc.Block() as block:
            @block.sync
            def _(sp):
                def load(n, g):
                    for st, a, runs in ((q_st, 0, Q_RUNS), (k_st, 1, K_RUNS)):
                        row = 0
                        for run in runs:
                            size = len(range(3)[run]) * HD
                            sp.dma_start(st[g][row:row + size, :, :].rearrange("p h s -> p (h s)"),
                                         K["qk_parts"][bass.ds(n * 2 + a, 1), run].rearrange("o a d h s -> (o a d) (h s)")
                                         if run.step is None else
                                         K["qk_parts"][bass.ds(n * 2 + a, 1), run].rearrange("o a d h s -> (o a) d (h s)")
                                         ).then_inc(stack_in[g], 16)
                            row += size

                def rows_of_max(n, g):
                    sp.wait_ge(mrow_ready, n + 1)
                    for j in range(3):
                        sp.dma_start(q_st[g][KR + j:KR + j + 1, :, :],
                                     mrow[4 * j:4 * j + 4, :]).then_inc(mrow_in[g], 16)

                def store(n, u):
                    sp.wait_ge(ot_ready, n + 1)
                    sp.dma_start(K["attended"][bass.ds(n * P, P), :], ot[u][:]).then_inc(ot_out[u], 16)

                def body(b, last=False):
                    for g in range(G):
                        n = b * G + g
                        if not (last and g > 0):
                            wait(sp, exp_scores, 12 * n)
                            load(n + 3, (g + 3) % NB)
                        if not (last and g == G - 1):
                            rows_of_max(n + 1, (g + 1) % NB)
                        if not (isinstance(n, int) and n < 2):
                            store(n - 2, g % 2)
                for g in range(3):
                    load(g, g)
                rows_of_max(0, 0)
                body(0)
                with sp.Fori(1, B - 1) as b:
                    body(b)
                body(B - 1, last=True)
                store(B * G - 2, 0)
                store(B * G - 1, 1)
                for u in range(2):
                    sp.wait_ge(ot_out[u], 16 * B * G // 2)

            @block.gpsimd
            def _(pool):
                for u in range(2):
                    nc.gpsimd.memset(v1[u][:, :, :, HD:HD + 1], 1.0).then_inc(ones_ready, 1)

                def body(b):
                    for g in range(G):
                        n, u = b * G + g, g % 2
                        wait(pool, pv_done, n - 1)
                        hold(pool, K)
                        nc.gpsimd.tensor_copy(v1[u][:, :, :, 0:HD],
                                              K["v"][:, bass.ds(b * NT, NT), g * 4 * HD:(g + 1) * 4 * HD]
                                              .rearrange("p i (h d) -> p i h d", d=HD)).then_inc(v1_ready, 1)
                        for h in range(4):
                            pool.wait_ge(exp_read, 12 * n + 3 * h + 3)
                            hold(pool, K)
                            for first in EXP_AT:
                                block_ = probs[u][:, h, first:first + P]
                                last = nc.gpsimd.affine_select(out=block_, in_=block_, compare_op=ALU.is_ge, fill=0.0, base=0,
                                                               pattern=[[1, P]], channel_multiplier=-1)
                            last.then_inc(masked, 1)
                body(0)
                with pool.Fori(1, B) as b:
                    body(b)

            @block.scalar
            def _(act):
                def keep_sums(n, u, stored):
                    act.wait_ge(pv_done, n + 1)
                    wait(act, ot_out[u], 16 * stored)
                    nc.scalar.activation(ot[u][:], ps_out[:], ACT.Copy).then_inc(ot_ready, 1)

                def copy_max_rows(n):
                    act.wait_ge(mt_ready, n + 1)
                    return nc.scalar.activation(mrow[:], ps_mt[0:12, 0:S], ACT.Copy).then_inc(mrow_ready, 1)

                def body(b, last=False):
                    for g in range(G):
                        n, u = b * G + g, g % 2
                        for h in range(4):
                            for j in range(3):
                                if h == 0:
                                    wait(act, pv_done, n - 1)
                                act.wait_ge(exp_scores, 12 * n + 3 * h + j + 1)
                                width = 256 if j == 2 else 512
                                nc.scalar.activation(probs[u][:, h, 512 * j:512 * j + width], ps_exp[j][:, 0:width],
                                                     ACT.Exp, scale=1.0 / D ** 0.5).then_inc(exp_read, 1)
                            if h == 1 and not (last and g == G - 1):
                                act.wait_ge(mrow_in[g], 48 * (b + 1))
                                copy_max_rows(n + 1)
                            if h == 0 and not (isinstance(n, int) and n < 2):
                                keep_sums(n - 2, u, 2 * b + g // 2 - 1)
                copy_max_rows(0)
                body(0)
                with act.Fori(1, B - 1) as b:
                    body(b)
                body(B - 1, last=True)
                keep_sums(B * G - 2, 0, 2 * B - 1)
                keep_sums(B * G - 1, 1, 2 * B - 1)

            @block.vector
            def _(dve):
                nc.vector.memset(ps_out[:], 0.0).then_inc(ones_ready, 1)
                for g in range(NB):
                    nc.vector.memset(k_st[g][KR:KR + 3, :, :], 1.0).then_inc(ones_ready, 1)
                LINKS = 4

                def maxima(n, h):
                    wait(dve, max_read, 12 * n + 3 * h)
                    for j in range(3):
                        dve.wait_ge(max_scores, 12 * n + 3 * h + j + 1)
                        hold(dve, K)
                        for i, col in MAX_JOBS[j]:
                            w = P * (i + 1)
                            last = nc.vector.tensor_tensor_reduce(
                                out=junk[:, i, 0:w], in0=ps_max[j][:, col:col + w], in1=K["causal"][:, S - w:S], scale=1.0,
                                scalar=LOW, op0=ALU.add, op1=ALU.max, accum_out=mx[:, i, h:h + 1])
                        last.then_inc(max_read, 1)

                def split_maxima(n, base):
                    ord_ = Order(dve, order, LINKS)
                    ord_.base = base
                    dve.wait_ge(max_read, 12 * n + 12)
                    wait(dve, mt_ready, n)
                    ord_.link(nc.vector.tensor_scalar(mparts[:, :, 0], mx[:], -1.0, None, ALU.mult))
                    ord_.link(nc.vector.scalar_tensor_tensor(mrest[:, 0], mx[:], -1.0, mparts[:, :, 0], ALU.mult, ALU.subtract))
                    ord_.link(nc.vector.tensor_copy(mparts[:, :, 1], mrest[:, 0]))
                    ord_.link(nc.vector.tensor_tensor(mrest[:, 1], mrest[:, 0], mparts[:, :, 1], ALU.subtract))
                    nc.vector.tensor_copy(mparts[:, :, 2], mrest[:, 1]).then_inc(mparts_ready, 1)

                def body(b, last=False):
                    for g in range(G):
                        n = b * G + g
                        for h in range(4):
                            if h == 0 and not (last and g == G - 1):
                                split_maxima(n + 1, (n + 1) * LINKS)
                            if not (last and g + 2 >= G):
                                maxima(n + 2, h)
                for h in range(4):
                    maxima(0, h)
                split_maxima(0, 0)
                for h in range(4):
                    maxima(1, h)
                body(0)
                with dve.Fori(1, B - 1) as b:
                    body(b)
                body(B - 1, last=True)

            @block.tensor
            def _(pe):
                def scores_for_max(n, b, g, h):
                    if h == 0:
                        pe.wait_ge(stack_in[g], 16 * LOADS * (b + 1))
                    for j in range(3):
                        wait(pe, max_read, 12 * n + 3 * h + j - 2)
                        for i, col in MAX_JOBS[j]:
                            last = nc.tensor.matmul(ps_max[j][:, col:col + P * (i + 1)], q_st[g][0:KR, h, P * i:P * (i + 1)],
                                                    k_st[g][0:KR, h, 0:P * (i + 1)], start=True, stop=True)
                        last.then_inc(max_scores, 1)

                def transpose_maxima(n):
                    pe.wait_ge(mparts_ready, n + 1)
                    wait(pe, mrow_ready, n)
                    for i in range(NT):
                        last = nc.tensor.transpose(ps_mt[0:12, i * P:(i + 1) * P],
                                                   mparts[:, i].rearrange("p a h -> p (a h)"), K["identb"][:])
                    last.then_inc(mt_ready, 1)

                def products_with_v(n, u, i):
                    if i == 0:
                        pe.wait_ge(masked, 4 * n + 4)
                        pe.wait_ge(v1_ready, n + 1)
                        wait(pe, ot_ready, n)
                    for h in range(4):
                        mm = nc.tensor.matmul(ps_out[32 * h:32 * h + HD + 1, P * i:S], v1[u][:, i, h, :],
                                              probs[u][:, h, EXP_AT[i]:EXP_AT[i] + S - P * i], start=(i == 0),
                                              stop=(i == NT - 1), skip_group_check=True)
                    if i == NT - 1:
                        mm.then_inc(pv_done, 1)

                def body(b, last=False):
                    for g in range(G):
                        n, u = b * G + g, g % 2
                        for h in range(4):
                            if not (last and g + 2 >= G):
                                scores_for_max(n + 2, b + (g + 2) // G, (g + 2) % G, h)
                            if h == 0:
                                pe.wait_ge(mrow_in[g], 48 * (b + 1))
                            for j in range(3):
                                wait(pe, exp_read, 12 * n + 3 * h + j - 2)
                                for i, col in EXP_JOBS[j]:
                                    last_mm = nc.tensor.matmul(ps_exp[j][:, col:col + S - P * i], k_st[g][:, h, P * i:P * (i + 1)],
                                                               q_st[g][:, h, P * i:S], start=True, stop=True)
                                last_mm.then_inc(exp_scores, 1)
                            if h == 0 and not (last and g == G - 1):
                                transpose_maxima(n + 1)
                            if not (isinstance(n, int) and n == 0):
                                for i in ((), (0,), (1,), (2, 3))[h]:
                                    products_with_v(n - 1, (u + 1) % 2, i)
                pe.wait_ge(ones_ready, NB + 3)
                for h in range(4):
                    scores_for_max(0, 0, 0, h)
                transpose_maxima(0)
                for h in range(4):
                    scores_for_max(1, 0, 1, h)
                body(0)
                with pe.Fori(1, B - 1) as b:
                    body(b)
                body(B - 1, last=True)
                for i in range(NT):
                    products_with_v(B * G - 1, 1, i)


TWO_PI = 2.0 * np.pi
PI_1 = 6.28125
PI_2 = float(np.float32(np.floor((TWO_PI - PI_1) * 2.0 ** 20) / 2.0 ** 20))
PI_3 = float(TWO_PI - PI_1 - PI_2)
ROUND = 12582912.0
PI_MAX = 3.1415925
KS = 64


def take_off_turns(nc, link, x, k, out):
    link(nc.vector.tensor_scalar(k, x, 1.0 / TWO_PI, ROUND, ALU.mult, ALU.add))
    link(nc.vector.tensor_scalar(k, k, ROUND, None, ALU.subtract))
    link(nc.vector.scalar_tensor_tensor(out, k, -PI_1, x, ALU.mult, ALU.add))
    link(nc.vector.scalar_tensor_tensor(out, k, -PI_2, out, ALU.mult, ALU.add))
    link(nc.vector.scalar_tensor_tensor(out, k, -PI_3, out, ALU.mult, ALU.add))


def prepare_middle(nc, K, W):
    with ExitStack() as ctx:
        sb = lambda name, shape, dt=F32: ctx.enter_context(nc.sbuf_tensor(name, shape, dt))
        sem = nc.alloc_semaphore
        den, inv = sb("m_den", [P, S]), sb("m_inv", [P, S])
        w0t, a1, a2, t1t = (sb(f"m_{n}", [P, NC, D]) for n in ("w0t", "a1", "a2", "t1t"))
        wc = sb("m_wc", [P, NC, D])
        opt = sb("m_opt", [P, D])
        bd, bds = sb("m_bd", [P, P]), sb("m_bds", [P, P])
        raw = {n: sb(f"m_raw_{n}", list(W[n + "_hi"].shape)) for n in ("win", "wins", "gate", "w1", "w2")}
        freq, decay, e, k1 = (sb(f"m_{n}", [P, 1]) for n in ("freq", "decay", "e", "k1"))
        f_hi, f_lo = sb("m_f_hi", [P, 1], F32R), sb("m_f_lo", [P, 1])
        ni, nf, r, k, ang = sb("m_ni", [P, S], I32), sb("m_nf", [P, S]), sb("m_r", [P, S]), sb("m_k", [P, S]), sb("m_ang", [P, 2, S])
        ps = [ctx.enter_context(nc.psum_tensor(f"m_ps{j}", [P, 512], F32)) for j in range(6)]
        den_in, inv_ready, inv_out = sem("m_den_in"), sem("m_inv_ready"), sem("m_inv_out")
        chain_in, raw_in, small_in, cleared, bd_in = sem("m_chain_in"), sem("m_raw_in"), sem("m_small_in"), sem("m_cleared"), sem("m_bd_in")
        mm, copied, grid, order, split, angles, tables, wide_in = (sem("m_mm"), sem("m_copied"), sem("m_grid"), sem("m_order"),
                                                                   sem("m_split"), sem("m_angles"), sem("m_tables"), sem("m_wide_in"))
        exped = sem("m_exped")
        with nc.Block() as block:
            @block.sync
            def _(sp):
                sp.dma_start(den[:], K["attended"].rearrange("(m r) s -> m r s", r=32)[:, HD, :]).then_inc(den_in, 16)
                for t, n in ((w0t, "w0t"), (a1, "a1"), (a2, "a2")):
                    sp.dma_start(t[:], K[n].rearrange("(c p) n -> p c n", p=P)).then_inc(chain_in, 16)
                sp.dma_start(opt[:], K["opt"]).then_inc(chain_in, 16)
                for half in range(2):
                    sp.dma_start(freq[KS * half:KS * half + KS, :], K["freq"]).then_inc(small_in, 16)
                    sp.dma_start(decay[KS * half:KS * half + KS, :], K["decay"]).then_inc(small_in, 16)
                sp.wait_ge(cleared, 3)
                for half in range(2):
                    for h in range(4):
                        at_, col = KS * half + 16 * h, KS * half + 16 * h
                        other = KS * (1 - half) + 16 * h
                        sp.dma_start(bd[at_:at_ + 16, col:col + 16], K["coupling"][h]).then_inc(bd_in, 16)
                        sp.dma_start(bds[at_:at_ + 16, other:other + 16], K["coupling"][h]).then_inc(bd_in, 16)
                for h in range(4):
                    sp.dma_start(W["wo"][32 * h:32 * h + HD, :, :],
                                 K["wo"].rearrange("(g h d) n -> h d g n", h=4, d=HD)[h]).then_inc(wide_in, 16)
                sp.wait_ge(inv_ready, 1)
                sp.dma_start(K["inverse"], inv[:]).then_inc(inv_out, 16)
                sp.wait_ge(inv_out, 16)
                sp.wait_ge(wide_in, 16 * (4 + 9))

            @block.scalar
            def _(act):
                act.dma_start(raw["win"][:], K["win"].rearrange("(c p) n -> p c n", p=P)).then_inc(raw_in, 16)
                for half in range(2):
                    act.dma_start(raw["wins"][:, :, KS * half:KS * half + KS],
                                  K["win"].rearrange("(c p) n -> p c n", p=P)[:, :, KS - KS * half:2 * KS - KS * half]).then_inc(raw_in, 16)
                act.dma_start(raw["gate"][:], K["gate_wt"].rearrange("(c p) n -> p c n", p=P)).then_inc(raw_in, 16)
                act.dma_start(raw["w1"][:], K["w1t"].rearrange("(c p) n -> p c n", p=P)).then_inc(raw_in, 16)
                act.dma_start(raw["w2"][:], K["w2t"].rearrange("(c p) n -> p c n", p=P)).then_inc(raw_in, 16)
                for n in ("bias0", "gate_b", "b2"):
                    act.dma_start(W[n][:], K[n].rearrange("(o d) -> o d", o=1).partition_broadcast(P)
                                  .rearrange("p o d -> p (o d)")).then_inc(wide_in, 16)
                for n in ("n1g", "n1b", "n2g", "n2b", "b1"):
                    act.dma_start(W[n][:], K[n]).then_inc(wide_in, 16)
                act.dma_start(W["wr"][:], K["wr"].rearrange("(c p) e -> p c e", p=P)).then_inc(wide_in, 16)
                act.wait_ge(small_in, 64)
                nc.scalar.activation(e[:], decay[:], ACT.Exp, scale=-1.0).then_inc(exped, 1)
                act.wait_ge(angles, 1)
                nc.scalar.activation(W["sin"][:], ang[:, 0], ACT.Sin).then_inc(tables, 1)
                nc.scalar.activation(W["cos"][:], ang[:, 1], ACT.Sin).then_inc(tables, 1)

            @block.gpsimd
            def _(pool):
                nc.gpsimd.iota(ni[:], [[1, S]], base=0, channel_multiplier=0).then_inc(grid, 1)
                for t in (bd, bds, W["wo"]):
                    nc.gpsimd.memset(t[:], 0.0).then_inc(cleared, 1)

            @block.vector
            def _(dve):
                ord_ = Order(dve, order, 0)
                link = ord_.link
                dve.wait_ge(den_in, 16)
                nc.vector.reciprocal(inv[:], den[:]).then_inc(inv_ready, 1)
                dve.wait_ge(exped, 1)
                link(nc.vector.tensor_scalar(e[:], e[:], 1.0, None, ALU.add))
                link(nc.vector.reciprocal(k1[:], e[:]))
                link(nc.vector.memset(W["mag"][:], 0.0))
                link(nc.vector.tensor_scalar(W["mag"][:], W["mag"][:], k1[:, 0:1], None, ALU.add))
                take_off_turns(nc, link, freq[:], k1[:], freq[:])
                link(nc.vector.tensor_copy(f_hi[:], freq[:]))
                link(nc.vector.tensor_tensor(f_lo[:], freq[:], f_hi[:].bitcast(F32), ALU.subtract))
                dve.wait_ge(grid, 1)
                link(nc.vector.tensor_copy(nf[:], ni[:]))
                link(nc.vector.tensor_scalar(r[:], nf[:], f_hi[:, 0:1].bitcast(F32), None, ALU.mult))
                take_off_turns(nc, link, r[:], k[:], r[:])
                link(nc.vector.scalar_tensor_tensor(r[:], nf[:], f_lo[:, 0:1], r[:], ALU.mult, ALU.add))
                for j in range(2):
                    if j:
                        link(nc.vector.tensor_scalar(r[:], r[:], TWO_PI / 4, None, ALU.add))
                    take_off_turns(nc, link, r[:], k[:], ang[:, j])
                    link(nc.vector.tensor_scalar(ang[:, j], ang[:, j], -PI_MAX, PI_MAX, ALU.max, ALU.min))
                nc.vector.tensor_scalar(ang[KS:P, 0], ang[KS:P, 0], -1.0, None, ALU.mult).then_inc(angles, 1)
                dve.wait_ge(mm, 1)
                for m in range(NC):
                    last = nc.vector.tensor_copy(t1t[:, m], ps[m][:, 0:D])
                last.then_inc(copied, 1)
                dve.wait_ge(mm, 2)
                for m in range(NC):
                    last = nc.vector.tensor_copy(wc[:, m], ps[2 + m][:, 0:D])
                link(last)
                for m, t in enumerate((W["mt"], W["mts"])):
                    last = nc.vector.tensor_copy(t[:], ps[4 + m][:, 0:D])
                link(last)
                dve.wait_ge(raw_in, 96)
                for src, n in [(wc, "wc")] + [(raw[n], n) for n in raw]:
                    link(nc.vector.tensor_copy(W[n + "_hi"][:], src[:]))
                    last = nc.vector.tensor_tensor(W[n + "_lo"][:], src[:], W[n + "_hi"][:].bitcast(F32), ALU.subtract)
                link(last)

            @block.tensor
            def _(pe):
                pe.wait_ge(chain_in, 64)
                for m in range(NC):
                    for c in range(NC):
                        last = nc.tensor.matmul(ps[m][:, 0:D], a1[:, c, m * P:(m + 1) * P], w0t[:, c], start=(c == 0), stop=(c == 1))
                last.then_inc(mm, 1)
                pe.wait_ge(copied, 1)
                pe.wait_ge(bd_in, 16 * 16)
                for m in range(NC):
                    for c in range(NC):
                        nc.tensor.matmul(ps[2 + m][:, 0:D], t1t[:, c, m * P:(m + 1) * P], a2[:, c], start=(c == 0), stop=(c == 1))
                nc.tensor.matmul(ps[4][:, 0:D], bd[:], opt[:], start=True, stop=True)
                nc.tensor.matmul(ps[5][:, 0:D], bds[:], opt[:], start=True, stop=True).then_inc(mm, 1)


def middle(nc, K, W):
    with ExitStack() as ctx:
        sb = lambda name, shape, dt=F32: ctx.enter_context(nc.sbuf_tensor(name, shape, dt))
        two = range(2)
        A = [sb(f"c_a{u}", [P, 4, S]) for u in two]
        V = [sb(f"c_v{u}", [P, 4, S]) for u in two]
        xn = [sb(f"c_xn{u}", [P, NT, D]) for u in two]
        h = [sb(f"c_h{u}", [P, NC, S]) for u in two]
        h_hi = [sb(f"c_h_hi{u}", [P, NC, S], F32R) for u in two]
        h_lo = [sb(f"c_h_lo{u}", [P, NC, S], F32R) for u in two]
        rows = [sb(f"c_rows{u}", [P, 7, D]) for u in two]
        mod = [sb(f"c_mod{u}", [P, 4, 1]) for u in two]
        stats, mv, root = sb("c_stats", [P, 2 * NT, 6]), sb("c_mv", [P, 2 * NT, 2]), sb("c_root", [P, 3, 2 * NT])
        hid_hi, hid_lo = sb("c_hid_hi", [P, 8, S], F32R), sb("c_hid_lo", [P, 8, S], F32R)
        ps = [[ctx.enter_context(nc.psum_tensor(f"c_ps{u}{j}", [P, 512], F32)) for j in range(4)] for u in two]
        hres = [V[u][:, 0:2, :].rearrange("p a s -> p (a s)").rearrange("p (i d) -> p i d", d=D) for u in two]
        gate = [V[u][:, 2:4, :].rearrange("p a s -> p (a s)").rearrange("p (i d) -> p i d", d=D) for u in two]
        row = lambda u, j: rows[u][:, j:j + 1, :].to_broadcast([P, NT, D])
        tok = lambda u, j: [ps[u][j][:].rearrange("p (i d) -> p i d", i=2), ps[u][j + 1][:].rearrange("p (i d) -> p i d", i=2)]
        sem = nc.alloc_semaphore
        names = """att_in inv_in rows_in att_ready mod_ready wo_ready x1_ready xn2 xt2 h2 lo2 z_ready zb_ready tanh_ready x2_ready
                   xn3 hres_ready xn4 xt4 h4 lo4 beta_ready gpre_ready gsum_ready gate_ready rot_ready o_ready x3_ready
                   xn5 xt5 h5 lo5 hid_ps hid_f hid_hi_ready hid_lo_ready y_ready x4_ready xn6 hrow_ready xt6 h6 h_out lg_ready lg_done
                   order""".split()
        Z = {n: sem("c_" + n) for n in names if n not in ("att_in", "inv_in", "rows_in", "h_out")}
        for n in ("att_in", "inv_in", "rows_in", "h_out"):
            Z[n] = [sem(f"c_{n}{u}") for u in two]

        with nc.Block() as block:
            @block.sync
            def _(sp):
                def body(it):
                    for u in two:
                        b = 2 * it + u
                        wait(sp, Z["o_ready"], at(it - 1, u))
                        sp.dma_start(A[u][:], K["attended"][bass.ds(b * S, S), :].rearrange("(g p) s -> p g s", p=P)).then_inc(Z["att_in"][u], 16)
                        wait(sp, Z["x4_ready"], at(it - 1, u))
                        for h_ in range(4):
                            sp.dma_start(V[u][32 * h_:32 * h_ + 32, :, :],
                                         K["inverse"].rearrange("(n h) s -> h n s", h=4)[h_, bass.ds(b * G, G), :]
                                         .partition_broadcast(32)).then_inc(Z["inv_in"][u], 16)
                        wait(sp, Z["hrow_ready"], at(it - 1, u))
                        for j, (l, m) in enumerate(((0, 2), (0, 5), (1, 1), (1, 0), (1, 2), (1, 4), (1, 3))):
                            sp.dma_start(rows[u][:, j, :], K["mod_rows"][l, bass.ds(b, 1), m * D:(m + 1) * D]
                                         .partition_broadcast(P).rearrange("p o d -> p (o d)")).then_inc(Z["rows_in"][u], 16)
                    for u in two:
                        sp.wait_ge(Z["hrow_ready"], at(it, u))
                        sp.dma_start(K["h_rows"][bass.ds((2 * it + u) * S, S), :].rearrange("(i p) d -> p i d", p=P),
                                     xn[u][:]).then_inc(Z["h_out"][u], 16)
                passes(sp, B // 2, body)
                for u in two:
                    sp.wait_ge(Z["h_out"][u], 16 * (B // 2))

            @block.gpsimd
            def _(pool):
                def body(it):
                    for u in two:
                        wait(pool, Z["h2"], at(it - 1, u))
                        hold(pool, K)
                        nc.gpsimd.tensor_copy(mod[u][:], K["mod_cols"][:, 0, 6:10, bass.ds(2 * it + u, 1)]).then_inc(Z["mod_ready"], 1)
                    for u in two:
                        pool.wait_ge(Z["att_in"][u], 16 * (it + 1))
                        pool.wait_ge(Z["inv_in"][u], 64 * (it + 1))
                        for g in range(G):
                            last = nc.gpsimd.tensor_tensor(A[u][:, g], A[u][:, g], V[u][:, g], ALU.mult)
                        last.then_inc(Z["att_ready"], 1)
                passes(pool, B // 2, body)

            @block.scalar
            def _(act):
                def spread(it, u, xt, done, scale, shift, used, bank, both=True):
                    act.wait_ge(Z[xt], at(it, u))
                    wait(act, *used)
                    for c in range(NC):
                        last = nc.scalar.activation(h[u][:, c], ps[u][bank + c][:], ACT.Identity, bias=shift[c], scale=scale[c])
                    if both:
                        for c in range(NC):
                            last = nc.scalar.activation(h_hi[u][:, c], ps[u][bank + c][:], ACT.Identity, bias=shift[c], scale=scale[c])
                    last.then_inc(Z[done], 1)

                def body(it):
                    cols = lambda t: [t[:, c:c + 1] for c in range(NC)]
                    for u in two:
                        act.wait_ge(Z["mod_ready"], at(it, u))
                        spread(it, u, "xt2", "h2", [mod[u][:, 2 + c] for c in range(NC)], [mod[u][:, c] for c in range(NC)],
                               (Z["lg_ready"], at(it - 1, u)), 0)
                    for u in two:
                        act.wait_ge(Z["zb_ready"], at(it, u))
                        nc.scalar.activation(xn[u][:], xn[u][:], ACT.Tanh).then_inc(Z["tanh_ready"], 1)
                    for u in two:
                        spread(it, u, "xt4", "h4", cols(W["n1g"]), cols(W["n1b"]), (Z["z_ready"], at(it, u)), 0)
                    for u in two:
                        act.wait_ge(Z["gsum_ready"], at(it, u))
                        nc.scalar.activation(gate[u], gate[u], ACT.Sigmoid).then_inc(Z["gate_ready"], 1)
                    for u in two:
                        spread(it, u, "xt5", "h5", cols(W["n2g"]), cols(W["n2b"]), (Z["gpre_ready"], at(it, u)), 2)
                    for u in two:
                        hf = xn[u][:].rearrange("p i d -> p (i d)").rearrange("p (j s) -> p j s", s=S)
                        for m in range(8):
                            step = 8 * (2 * it + u) + m
                            act.wait_ge(Z["hid_ps"], step + 1)
                            if m >= 2:
                                act.wait_ge(Z["hid_lo_ready"], step - 1)
                            nc.scalar.activation(hf[:, m % 2], ps[u][m % 4][:], ACT.Silu, bias=W["b1"][:, m:m + 1]).then_inc(Z["hid_f"], 1)
                    for u in two:
                        act.wait_ge(Z["xt6"], at(it, u))
                        for c in range(NC):
                            last = nc.scalar.activation(h[u][:, c], ps[u][2 + c][:], ACT.Copy)
                        last.then_inc(Z["h6"], 1)
                passes(act, B // 2, body)

            @block.vector
            def _(dve):
                ord_ = Order(dve, Z["order"], 5 * LN_LINKS + 2 * (1 + 1 + 1 + 3 + 1 + 3 + 1))
                link = ord_.link

                def norm(it, src, name):
                    layer_norm(nc, K, dve, link, src, stats, mv, root, [xn[u][:, i, :] for u in two for i in range(NT)], Z[name])

                def low(it, u, hs, lo):
                    dve.wait_ge(Z[hs], at(it, u))
                    nc.vector.tensor_tensor(h_lo[u][:], h[u][:], h_hi[u][:].bitcast(F32), ALU.subtract).then_inc(Z[lo], 1)

                def body(it):
                    ord_.at(it)
                    x = [K["x_sb"][:, bass.ds((2 * it + u) * NT, NT), :] for u in two]
                    xt = [K["x_sb"][:, bass.ds(2 * NT * it + i, 1), :] for i in range(2 * NT)]
                    for u in two:
                        dve.wait_ge(Z["rows_in"][u], 16 * 7 * (it + 1))
                        wait(dve, Z["h_out"][u], 16 * it)
                        dve.wait_ge(Z["wo_ready"], at(it, u))
                        for j in two:
                            last = nc.vector.tensor_tensor(xn[u][:, 2 * j:2 * j + 2], tok(u, 2)[j], rows[u][:, 0:1, :].to_broadcast([P, 2, D]), ALU.mult)
                        link(last)
                        last = nc.vector.tensor_tensor(x[u], x[u], xn[u][:], ALU.add)
                        last.then_inc(Z["x1_ready"], 1)
                    dve.wait_ge(Z["x1_ready"], at(it, 1))
                    norm(it, xt, "xn2")
                    for u in two:
                        low(it, u, "h2", "lo2")
                    for u in two:
                        dve.wait_ge(Z["z_ready"], at(it, u))
                        for j in two:
                            last = nc.vector.tensor_tensor(xn[u][:, 2 * j:2 * j + 2], tok(u, 2)[j], W["bias0"][:].rearrange("p (o d) -> p o d", o=1)
                                                           .to_broadcast([P, 2, D]), ALU.add)
                        last.then_inc(Z["zb_ready"], 1)
                    for u in two:
                        dve.wait_ge(Z["tanh_ready"], at(it, u))
                        link(nc.vector.tensor_tensor(xn[u][:], xn[u][:], row(u, 1), ALU.mult))
                        nc.vector.tensor_tensor(x[u], x[u], xn[u][:], ALU.add).then_inc(Z["x2_ready"], 1)
                    dve.wait_ge(Z["x2_ready"], at(it, 1))
                    norm(it, xt, "xn3")
                    for u in two:
                        dve.wait_ge(Z["xn3"], at(it, u))
                        link(nc.vector.tensor_tensor(hres[u], xn[u][:], row(u, 2), ALU.mult))
                        nc.vector.tensor_tensor(hres[u], hres[u], row(u, 3), ALU.add).then_inc(Z["hres_ready"], 1)
                    dve.wait_ge(Z["hres_ready"], at(it, 1))
                    norm(it, [hres[u][:, i:i + 1, :] for u in two for i in range(NT)], "xn4")
                    for u in two:
                        low(it, u, "h4", "lo4")
                    for u in two:
                        dve.wait_ge(Z["beta_ready"], at(it, u))
                        nc.vector.tensor_tensor(A[u][:, 0], ps[u][0][:], W["cos"][:], ALU.mult)
                        link(nc.vector.tensor_tensor(A[u][:, 1], ps[u][1][:], W["sin"][:], ALU.mult))
                        link(nc.vector.tensor_tensor(A[u][:, 0], A[u][:, 0], A[u][:, 1], ALU.add))
                        hold(dve, K)
                        link(nc.vector.tensor_tensor_scan(A[u][:, 1], W["mag"][:], A[u][:, 0], 0.0, ALU.mult, ALU.add))
                        nc.vector.tensor_tensor(A[u][:, 2], A[u][:, 1], W["cos"][:], ALU.mult)
                        nc.vector.tensor_tensor(A[u][:, 3], A[u][:, 1], W["sin"][:], ALU.mult).then_inc(Z["rot_ready"], 1)
                        dve.wait_ge(Z["gpre_ready"], at(it, u))
                        for j in two:
                            last = nc.vector.tensor_tensor(gate[u][:, 2 * j:2 * j + 2], tok(u, 2)[j], W["gate_b"][:].rearrange("p (o d) -> p o d", o=1)
                                                           .to_broadcast([P, 2, D]), ALU.add)
                        last.then_inc(Z["gsum_ready"], 1)
                    for u in two:
                        dve.wait_ge(Z["gate_ready"], at(it, u))
                        dve.wait_ge(Z["o_ready"], at(it, u))
                        for j in two:
                            last = nc.vector.tensor_tensor(gate[u][:, 2 * j:2 * j + 2], gate[u][:, 2 * j:2 * j + 2], tok(u, 0)[j], ALU.mult)
                        link(last)
                        nc.vector.tensor_tensor(hres[u], hres[u], gate[u], ALU.add).then_inc(Z["x3_ready"], 1)
                    dve.wait_ge(Z["x3_ready"], at(it, 1))
                    norm(it, [hres[u][:, i:i + 1, :] for u in two for i in range(NT)], "xn5")
                    for u in two:
                        low(it, u, "h5", "lo5")
                    for u in two:
                        hf = xn[u][:].rearrange("p i d -> p (i d)").rearrange("p (j s) -> p j s", s=S)
                        for m in range(8):
                            step = 8 * (2 * it + u) + m
                            dve.wait_ge(Z["hid_f"], step + 1)
                            if m == 0:
                                wait(dve, Z["y_ready"], 2 * it + u)
                            nc.vector.tensor_copy(hid_hi[:, m], hf[:, m % 2]).then_inc(Z["hid_hi_ready"], 1)
                            dve.wait_ge(Z["hid_hi_ready"], step + 1)
                            nc.vector.tensor_tensor(hid_lo[:, m], hf[:, m % 2], hid_hi[:, m].bitcast(F32), ALU.subtract).then_inc(Z["hid_lo_ready"], 1)
                    for u in two:
                        link(nc.vector.tensor_tensor(hres[u], hres[u], W["b2"][:].rearrange("p (o d) -> p o d", o=1).to_broadcast([P, NT, D]), ALU.add))
                        dve.wait_ge(Z["y_ready"], at(it, u))
                        for j in two:
                            last = nc.vector.tensor_tensor(hres[u][:, 2 * j:2 * j + 2], hres[u][:, 2 * j:2 * j + 2], tok(u, 0)[j], ALU.add)
                        link(last)
                        link(nc.vector.tensor_tensor(hres[u], hres[u], row(u, 4), ALU.mult))
                        nc.vector.tensor_tensor(x[u], x[u], hres[u], ALU.add).then_inc(Z["x4_ready"], 1)
                    dve.wait_ge(Z["x4_ready"], at(it, 1))
                    norm(it, xt, "xn6")
                    for u in two:
                        dve.wait_ge(Z["xn6"], at(it, u))
                        link(nc.vector.tensor_tensor(xn[u][:], xn[u][:], row(u, 5), ALU.mult))
                        nc.vector.tensor_tensor(xn[u][:], xn[u][:], row(u, 6), ALU.add).then_inc(Z["hrow_ready"], 1)
                    for u in two:
                        dve.wait_ge(Z["lg_ready"], at(it, u))
                        nc.vector.tensor_copy(K["logits"][:, bass.ds((2 * it + u) * NT, NT), :],
                                              ps[u][0][:, 0:NT * 8].rearrange("p (i e) -> p i e", e=8)).then_inc(Z["lg_done"], 1)
                    ord_.done()
                passes(dve, B // 2, body)

            @block.tensor
            def _(pe):
                def transposes(it, u, xns, xt, bank, used):
                    pe.wait_ge(Z[xns], at(it, u))
                    wait(pe, *used)
                    for c in range(NC):
                        for i in range(NT):
                            last = nc.tensor.transpose(ps[u][bank + c][:, i * P:(i + 1) * P], xn[u][:, i, c * P:(c + 1) * P], K["ident"][:])
                    last.then_inc(Z[xt], 1)

                def by_tokens(u, bank, n_c, x_hi, x_lo, w_hi, w_lo, done):
                    for i in range(NT):
                        out, n = ps[u][bank + i // 2][:, (i % 2) * D:(i % 2) * D + D], 0
                        t = slice(i * P, (i + 1) * P)
                        for c in range(n_c):
                            for a, w in ((x_hi, w_hi), (x_lo, w_hi), (x_hi, w_lo)):
                                last = nc.tensor.matmul(out, a[:, c, t], w[:, c, :], start=(n == 0), stop=(n == 3 * n_c - 1))
                                n += 1
                    last.then_inc(Z[done], 1)

                def by_features(out, w_hi, w_lo, cols, x_hi, x_lo):
                    n = 0
                    for c in range(NC):
                        for w, a in ((w_hi, x_hi), (w_hi, x_lo), (w_lo, x_hi)):
                            last = nc.tensor.matmul(out, w[:, c, cols], a[:, c], start=(n == 0), stop=(n == 5))
                            n += 1
                    return last

                def body(it):
                    for u in two:
                        pe.wait_ge(Z["att_ready"], at(it, u))
                        wait(pe, Z["h6"], at(it - 1, u))
                        for i in range(NT):
                            for g in range(G):
                                last = nc.tensor.matmul(ps[u][2 + i // 2][:, (i % 2) * D:(i % 2) * D + D], A[u][:, g, i * P:(i + 1) * P],
                                                        W["wo"][:, g, :], start=(g == 0), stop=(g == G - 1))
                        last.then_inc(Z["wo_ready"], 1)
                    for u in two:
                        transposes(it, u, "xn2", "xt2", 0, (Z["lg_done"], at(it - 1, u)))
                    for u in two:
                        pe.wait_ge(Z["lo2"], at(it, u))
                        pe.wait_ge(Z["x1_ready"], at(it, u))
                        by_tokens(u, 2, NC, h_hi[u], h_lo[u], W["wc_hi"], W["wc_lo"], "z_ready")
                    for u in two:
                        transposes(it, u, "xn4", "xt4", 0, (Z["h2"], at(it, u)))
                    for u in two:
                        pe.wait_ge(Z["lo4"], at(it, u))
                        by_features(ps[u][0][:], W["win_hi"], W["win_lo"], slice(0, P), h_hi[u], h_lo[u])
                        by_features(ps[u][1][:], W["wins_hi"], W["wins_lo"], slice(0, P), h_hi[u], h_lo[u]).then_inc(Z["beta_ready"], 1)
                        pe.wait_ge(Z["zb_ready"], at(it, u))
                        by_tokens(u, 2, NC, h_hi[u], h_lo[u], W["gate_hi"], W["gate_lo"], "gpre_ready")
                    for u in two:
                        pe.wait_ge(Z["rot_ready"], at(it, u))
                        for i in range(NT):
                            for n, m in enumerate(("mt", "mts")):
                                last = nc.tensor.matmul(ps[u][i // 2][:, (i % 2) * D:(i % 2) * D + D], A[u][:, 2 + n, i * P:(i + 1) * P],
                                                        W[m][:], start=(n == 0), stop=(n == 1))
                        last.then_inc(Z["o_ready"], 1)
                    for u in two:
                        transposes(it, u, "xn5", "xt5", 2, (Z["gsum_ready"], at(it, u)))
                    for u in two:
                        pe.wait_ge(Z["lo5"], at(it, u))
                        pe.wait_ge(Z["x3_ready"], at(it, u))
                        for m in range(8):
                            step = 8 * (2 * it + u) + m
                            if m >= 4:
                                pe.wait_ge(Z["hid_f"], step - 3)
                            by_features(ps[u][m % 4][:], W["w1_hi"], W["w1_lo"], slice(m * P, (m + 1) * P), h_hi[u], h_lo[u]).then_inc(Z["hid_ps"], 1)
                        pe.wait_ge(Z["hid_lo_ready"], 8 * (2 * it + u) + 8)
                        by_tokens(u, 0, 8, hid_hi, hid_lo, W["w2_hi"], W["w2_lo"], "y_ready")
                    for u in two:
                        pe.wait_ge(Z["hrow_ready"], at(it, u))
                        pe.wait_ge(Z["hid_f"], 8 * (2 * it + u) + 8)
                        for c in range(NC):
                            for i in range(NT):
                                last = nc.tensor.transpose(ps[u][2 + c][:, i * P:(i + 1) * P], xn[u][:, i, c * P:(c + 1) * P], K["ident"][:])
                        last.then_inc(Z["xt6"], 1)
                    for u in two:
                        pe.wait_ge(Z["h6"], at(it, u))
                        pe.wait_ge(Z["x4_ready"], at(it, u))
                        for i in range(NT):
                            for c in range(NC):
                                last = nc.tensor.matmul(ps[u][0][:, 8 * i:8 * i + 8], h[u][:, c, i * P:(i + 1) * P], W["wr"][:, c, :],
                                                        start=(c == 0), stop=(c == NC - 1))
                        last.then_inc(Z["lg_ready"], 1)
                passes(pe, B // 2, body)


E = 8
F = 4 * D
STEP = 2 * P
STEPS = B * S * E // STEP
TILES = 2 * (STEPS + 3)
NOWHERE = float(1 << 23)
SIDE = 8


def route(nc, K):
    n = T * E
    with ExitStack() as ctx:
        sb = lambda name, shape, dt=F32: ctx.enter_context(nc.sbuf_tensor(name, shape, dt))
        sem = nc.alloc_semaphore
        lg, top, mask, ex, gate, rank = (sb(f"r_{x}", [P, T, E]) for x in ("lg", "top", "mask", "ex", "gate", "rank"))
        pos, sel, tmp = (sb(f"r_{x}", [P, T, E]) for x in ("pos", "sel", "tmp"))
        tot, run = sb("r_tot", [P, E, T]), sb("r_run", [P, E, T])
        same_token, same_expert = sb("r_same_token", [P, T, E]), sb("r_same_expert", [P, E, T])
        total, slot_f = sb("r_total", [P, T]), sb("r_slot_f", [P, E * T])
        tile_i, tile_f = sb("r_tile_i", [P, E * T], I32), sb("r_tile_f", [P, E * T])
        cnt, steps_f, base_f, ones_e = sb("r_cnt", [P, E]), sb("r_steps_f", [P, E]), sb("r_base_f", [P, E]), sb("r_ones_e", [P, E])
        cnt_i = sb("r_cnt_i", [P, E], I32)
        most, most_all = sb("r_most", [P, 1]), sb("r_most_all", [P, 1])
        before, ones = sb("r_before", [P, P]), sb("r_ones", [P, P])
        slots = sb("r_slots", [P, E * T], I32)
        entries = sb("r_entries", [P, E * T, 2], I32)
        token = sb("r_token", [P, T], I32)
        blank = sb("r_blank", [P, TILES, 2], I32)
        zeros = sb("r_zeros", [P, 17 * D])
        br = sb("r_br", [P, E])
        sl = [sb(f"r_sl{u}", [P, SIDE], I32) for u in range(2)]
        en = [sb(f"r_en{u}", [P, SIDE, 2], I32) for u in range(2)]
        ps_in, ps_tot = (ctx.enter_context(nc.psum_tensor(f"r_ps{j}", [P, 512], F32)) for j in range(2))
        cleared, filled, br_in, exped, order, mask_ready, counted, slots_ready, consts, most_ready, most_done, moved = (
            sem("r_" + x) for x in ("cleared", "filled", "br_in", "exped", "order", "mask_ready", "counted",
                                    "slots_ready", "consts", "most_ready", "most_done", "moved"))
        scattered = [sem(f"r_scattered{u}") for u in range(2)]
        with nc.Block() as block:
            @block.sync
            def _(sp):
                sp.dma_start(br[:], K["br"].rearrange("(o e) -> o e", o=1).partition_broadcast(P).rearrange("p o e -> p (o e)")).then_inc(br_in, 16)
                sp.wait_ge(cleared, 2)
                rows = K["mixed"].rearrange("(p a) d -> p (a d)", p=P)
                for j in range(2):
                    sp.dma_start(rows[:, 17 * D * j:17 * D * (j + 1)], zeros[:]).then_inc(filled, 16)
                sp.dma_start(K["h_rows"][B * S:B * S + STEP, :].rearrange("(a p) d -> p a d", p=P),
                             zeros[:, 0:2 * D].rearrange("p (a d) -> p a d", a=2)).then_inc(filled, 16)
                sp.dma_start(K["table"].rearrange("(p a) c -> p a c", p=P), blank[:]).then_inc(filled, 16)
                sp.wait_ge(filled, 64)

            @block.scalar
            def _(act):
                act.wait_ge(mask_ready, 1)
                nc.scalar.activation(ex[:], ex[:], ACT.Exp).then_inc(exped, 1)

            @block.tensor
            def _(pe):
                pe.wait_ge(mask_ready, 1)
                pe.wait_ge(consts, 6)
                flat = mask[:].rearrange("p t e -> p (t e)")
                nc.tensor.matmul(ps_in[:, 0:n], before[:], flat, start=True, stop=True).then_inc(counted, 1)
                nc.tensor.matmul(ps_tot[:, 0:n], ones[:], flat, start=True, stop=True).then_inc(counted, 1)

            @block.gpsimd
            def _(pool):
                nc.gpsimd.memset(zeros[:], 0.0).then_inc(cleared, 1)
                nc.gpsimd.memset(blank[:], 0).then_inc(consts, 1)
                pool.wait_ge(consts, 1)
                nc.gpsimd.iota(blank[:, :, 0], [[P, TILES]], base=0, channel_multiplier=1).then_inc(consts, 1)
                nc.gpsimd.memset(before[:], 1.0).then_inc(consts, 1)
                nc.gpsimd.memset(ones[:], 1.0).then_inc(consts, 1)
                nc.gpsimd.iota(token[:], [[P, T]], base=0, channel_multiplier=1).then_inc(consts, 1)
                pool.wait_ge(consts, 5)
                nc.gpsimd.affine_select(out=before[:], in_=before[:], compare_op=ALU.is_gt, fill=0.0, base=0,
                                        pattern=[[1, P]], channel_multiplier=-1).then_inc(consts, 1)
                pool.wait_ge(most_ready, 1)
                pool.partition_all_reduce(most_all[:], most[:], P, bass.bass_isa.ReduceOp.max).then_inc(most_done, 1)
                pool.wait_ge(slots_ready, 2)
                pool.wait_ge(filled, 64)
                ranks = pool.value_load(K["ranks"][0:1, 0:1], min_val=2, max_val=E)

                def body(j):
                    for u in range(2):
                        wait(pool, scattered[u], 16 * SIDE * j)
                        c0 = (2 * j + u) * SIDE
                        hold(pool, K)
                        nc.gpsimd.tensor_copy(sl[u][:], slots[:, bass.ds(c0, SIDE)]).then_inc(moved, 1)
                        nc.gpsimd.tensor_copy(en[u][:], entries[:, bass.ds(c0, SIDE), :]).then_inc(moved, 1)
                        pool.wait_ge(moved, 4 * j + 2 * u + 2)
                        hold(pool, K)
                        for i in range(SIDE):
                            pool.indirect_dma_start(K["table"], bass.IndirectOffsetOnAxis(ap=sl[u][:, i:i + 1], axis=0), en[u][:, i, :],
                                                    None, bounds_check=P * TILES - 1, oob_is_err=False).then_inc(scattered[u], 16)
                body(0)
                with pool.Fori(1, ranks * (T // SIDE // 2)) as j:
                    body(j)
                for u in range(2):
                    pool.wait_ge(scattered[u], ranks * (16 * SIDE * T // SIDE // 2))
                hold(pool, K)

            @block.vector
            def _(dve):
                ord_ = Order(dve, order, 0)
                link = ord_.link
                fl = lambda t: t[:].rearrange("p a b -> p (a b)")
                nc.vector.memset(same_token[:], 1.0)
                nc.vector.memset(same_expert[:], 1.0)
                link(nc.vector.memset(ones_e[:], 1.0))
                nc.vector.memset(same_token[:, :, 0], 0.0)
                link(nc.vector.memset(same_expert[:, :, 0], 0.0))
                dve.wait_ge(consts, 2)
                link(nc.vector.tensor_scalar(blank[:, :, 0], blank[:, :, 0], STEP - 1, B * S, ALU.bitwise_and, ALU.bitwise_or))
                dve.sem_inc(cleared, 1)
                dve.wait_ge(br_in, 16)
                link(nc.vector.tensor_tensor(lg[:], K["logits"][:], br[:].rearrange("p (o e) -> p o e", o=1).to_broadcast([P, T, E]), ALU.add))
                for t in range(T):
                    last = nc.vector.max(top[:, t, :], lg[:, t, :])
                link(last)
                link(nc.vector.tensor_tensor(ex[:], lg[:], top[:, :, 0:1].to_broadcast([P, T, E]), ALU.subtract))
                nc.vector.tensor_tensor(mask[:], lg[:], top[:, :, 1:2].to_broadcast([P, T, E]), ALU.is_ge).then_inc(mask_ready, 1)
                dve.wait_ge(mask_ready, 1)
                link(nc.vector.tensor_tensor_scan(fl(rank), fl(same_token), fl(mask), 0.0, ALU.mult, ALU.add))
                link(nc.vector.tensor_reduce(most[:], rank[:, :, E - 1], AX.X, ALU.max))
                dve.sem_inc(most_ready, 1)
                dve.wait_ge(exped, 1)
                link(nc.vector.tensor_tensor(ex[:], ex[:], mask[:], ALU.mult))
                link(nc.vector.tensor_reduce(total[:], ex[:], AX.X, ALU.add))
                link(nc.vector.reciprocal(total[:], total[:]))
                link(nc.vector.tensor_tensor(gate[:], ex[:], total[:].rearrange("p (t o) -> p t o", o=1).to_broadcast([P, T, E]), ALU.mult))
                dve.wait_ge(counted, 2)
                link(nc.vector.tensor_copy(tot[:], ps_tot[:, 0:n].rearrange("p (t e) -> p e t", e=E)))
                link(nc.vector.tensor_tensor_scan(fl(run), fl(same_expert), fl(tot), 0.0, ALU.mult, ALU.add))
                link(nc.vector.tensor_scalar(cnt[:], run[:, :, T - 1], 1.0, float(STEP - 1), ALU.max, ALU.add))
                link(nc.vector.tensor_copy(cnt_i[:], cnt[:]))
                link(nc.vector.tensor_scalar(K["steps"][:], cnt_i[:], 8, None, ALU.logical_shift_right))
                link(nc.vector.tensor_copy(steps_f[:], K["steps"][:]))
                link(nc.vector.tensor_tensor_scan(base_f[:], ones_e[:], steps_f[:], 0.0, ALU.mult, ALU.add))
                link(nc.vector.tensor_tensor(base_f[:], base_f[:], steps_f[:], ALU.subtract))
                link(nc.vector.tensor_copy(K["base"][:], base_f[:]))
                link(nc.vector.scalar_tensor_tensor(steps_f[:], steps_f[:], -1.0, base_f[:], ALU.add, ALU.add))
                link(nc.vector.tensor_copy(K["final"][:], steps_f[:]))
                link(nc.vector.tensor_tensor(run[:], run[:], tot[:], ALU.subtract))
                link(nc.vector.tensor_scalar(base_f[:], base_f[:], float(STEP), -NOWHERE, ALU.mult, ALU.add))
                link(nc.vector.tensor_tensor(run[:], run[:], base_f[:].rearrange("p (e o) -> p e o", o=1).to_broadcast([P, E, T]), ALU.add))
                link(nc.vector.tensor_tensor(pos[:], ps_in[:, 0:n].rearrange("p (t e) -> p t e", e=E), run[:].rearrange("p e t -> p t e"), ALU.add))
                for r in range(E):
                    link(nc.vector.scalar_tensor_tensor(sel[:], rank[:], float(r + 1), mask[:], ALU.is_equal, ALU.mult))
                    link(nc.vector.tensor_tensor(tmp[:], sel[:], pos[:], ALU.mult))
                    link(nc.vector.tensor_reduce(slot_f[:, T * r:T * r + T], tmp[:], AX.X, ALU.add))
                    link(nc.vector.tensor_tensor(tmp[:], sel[:], gate[:], ALU.mult))
                    link(nc.vector.tensor_reduce(entries[:, T * r:T * r + T, 1].bitcast(F32), tmp[:], AX.X, ALU.add))
                    link(nc.vector.tensor_copy(entries[:, T * r:T * r + T, 0], token[:]))
                link(nc.vector.tensor_scalar(slot_f[:], slot_f[:], NOWHERE, None, ALU.add))
                link(nc.vector.tensor_copy(slots[:], slot_f[:]))
                link(nc.vector.tensor_scalar(tile_i[:], slots[:], 7, None, ALU.logical_shift_right))
                link(nc.vector.tensor_copy(tile_f[:], tile_i[:]))
                link(nc.vector.scalar_tensor_tensor(slot_f[:], tile_f[:], -float(P), slot_f[:], ALU.mult, ALU.add))
                link(nc.vector.scalar_tensor_tensor(slot_f[:], slot_f[:], float(TILES), tile_f[:], ALU.mult, ALU.add))
                link(nc.vector.tensor_copy(slots[:], slot_f[:]))
                dve.sem_inc(slots_ready, 1)
                dve.wait_ge(most_done, 1)
                link(nc.vector.tensor_scalar(K["ranks"][:], most_all[:], 2.0, None, ALU.max))
                dve.sem_inc(slots_ready, 1)


def experts(nc, K):
    with ExitStack() as ctx:
        sb = lambda name, shape, dt=F32: ctx.enter_context(nc.sbuf_tensor(name, shape, dt))
        sem = nc.alloc_semaphore
        two = range(2)
        table = sb("e_table", [P, TILES, 2], I32)
        w1f, w2f = sb("e_w1f", [P, NC, F]), sb("e_w2f", [P, 8, D])
        w1_hi, w1_lo = ([sb(f"e_w1{x}{p}", [P, NC, F], F32R) for p in two] for x in ("hi", "lo"))
        w2_hi, w2_lo = ([sb(f"e_w2{x}{p}", [P, 8, D], F32R) for p in two] for x in ("hi", "lo"))
        b1 = [sb(f"e_b1{p}", [P, 8]) for p in two]
        b2 = [sb(f"e_b2{p}", [P, D]) for p in two]
        rows, cur = sb("e_rows", [P, 2, 2], I32), sb("e_cur", [P, 2, 2], I32)
        xg = sb("e_xg", [P, 2, D])
        xf = sb("e_xf", [P, NC, STEP])
        x_hi, x_lo = sb("e_x_hi", [P, NC, STEP], F32R), sb("e_x_lo", [P, NC, STEP], F32R)
        gf = sb("e_gf", [P, 8, STEP])
        g_hi, g_lo = sb("e_g_hi", [P, 8, STEP], F32R), sb("e_g_lo", [P, 8, STEP], F32R)
        yb, yv = sb("e_yb", [P, 2, D]), sb("e_yv", [P, 2, D])
        ps_t = ctx.enter_context(nc.psum_tensor("e_ps_t", [P, 512], F32))
        ps_y = ctx.enter_context(nc.psum_tensor("e_ps_y", [P, 512], F32))
        ps_h = [ctx.enter_context(nc.psum_tensor(f"e_ps_h{j}", [P, 512], F32)) for j in range(4)]
        names = """gathered picked transposed xf_ready x_hi_ready x_ready hid_ps gelu_ready g_hi_ready g_ready g_used yb_ready
                   yv_ready scattered raw_in whi_ready w_ready weights_used""".split()
        Z = {n: sem("e_" + n) for n in names}
        Z["bias_in"] = [sem(f"e_bias_in{p}") for p in two]

        def step_range(eng, e):
            steps = eng.value_load(K["steps"][0:1, bass.ds(e, 1)], min_val=1, max_val=B * S // STEP)
            base = eng.value_load(K["base"][0:1, bass.ds(e, 1)], min_val=0, max_val=STEPS - B * S // STEP)
            final = eng.value_load(K["final"][0:1, bass.ds(e, 1)], min_val=0, max_val=STEPS - 1)
            return base, steps, final

        def slots_of(eng, e, p, slot, last=False):
            base, steps, final = step_range(eng, e)
            with eng.If(steps > 1):
                with eng.Fori(0, steps - 1) as i:
                    slot(base + i, p, p)
            slot(final, p, None if last else 1 - p)

        with nc.Block() as block:
            @block.sync
            def _(sp):
                def raw(e):
                    sp.dma_start(w1f[:], K["ew1"][bass.ds(e, 1)].rearrange("o (c p) n -> (o p) c n", p=P)).then_inc(Z["raw_in"], 16)
                    sp.dma_start(w2f[:], K["ew2"][bass.ds(e, 1)].rearrange("o (c p) n -> (o p) c n", p=P)).then_inc(Z["raw_in"], 16)
                raw(0)
                with sp.Fori(1, E) as e:
                    sp.wait_ge(Z["w_ready"], e)
                    raw(e)

            @block.gpsimd
            def _(pool):
                def gather(g, picked):
                    nc.gpsimd.tensor_copy(rows[:], table[:, bass.ds(2 * g, 2), :]).then_inc(Z["picked"], 1)
                    pool.wait_ge(Z["picked"], picked)
                    hold(pool, K)
                    for s in two:
                        pool.indirect_dma_start(xg[:, s, :], None, K["h_rows"], bass.IndirectOffsetOnAxis(ap=rows[:, s, 0:1], axis=0)
                                                ).then_inc(Z["gathered"], 16)

                for half in two:
                    pool.dma_start(table[:, half * (TILES // 2):(half + 1) * (TILES // 2), :],
                                   K["table"].rearrange("(p a) c -> p a c", p=P)[:, half * (TILES // 2):(half + 1) * (TILES // 2), :]
                                   ).then_inc(Z["scattered"], 16)
                pool.wait_ge(Z["scattered"], 32)
                gather(0, 1)
                pool.wait_ge(Z["transposed"], 1)
                gather(1, 2)
                pool.wait_ge(Z["transposed"], 2)
                gather(2, 3)

                def slot(g, p, q):
                    if q is not None:
                        pool.wait_ge(Z["transposed"], g + 3)
                        hold(pool, K)
                        gather(g + 3, 2 * g + 4)
                    pool.wait_ge(Z["scattered"], 32 * (g + 1))
                    hold(pool, K)
                    nc.gpsimd.tensor_copy(cur[:], table[:, bass.ds(2 * g, 2), :]).then_inc(Z["picked"], 1)
                    pool.wait_ge(Z["picked"], 2 * g + (4 if q is None else 5))
                    pool.wait_ge(Z["yv_ready"], g + 2)
                    hold(pool, K)
                    for s in two:
                        pool.indirect_dma_start(K["mixed"], bass.IndirectOffsetOnAxis(ap=cur[:, s, 0:1], axis=0), yv[:, s, :],
                                                None, compute_op=ALU.add).then_inc(Z["scattered"], 16)
                    if q is None:
                        pool.wait_ge(Z["scattered"], 32 * (g + 2))
                        hold(pool, K)

                def body(it, last=False):
                    for p in two:
                        slots_of(pool, 2 * it + p, p, slot, last and p == 1)
                body(0)
                with pool.Fori(1, E // 2 - 1) as it:
                    body(it)
                body(E // 2 - 1, last=True)

            @block.scalar
            def _(act):
                def biases(e, p):
                    act.dma_start(b1[p][:], K["eb1"][bass.ds(e, 1)].rearrange("o p m -> (o p) m")).then_inc(Z["bias_in"][p], 16)
                    act.dma_start(b2[p][:], K["eb2"][bass.ds(e, 1), :].partition_broadcast(P).rearrange("p o d -> p (o d)")).then_inc(Z["bias_in"][p], 16)

                def take_rows(g):
                    act.wait_ge(Z["transposed"], g + 1)
                    wait(act, Z["x_ready"], g)
                    nc.scalar.activation(xf[:], ps_t[:].rearrange("p (c n) -> p c n", c=NC), ACT.Copy).then_inc(Z["xf_ready"], 1)

                def gelu(g, q):
                    for k in range(4):
                        act.wait_ge(Z["hid_ps"], g * 4 + (k + 5))
                        wait(act, Z["g_ready"], g * 4 + (k + 1))
                        for m in (2 * k, 2 * k + 1):
                            ins = nc.scalar.activation(gf[:, m], ps_h[k][:, (m % 2) * STEP:(m % 2) * STEP + STEP],
                                                       ACT.Gelu, bias=b1[q][:, m:m + 1])
                        ins.then_inc(Z["gelu_ready"], 1)

                biases(0, 0)
                act.sem_inc(Z["yv_ready"], 1)
                take_rows(0)
                act.wait_ge(Z["bias_in"][0], 32)
                gelu(-1, 0)
                take_rows(1)

                def slot(g, p, q):
                    if q is not None:
                        gelu(g, q)
                        take_rows(g + 2)
                    act.wait_ge(Z["picked"], 2 * g + (4 if q is None else 5))
                    act.wait_ge(Z["yb_ready"], g + 2)
                    for s in two:
                        ins = nc.scalar.activation(yv[:, s], yb[:, s], ACT.Copy, scale=cur[:, s, 1:2].bitcast(F32))
                    ins.then_inc(Z["yv_ready"], 1)

                def body(it, last=False):
                    for p in two:
                        e = 2 * it + p
                        final = last and p == 1
                        if not final:
                            biases(e + 1, 1 - p)
                            act.wait_ge(Z["bias_in"][1 - p], 32 * (it + p + 1))
                            hold(act, K)
                        slots_of(act, e, p, slot, final)
                body(0)
                with act.Fori(1, E // 2 - 1) as it:
                    body(it)
                body(E // 2 - 1, last=True)

            @block.vector
            def _(dve):
                def split_weights(e, p):
                    dve.wait_ge(Z["raw_in"], 32 * (e + 1))
                    nc.vector.tensor_copy(w1_hi[p][:], w1f[:])
                    nc.vector.tensor_copy(w2_hi[p][:], w2f[:]).then_inc(Z["whi_ready"], 1)
                    dve.wait_ge(Z["whi_ready"], e + 1)
                    nc.vector.tensor_tensor(w1_lo[p][:], w1f[:], w1_hi[p][:].bitcast(F32), ALU.subtract)
                    nc.vector.tensor_tensor(w2_lo[p][:], w2f[:], w2_hi[p][:].bitcast(F32), ALU.subtract).then_inc(Z["w_ready"], 1)

                def split_rows(g):
                    dve.wait_ge(Z["xf_ready"], g + 1)
                    wait(dve, Z["hid_ps"], 4 * g)
                    nc.vector.tensor_copy(x_hi[:], xf[:]).then_inc(Z["x_hi_ready"], 1)
                    dve.wait_ge(Z["x_hi_ready"], g + 1)
                    nc.vector.tensor_tensor(x_lo[:], xf[:], x_hi[:].bitcast(F32), ALU.subtract).then_inc(Z["x_ready"], 1)

                def split_hidden(g, k):
                    n = g * 4 + (k + 5)
                    dve.wait_ge(Z["gelu_ready"], n)
                    wait(dve, Z["g_used"], g * 4 + (k + 1))
                    nc.vector.tensor_copy(g_hi[:, 2 * k:2 * k + 2], gf[:, 2 * k:2 * k + 2]).then_inc(Z["g_hi_ready"], 1)
                    dve.wait_ge(Z["g_hi_ready"], n)
                    nc.vector.tensor_tensor(g_lo[:, 2 * k:2 * k + 2], gf[:, 2 * k:2 * k + 2], g_hi[:, 2 * k:2 * k + 2].bitcast(F32),
                                            ALU.subtract).then_inc(Z["g_ready"], 1)

                dve.sem_inc(Z["yb_ready"], 1)
                split_weights(0, 0)
                split_rows(0)
                for k in range(4):
                    split_hidden(-1, k)
                split_rows(1)

                def slot(g, p, q):
                    for k in range(4):
                        if q is not None:
                            split_hidden(g, k)
                            if k == 1:
                                split_rows(g + 2)
                    dve.wait_ge(Z["g_used"], 4 * (g + 1))
                    dve.wait_ge(Z["yv_ready"], g + 1)
                    nc.vector.tensor_tensor(yb[:], ps_y[:].rearrange("p (s d) -> p s d", s=2),
                                            b2[p][:].rearrange("p (o d) -> p o d", o=1).to_broadcast([P, 2, D]), ALU.add
                                            ).then_inc(Z["yb_ready"], 1)

                def body(it, last=False):
                    for p in two:
                        e = 2 * it + p
                        final = last and p == 1
                        if not final:
                            wait(dve, Z["weights_used"], e)
                            split_weights(e + 1, 1 - p)
                        dve.wait_ge(Z["bias_in"][p], 32 * (it + 1))
                        hold(dve, K)
                        slots_of(dve, e, p, slot, final)
                body(0)
                with dve.Fori(1, E // 2 - 1) as it:
                    body(it)
                body(E // 2 - 1, last=True)

            @block.tensor
            def _(pe):
                def transposes(g):
                    pe.wait_ge(Z["gathered"], 32 * (g + 1))
                    wait(pe, Z["xf_ready"], g)
                    for c in range(NC):
                        for s in two:
                            last = nc.tensor.transpose(ps_t[:, c * STEP + s * P:c * STEP + (s + 1) * P], xg[:, s, c * P:(c + 1) * P], K["ident"][:])
                    last.then_inc(Z["transposed"], 1)

                def hidden(g, q):
                    pe.wait_ge(Z["x_ready"], g + 2)
                    for m in range(8):
                        if m % 2 == 0:
                            wait(pe, Z["gelu_ready"], g * 4 + (m // 2 + 1))
                        n = 0
                        for c in range(NC):
                            for w, a in ((w1_hi, x_hi), (w1_hi, x_lo), (w1_lo, x_hi)):
                                last = nc.tensor.matmul(ps_h[m // 2][:, (m % 2) * STEP:(m % 2) * STEP + STEP],
                                                        w[q][:, c, m * P:(m + 1) * P], a[:, c], start=(n == 0), stop=(n == 5))
                                n += 1
                        if m % 2:
                            last.then_inc(Z["hid_ps"], 1)

                transposes(0)
                pe.wait_ge(Z["w_ready"], 1)
                hidden(-1, 0)
                transposes(1)

                def slot(g, p, q):
                    if q is not None:
                        hidden(g, q)
                    pe.wait_ge(Z["yb_ready"], g + 1)
                    for k in range(4):
                        pe.wait_ge(Z["g_ready"], g * 4 + (k + 1))
                        for s in two:
                            n = 0
                            for c in (2 * k, 2 * k + 1):
                                for a, w in ((g_hi, w2_hi), (g_lo, w2_hi), (g_hi, w2_lo)):
                                    last = nc.tensor.matmul(ps_y[:, s * D:(s + 1) * D], a[:, c, s * P:(s + 1) * P], w[p][:, c, :],
                                                            start=(k == s == n == 0), stop=(k == 3 and s == 1 and n == 5), skip_group_check=True)
                                    n += 1
                        last.then_inc(Z["g_used"], 1)
                        if k == 1 and q is not None:
                            transposes(g + 2)

                def body(it, last=False):
                    for p in two:
                        e = 2 * it + p
                        final = last and p == 1
                        if not final:
                            pe.wait_ge(Z["w_ready"], e + 2)
                            hold(pe, K)
                        slots_of(pe, e, p, slot, final)
                        pe.drain().then_inc(Z["weights_used"], 1)
                body(0)
                with pe.Fori(1, E // 2 - 1) as it:
                    body(it)
                body(E // 2 - 1, last=True)


def finish(nc, K):
    with ExitStack() as ctx:
        sb = lambda name, shape, dt=F32: ctx.enter_context(nc.sbuf_tensor(name, shape, dt))
        sem = nc.alloc_semaphore
        two = range(2)
        acc = [sb(f"f_acc{u}", [P, NT, D]) for u in two]
        gb = [sb(f"f_gb{u}", [P, D]) for u in two]
        loaded, stored = [sem(f"f_loaded{u}") for u in two], [sem(f"f_stored{u}") for u in two]
        summed = sem("f_summed")
        with nc.Block() as block:
            @block.sync
            def _(sp):
                def body(it):
                    for u in two:
                        b = 2 * it + u
                        wait(sp, stored[u], 16 * it)
                        sp.dma_start(acc[u][:], K["mixed"][bass.ds(b * S, S), :].rearrange("(i p) d -> p i d", p=P)).then_inc(loaded[u], 16)
                        sp.dma_start(gb[u][:], K["mod_rows"][1, bass.ds(b, 1), 5 * D:6 * D].partition_broadcast(P)
                                     .rearrange("p o d -> p (o d)")).then_inc(loaded[u], 16)
                passes(sp, B // 2, body)

            @block.scalar
            def _(act):
                def body(it):
                    for u in two:
                        act.wait_ge(summed, 2 * at(it, u))
                        act.dma_start(K["out"][bass.ds(2 * it + u, 1)].rearrange("o (i p) d -> p (o i) d", p=P), acc[u][:]).then_inc(stored[u], 16)
                passes(act, B // 2, body)
                for u in two:
                    act.wait_ge(stored[u], 16 * (B // 2))

            @block.vector
            def _(dve):
                def body(it):
                    for u in two:
                        dve.wait_ge(loaded[u], 32 * (it + 1))
                        nc.vector.tensor_tensor(acc[u][:], acc[u][:], gb[u][:].rearrange("p (o d) -> p o d", o=1).to_broadcast([P, NT, D]),
                                                ALU.mult).then_inc(summed, 1)
                        dve.wait_ge(summed, 2 * at(it, u) - 1)
                        nc.vector.tensor_tensor(acc[u][:], acc[u][:], K["x_sb"][:, bass.ds((2 * it + u) * NT, NT), :], ALU.add).then_inc(summed, 1)
                passes(dve, B // 2, body)
def lay_out(a):
    import numpy as np
    t = lambda x: np.ascontiguousarray(np.swapaxes(x, 0, 1))
    col = lambda x: np.ascontiguousarray(x.reshape(-1, P).T)
    cols = lambda c: np.ascontiguousarray(c.reshape(B, NC, P).transpose(2, 1, 0))
    return {
        "x": a["L0_attn_h"], "ct0": cols(a["L0_c"]), "ct1": cols(a["L1_c"]), "wmod0": a["L0_wmod"], "wmod1": a["L1_wmod"],
        "wqkv": a["L0_attn_Wqvk"], "wo": a["L0_attn_Wo"],
        "w0t": t(a["L0_ffn_weight"]), "a1": a["L0_ffn_aux_weight1"], "a2": a["L0_ffn_aux_weight2"], "bias0": a["L0_ffn_bias"],
        "win": t(a["L1_attn_in_proj_w"]), "opt": t(a["L1_attn_out_proj_w"]), "coupling": a["L1_attn_coupling"],
        "freq": a["L1_attn_frequency"].reshape(KS, 1), "decay": a["L1_attn_log_decay"].reshape(KS, 1),
        "gate_wt": t(a["L1_attn_gate_w"]), "gate_b": a["L1_attn_gate_b"], "w1t": t(a["L1_attn_mlp_w1"]), "w2t": t(a["L1_attn_mlp_w2"]),
        "b1": col(a["L1_attn_mlp_b1"]), "b2": a["L1_attn_mlp_b2"], "n1g": col(a["L1_attn_n1_g"]), "n1b": col(a["L1_attn_n1_b"]),
        "n2g": col(a["L1_attn_n2_g"]), "n2b": col(a["L1_attn_n2_b"]), "wr": a["L1_ffn_Wr"],
        "br": a["L1_ffn_br"], "ew1": a["L1_ffn_W1"], "ew2": a["L1_ffn_W2"], "eb2": a["L1_ffn_b2"],
        "eb1": np.ascontiguousarray(a["L1_ffn_b1"].reshape(E, 8, P).swapaxes(1, 2)),
    }
def adaln_two_layers(nc, I, out):
    with ExitStack() as ctx:
        sb = lambda name, shape, dt=F32: ctx.enter_context(nc.sbuf_tensor(name, shape, dt))
        dram = lambda name, shape, dt=F32: nc.dram_tensor(name, shape, dt, kind="Internal").ap()
        K = dict(I)
        K["x_sb"] = sb("x_sb", [P, T, D])
        K["logits"] = sb("logits", [P, T, 8])
        K["mod_cols"] = sb("mod_cols", [P, 2, 12, B])
        K["ident"] = sb("ident", [P, P])
        K["identb"] = sb("identb", [P, P], BF16)
        K["mod_rows"] = dram("mod_rows", [2, B, 6 * D])
        K["qk_parts"] = dram("qk_parts", [B * G * 2, 3, HD, 4, S], BF16)
        K["attended"] = dram("attended", [B * G * P, S])
        K["inverse"] = dram("inverse", [P, S])
        K["h_rows"] = dram("h_rows", [B * S + STEP, D])
        K["mixed"] = dram("mixed", [B * S + STEP, D])
        K["table"] = dram("table", [P * TILES, 2], I32)
        K["steps"] = sb("steps", [P, E], I32)
        K["base"] = sb("base", [P, E], I32)
        K["final"] = sb("final", [P, E], I32)
        K["ranks"] = sb("ranks", [P, 1], I32)
        K["out"] = out
        K["held"] = nc.alloc_semaphore("held")
        with ExitStack() as first:
            K["causal"] = first.enter_context(nc.sbuf_tensor("causal", [P, S], F32))
            setup_modulation(nc, K)
            K["v"] = first.enter_context(nc.sbuf_tensor("v_sb", [P, T, D], F32))
            project_qkv(nc, K)
            attend(nc, K)
        with ExitStack() as second:
            W = {}
            for name, shape, dt in (("wo", [P, G, D], F32), ("mt", [P, D], F32), ("mts", [P, D], F32), ("wr", [P, NC, 8], F32),
                                    ("sin", [P, S], F32), ("cos", [P, S], F32), ("mag", [P, S], F32), ("bias0", [P, D], F32),
                                    ("gate_b", [P, D], F32), ("b2", [P, D], F32), ("n1g", [P, NC], F32), ("n1b", [P, NC], F32),
                                    ("n2g", [P, NC], F32), ("n2b", [P, NC], F32), ("b1", [P, 8], F32)):
                W[name] = second.enter_context(nc.sbuf_tensor("w_" + name, shape, dt))
            for name, shape in (("wc", [P, NC, D]), ("win", [P, NC, P]), ("wins", [P, NC, P]), ("gate", [P, NC, D]),
                                ("w1", [P, NC, 4 * D]), ("w2", [P, 8, D])):
                for part in ("_hi", "_lo"):
                    W[name + part] = second.enter_context(nc.sbuf_tensor("w_" + name + part, shape, F32R))
            prepare_middle(nc, K, W)
            middle(nc, K, W)
        route(nc, K)
        experts(nc, K)
        finish(nc, K)


def kernel(**inputs):
    import concourse.bacc as bacc
    from concourse.bass_utils import run_bass_kernel_spmd

    arrays = lay_out({name: np.asarray(a) for name, a in inputs.items()})
    arrays = {f"in_{name}_dram": np.ascontiguousarray(a) for name, a in arrays.items()}
    nc = bacc.Bacc("TRN2", target_bir_lowering=False, num_devices=1)
    given = {name[3:-5]: nc.dram_tensor(name, a.shape, mybir.dt.from_np(a.dtype), kind="ExternalInput").ap()
             for name, a in arrays.items()}
    out = nc.dram_tensor("out_0_dram", (B, S, D), F32, kind="ExternalOutput").ap()
    adaln_two_layers(nc, given, out)
    nc.compile() if not nc.is_finalized() else None
    return run_bass_kernel_spmd(nc, [arrays], core_ids=[0]).results[0]["out_0_dram"]
```

```python
import numpy as np
import concourse.bass as bass
from concourse import mybir
from contextlib import ExitStack

F32 = mybir.dt.float32
F32R = mybir.dt.float32r
BF16 = mybir.dt.bfloat16
I32 = mybir.dt.int32
ACT = mybir.ActivationFunctionType
ALU = mybir.AluOpType
AX = mybir.AxisListType

B, S, D, H = 8, 512, 256, 16
HD = D // H
P = 128
NT = S // P
NC = D // P
T = B * NT
G = H // 4
TERMS = 6
Q_RUNS = (slice(0, 3), slice(0, 2), slice(0, 1))
K_RUNS = (slice(0, 2), slice(0, 2), slice(0, 3, 2))
LOADS = len(Q_RUNS) + len(K_RUNS)
KR = TERMS * HD
EPS = 1e-5
LOW = -3.0e38


def wait(eng, sem, value):
    if isinstance(value, int) and value <= 0:
        return
    eng.wait_ge(sem, value)


def hold(eng, K):
    eng.sem_inc(K["held"], 1)


def passes(eng, n, body, last_apart=False):
    body(0)
    with eng.Fori(1, n - 1 if last_apart else n) as i:
        body(i)
    if last_apart:
        body(n - 1)


def at(it, u, j=0, n=1):
    return it * (2 * n) + (2 * j + u + 1)


class Order:

    def __init__(self, eng, sem, per_pass):
        self.eng, self.sem, self.per_pass, self.n, self.base = eng, sem, per_pass, 0, 0

    def at(self, i):
        self.base, self.n = i * self.per_pass, 0

    def link(self, ins):
        self.n += 1
        ins.then_inc(self.sem, 1)
        self.eng.wait_ge(self.sem, self.base + self.n)

    def done(self):
        assert self.n == self.per_pass, (self.n, self.per_pass)


ROWS = ((0, 2), (0, 5)) + tuple((1, j) for j in range(6))


def setup_modulation(nc, K):
    with ExitStack() as ctx:
        sb = lambda name, shape, dt=F32: ctx.enter_context(nc.sbuf_tensor(name, shape, dt))
        wmod = sb("wmod", [P, 2, NC, 6 * D])
        ct = sb("ct", [P, 2, NC, B])
        silu = sb("silu", [P, 2, NC, B])
        rows = sb("rows", [B, len(ROWS), D])
        sign, size = sb("sign", [B, D]), sb("size", [B, D])
        w = sb("qkv_w", [P, NC, 3 * D])
        ps_col = ctx.enter_context(nc.psum_tensor("ps_col", [P, 512], F32))
        ps_row = [ctx.enter_context(nc.psum_tensor(f"ps_row{j}", [P, 512], F32)) for j in range(len(ROWS) // 2)]
        w_in = nc.alloc_semaphore("mod_w_in")
        w1_in = nc.alloc_semaphore("mod_w1_in")
        x_in = nc.alloc_semaphore("mod_x_in")
        wqkv_in = nc.alloc_semaphore("mod_wqkv_in")
        silu_ready = nc.alloc_semaphore("mod_silu_ready")
        cols_ready = nc.alloc_semaphore("mod_cols_ready")
        rows_ready = nc.alloc_semaphore("mod_rows_ready")
        fixed = nc.alloc_semaphore("mod_fixed")
        stored = nc.alloc_semaphore("mod_stored")
        squares = nc.alloc_semaphore("mod_squares")
        order = nc.alloc_semaphore("mod_dve_order")

        with nc.Block() as block:
            @block.sync
            def _(sp):
                for l in range(2):
                    sp.dma_start(ct[:, l], K[f"ct{l}"]).then_inc(w_in, 16)
                for l, loaded in ((0, w_in), (1, w1_in)):
                    sp.dma_start(wmod[:, l], K[f"wmod{l}"].rearrange("(c p) n -> p c n", p=P)).then_inc(loaded, 16)
                for b in range(B):
                    sp.dma_start(K["x_sb"][:, b * NT:(b + 1) * NT, :],
                                 K["x"][b].rearrange("(i p) d -> p i d", p=P)).then_inc(x_in, 16)
                sp.wait_ge(fixed, 1)
                sp.dma_start(K["mod_rows"], rows[:]).then_inc(stored, 16)
                sp.wait_ge(stored, 16)
                sp.wait_ge(x_in, 16 * B)

            @block.scalar
            def _(act):
                act.dma_start(w[:], K["wqkv"].rearrange("(c p) n -> p c n", p=P)).then_inc(wqkv_in, 16)
                act.wait_ge(w_in, 48)
                nc.scalar.activation(silu[:], ct[:], ACT.Silu).then_inc(silu_ready, 1)

            @block.tensor
            def _(pe):
                pe.wait_ge(silu_ready, 1)
                for j in (0, 1, 3, 4):
                    for m in (j * NC, j * NC + 1):
                        for c in range(NC):
                            last = nc.tensor.matmul(ps_col[:, m * B:(m + 1) * B], wmod[:, 0, c, m * P:(m + 1) * P],
                                                    silu[:, 0, c, :], start=(c == 0), stop=(c == NC - 1))
                last.then_inc(cols_ready, 1)
                for n, (l, j) in enumerate(ROWS):
                    if n == 2:
                        pe.wait_ge(w1_in, 16)
                    for c in range(NC):
                        last = nc.tensor.matmul(ps_row[n // 2][0:B, n % 2 * D:(n % 2 + 1) * D], silu[:, l, c, :],
                                                wmod[:, l, c, j * D:(j + 1) * D], start=(c == 0), stop=(c == NC - 1))
                    if n % 2:
                        last.then_inc(rows_ready, 1)

            @block.vector
            def _(dve):
                ord_ = Order(dve, order, 0)
                dve.wait_ge(wqkv_in, 16)
                ord_.link(nc.vector.tensor_copy(K["w_hi"][:], w[:]))
                nc.vector.tensor_tensor(K["w_lo"][:], w[:], K["w_hi"][:].bitcast(F32), ALU.subtract)
                dve.wait_ge(cols_ready, 1)
                for j in (0, 1, 3, 4):
                    nc.vector.tensor_scalar(K["mod_cols"][:, j * NC:(j + 1) * NC, :],
                                            ps_col[:, j * NC * B:(j + 1) * NC * B].rearrange("p (m b) -> p m b", b=B),
                                            1.0 if j in (1, 4) else 0.0, None, ALU.add)
                for n, (l, j) in enumerate(ROWS):
                    dve.wait_ge(rows_ready, n // 2 + 1)
                    src, row = ps_row[n // 2][0:B, n % 2 * D:(n % 2 + 1) * D], rows[:, n, :]
                    if j in (2, 5):
                        ord_.link(nc.vector.tensor_copy(row, src))
                        ord_.link(nc.vector.tensor_scalar(sign[:], row, 0.0, 2.0, ALU.is_ge, ALU.mult))
                        ord_.link(nc.vector.scalar_tensor_tensor(size[:], row, -1.0, row, ALU.mult, ALU.max))
                        ord_.link(nc.vector.tensor_scalar(size[:], size[:], 0.25, None, ALU.max))
                        ord_.link(nc.vector.scalar_tensor_tensor(row, sign[:], -1.0, size[:], ALU.add, ALU.mult))
                    else:
                        ord_.link(nc.vector.tensor_scalar(row, src, 1.0 if j in (1, 4) else 0.0, None, ALU.add))
                dve.sem_inc(fixed, 1)

            @block.gpsimd
            def _(pool):
                nc.gpsimd.memset(K["ident"][:], 0.0).then_inc(squares, 1)
                nc.gpsimd.memset(K["identb"][:], 0.0).then_inc(squares, 1)
                nc.gpsimd.memset(K["causal"][:], 0.0).then_inc(squares, 1)
                pool.wait_ge(squares, 3)
                for m in ("ident", "identb"):
                    nc.gpsimd.affine_select(out=K[m][:], in_=K[m][:], compare_op=ALU.not_equal, fill=1.0, base=0,
                                            pattern=[[-1, P]], channel_multiplier=1).then_inc(squares, 1)
                tri = K["causal"][:, S - P:S]
                nc.gpsimd.affine_select(out=tri, in_=tri, compare_op=ALU.is_ge, fill=LOW, base=0,
                                        pattern=[[-1, P]], channel_multiplier=1).then_inc(squares, 1)
                pool.wait_ge(squares, 6)


def means_and_variances(nc, K, dve, link, src, stats, mv):
    hold(dve, K)
    for i, x in enumerate(src):
        last = nc.vector.bn_stats(stats[:, i, :], x)
    link(last)
    hold(dve, K)
    for i in range(len(src)):
        last = nc.vector.bn_aggr(mv[:, i, :], stats[:, i, :])
    return last


def inverse_roots(nc, link, mv, root):
    v, y, t = root[:, 0], root[:, 1], root[:, 2]
    link(nc.vector.tensor_scalar(v, mv[:, :, 1], EPS, None, ALU.add))
    link(nc.vector.tensor_scalar(y.bitcast(I32), v.bitcast(I32), -0.5, float(0x5F3759DF), ALU.mult, ALU.add))
    link(nc.vector.tensor_tensor(t, y, y, ALU.mult))
    link(nc.vector.tensor_tensor(t, t, v, ALU.mult))
    link(nc.vector.scalar_tensor_tensor(t, t, -10 / 3, t, ALU.add, ALU.mult))
    link(nc.vector.scalar_tensor_tensor(y, t, 5.0, y, ALU.add, ALU.mult))
    link(nc.vector.tensor_tensor(t, y, y, ALU.mult))
    link(nc.vector.scalar_tensor_tensor(t, t, -0.5 * 0.375 ** 3, v, ALU.mult, ALU.mult))
    return nc.vector.scalar_tensor_tensor(y, t, 1.5 * 0.375, y, ALU.add, ALU.mult)


def layer_norm(nc, K, dve, link, src, stats, mv, root, dst, ready):
    link(means_and_variances(nc, K, dve, link, src, stats, mv))
    link(inverse_roots(nc, link, mv, root))
    for i in range(len(src)):
        last = nc.vector.tensor_scalar(dst[i], src[i], mv[:, i, 0:1], root[:, 1, i:i + 1], ALU.subtract, ALU.mult)
        if i % NT == NT - 1:
            last.then_inc(ready, 1)


ROOT_LINKS = 2 + 7
LN_LINKS = 2 + ROOT_LINKS


def project_qkv(nc, K):
    with ExitStack() as ctx:
        sb = lambda name, shape, dt=F32: ctx.enter_context(nc.sbuf_tensor(name, shape, dt))
        w_hi, w_lo = K["w_hi"], K["w_lo"]
        two = range(2)
        stats, mv, root = sb("q_stats", [P, 2 * NT, 6]), sb("q_mv", [P, 2 * NT, 2]), sb("q_root", [P, 3, 2 * NT])
        xn = [sb(f"q_xn{u}", [P, NT, D]) for u in two]
        mod = [sb(f"q_mod{u}", [P, 4, 1]) for u in two]
        h = [sb(f"q_h{u}", [P, NC, S]) for u in two]
        h_hi = [sb(f"q_h_hi{u}", [P, NC, S], F32R) for u in two]
        h_lo = [sb(f"q_h_lo{u}", [P, NC, S], F32R) for u in two]
        rest = [sb(f"q_rest{u}", [P, 4, S]) for u in two]
        parts = [sb(f"q_parts{u}", [P, 4, 3, S], BF16) for u in two]
        ps = [[ctx.enter_context(nc.psum_tensor(f"q_ps{u}{j}", [P, 512], F32)) for j in range(4)] for u in two]
        sem = nc.alloc_semaphore
        mod_ready = sem("q_mod_ready")
        xn_ready, xt_ready, h_ready, hlo_ready = sem("q_xn_ready"), sem("q_xt_ready"), sem("q_h_ready"), sem("q_hlo_ready")
        qk_ready, hi_ready, rest_ready, mid_ready, lo_ready = (sem("q_qk_ready"), sem("q_hi_ready"), sem("q_rest_ready"),
                                                               sem("q_mid_ready"), sem("q_lo_ready"))
        v_ready, v_kept = sem("q_v_ready"), sem("q_v_kept")
        parts_out = [sem(f"q_parts_out{u}") for u in two]
        order = sem("q_dve_order")
        COLS = (0, P, 2 * D, 2 * D + P)

        with nc.Block() as block:
            @block.sync
            def _(sp):
                def body(it):
                    for m in range(4):
                        for u in two:
                            sp.wait_ge(lo_ready, at(it, u, m, 4))
                            for g in range(2):
                                for a in range(3):
                                    quad = (2 * it + u) * G + (m % 2) * 2 + g
                                    sp.dma_start(K["qk_parts"][bass.ds(quad * 2 + m // 2, 1), a].rearrange("o d h s -> (o h) d s"),
                                                 parts[u][64 * g:64 * g + 64, m, a]).then_inc(parts_out[u], 16)
                passes(sp, B // 2, body)
                for u in two:
                    sp.wait_ge(parts_out[u], 16 * 24 * (B // 2))

            @block.gpsimd
            def _(pool):
                def body(it):
                    for u in two:
                        wait(pool, h_ready, at(it - 1, u))
                        hold(pool, K)
                        nc.gpsimd.tensor_copy(mod[u][:], K["mod_cols"][:, 0:4, bass.ds(2 * it + u, 1)]).then_inc(mod_ready, 1)
                    for m in range(4):
                        for u in two:
                            wait(pool, parts_out[u], 384 * it)
                            pool.wait_ge(rest_ready, at(it, u, m, 4))
                            hold(pool, K)
                            nc.gpsimd.tensor_copy(parts[u][:, m, 1], rest[u][:, m]).then_inc(mid_ready, 1)
                passes(pool, B // 2, body)

            @block.scalar
            def _(act):
                def body(it):
                    for u in two:
                        act.wait_ge(xt_ready, at(it, u))
                        act.wait_ge(mod_ready, at(it, u))
                        wait(act, v_ready, at(it - 1, u, 1, 2))
                        for c in range(NC):
                            sc, sh = mod[u][:, 2 + c], mod[u][:, c]
                            nc.scalar.activation(h[u][:, c], ps[u][c][:], ACT.Identity, bias=sh, scale=sc)
                        for c in range(NC):
                            sc, sh = mod[u][:, 2 + c], mod[u][:, c]
                            last = nc.scalar.activation(h_hi[u][:, c], ps[u][c][:], ACT.Identity, bias=sh, scale=sc)
                        last.then_inc(h_ready, 1)
                    for m in range(4):
                        for u in two:
                            act.wait_ge(qk_ready, at(it, u, m, 4))
                            wait(act, parts_out[u], 384 * it)
                            nc.scalar.activation(parts[u][:, m, 0], ps[u][(m + 2) % 4][:], ACT.Copy).then_inc(hi_ready, 1)
                    for j in two:
                        for u in two:
                            act.wait_ge(v_ready, at(it, u, j, 2))
                            nc.scalar.activation(K["v"][:, bass.ds((2 * it + u) * NT + 2 * j, 2), :],
                                                 ps[u][2 + j][:].rearrange("p (i d) -> p i d", i=2), ACT.Copy).then_inc(v_kept, 1)
                passes(act, B // 2, body)

            @block.vector
            def _(dve):
                ord_ = Order(dve, order, LN_LINKS)
                def body(it):
                    ord_.at(it)
                    for u in two:
                        wait(dve, xt_ready, at(it - 1, u))
                    layer_norm(nc, K, dve, ord_.link, [K["x_sb"][:, bass.ds(2 * NT * it + i, 1), :] for i in range(2 * NT)], stats, mv, root,
                               [xn[u][:, i, :] for u in two for i in range(NT)], xn_ready)
                    for u in two:
                        dve.wait_ge(h_ready, at(it, u))
                        nc.vector.tensor_tensor(h_lo[u][:], h[u][:], h_hi[u][:].bitcast(F32), ALU.subtract).then_inc(hlo_ready, 1)
                    for m in range(5):
                        for u in two:
                            if m < 4:
                                dve.wait_ge(hi_ready, at(it, u, m, 4))
                                nc.vector.tensor_tensor(rest[u][:, m], ps[u][(m + 2) % 4][:], parts[u][:, m, 0],
                                                        ALU.subtract).then_inc(rest_ready, 1)
                        for u in two:
                            if m > 0:
                                dve.wait_ge(mid_ready, at(it, u, m - 1, 4))
                                nc.vector.tensor_tensor(parts[u][:, m - 1, 2], rest[u][:, m - 1], parts[u][:, m - 1, 1],
                                                        ALU.subtract).then_inc(lo_ready, 1)
                    ord_.done()
                passes(dve, B // 2, body)

            @block.tensor
            def _(pe):
                def body(it):
                    for u in two:
                        pe.wait_ge(xn_ready, at(it, u))
                        wait(pe, rest_ready, at(it - 1, u, 3, 4))
                        for c in range(NC):
                            for i in range(NT):
                                last = nc.tensor.transpose(ps[u][c][:, i * P:(i + 1) * P], xn[u][:, i, c * P:(c + 1) * P], K["ident"][:])
                        last.then_inc(xt_ready, 1)
                    for m in range(4):
                        for u in two:
                            pe.wait_ge(hlo_ready, at(it, u))
                            if m < 2:
                                wait(pe, v_kept, at(it - 1, u, m, 2))
                            bank, n = ps[u][(m + 2) % 4][:], 0
                            for c in range(NC):
                                for a, x in ((w_hi, h_hi), (w_hi, h_lo), (w_lo, h_hi)):
                                    last = nc.tensor.matmul(bank, a[:, c, COLS[m]:COLS[m] + P], x[u][:, c], start=(n == 0), stop=(n == 5))
                                    n += 1
                            last.then_inc(qk_ready, 1)
                    for j in two:
                        for u in two:
                            pe.wait_ge(rest_ready, at(it, u, j, 4))
                            for i in two:
                                n = 0
                                for c in range(NC):
                                    for x, a in ((h_hi, w_hi), (h_lo, w_hi), (h_hi, w_lo)):
                                        t = (2 * j + i) * P
                                        last = nc.tensor.matmul(ps[u][2 + j][:, i * D:(i + 1) * D], x[u][:, c, t:t + P],
                                                                a[:, c, D:2 * D], start=(n == 0), stop=(n == 5))
                                        n += 1
                            last.then_inc(v_ready, 1)
                passes(pe, B // 2, body)


EXP_JOBS = (((0, 0),), ((1, 0), (3, 384)), ((2, 0),))
MAX_JOBS = (((3, 0),), ((2, 0), (0, 384)), ((1, 0),))
EXP_AT = (0, 512, 1024, 896)
COLS = 1280


def attend(nc, K):
    with ExitStack() as ctx:
        sb = lambda name, shape, dt=F32: ctx.enter_context(nc.sbuf_tensor(name, shape, dt))
        ps = lambda name: ctx.enter_context(nc.psum_tensor(name, [P, 512], F32))
        sem = nc.alloc_semaphore
        NB = 4
        q_st = [sb(f"q_stack{g}", [KR + 3, 4, S], BF16) for g in range(NB)]
        k_st = [sb(f"k_stack{g}", [KR + 3, 4, S], BF16) for g in range(NB)]
        probs = [sb(f"probs{u}", [P, 4, COLS]) for u in range(2)]
        v1 = [sb(f"v_ones{u}", [P, NT, 4, HD + 1]) for u in range(2)]
        junk = sb("a_junk", [P, NT, S], BF16)
        mx = sb("a_mx", [P, NT, 4])
        mrest = sb("a_mrest", [P, 2, NT, 4])
        mparts = sb("a_mparts", [P, NT, 3, 4], BF16)
        mrow = sb("a_mrow", [12, S], BF16)
        ot = [sb(f"a_ot{u}", [P, S]) for u in range(2)]
        ps_max = [ps(f"a_ps_max{j}") for j in range(3)]
        ps_exp = [ps(f"a_ps_exp{j}") for j in range(3)]
        ps_out, ps_misc = ps("a_ps_out"), ps("a_ps_misc")
        ps_mt = ps_misc[:].bitcast(BF16)
        stack_in = [sem(f"a_stack_in{g}") for g in range(NB)]
        mrow_in = [sem(f"a_mrow_in{g}") for g in range(NB)]
        ot_out = [sem(f"a_ot_out{u}") for u in range(2)]
        ones_ready, v1_ready = sem("a_ones_ready"), sem("a_v1_ready")
        max_scores, max_read, mparts_ready, mt_ready, mrow_ready = (
            sem("a_max_scores"), sem("a_max_read"), sem("a_mparts_ready"), sem("a_mt_ready"), sem("a_mrow_ready"))
        exp_scores, exp_read, masked, pv_done = sem("a_exp_scores"), sem("a_exp_read"), sem("a_masked"), sem("a_pv_done")
        ot_ready = sem("a_ot_ready")
        order = sem("a_dve_order")

        with nc.Block() as block:
            @block.sync
            def _(sp):
                def load(n, g):
                    for st, a, runs in ((q_st, 0, Q_RUNS), (k_st, 1, K_RUNS)):
                        row = 0
                        for run in runs:
                            size = len(range(3)[run]) * HD
                            sp.dma_start(st[g][row:row + size, :, :].rearrange("p h s -> p (h s)"),
                                         K["qk_parts"][bass.ds(n * 2 + a, 1), run].rearrange("o a d h s -> (o a d) (h s)")
                                         if run.step is None else
                                         K["qk_parts"][bass.ds(n * 2 + a, 1), run].rearrange("o a d h s -> (o a) d (h s)")
                                         ).then_inc(stack_in[g], 16)
                            row += size

                def rows_of_max(n, g):
                    sp.wait_ge(mrow_ready, n + 1)
                    for j in range(3):
                        sp.dma_start(q_st[g][KR + j:KR + j + 1, :, :],
                                     mrow[4 * j:4 * j + 4, :]).then_inc(mrow_in[g], 16)

                def store(n, u):
                    sp.wait_ge(ot_ready, n + 1)
                    sp.dma_start(K["attended"][bass.ds(n * P, P), :], ot[u][:]).then_inc(ot_out[u], 16)

                def body(b, last=False):
                    for g in range(G):
                        n = b * G + g
                        if not (last and g > 0):
                            wait(sp, exp_scores, 12 * n)
                            load(n + 3, (g + 3) % NB)
                        if not (last and g == G - 1):
                            rows_of_max(n + 1, (g + 1) % NB)
                        if not (isinstance(n, int) and n < 2):
                            store(n - 2, g % 2)
                for g in range(3):
                    load(g, g)
                rows_of_max(0, 0)
                body(0)
                with sp.Fori(1, B - 1) as b:
                    body(b)
                body(B - 1, last=True)
                store(B * G - 2, 0)
                store(B * G - 1, 1)
                for u in range(2):
                    sp.wait_ge(ot_out[u], 16 * B * G // 2)

            @block.gpsimd
            def _(pool):
                for u in range(2):
                    nc.gpsimd.memset(v1[u][:, :, :, HD:HD + 1], 1.0).then_inc(ones_ready, 1)

                def body(b):
                    for g in range(G):
                        n, u = b * G + g, g % 2
                        wait(pool, pv_done, n - 1)
                        hold(pool, K)
                        nc.gpsimd.tensor_copy(v1[u][:, :, :, 0:HD],
                                              K["v"][:, bass.ds(b * NT, NT), g * 4 * HD:(g + 1) * 4 * HD]
                                              .rearrange("p i (h d) -> p i h d", d=HD)).then_inc(v1_ready, 1)
                        for h in range(4):
                            pool.wait_ge(exp_read, 12 * n + 3 * h + 3)
                            hold(pool, K)
                            for first in EXP_AT:
                                block_ = probs[u][:, h, first:first + P]
                                last = nc.gpsimd.affine_select(out=block_, in_=block_, compare_op=ALU.is_ge, fill=0.0, base=0,
                                                               pattern=[[1, P]], channel_multiplier=-1)
                            last.then_inc(masked, 1)
                body(0)
                with pool.Fori(1, B) as b:
                    body(b)

            @block.scalar
            def _(act):
                def keep_sums(n, u, stored):
                    act.wait_ge(pv_done, n + 1)
                    wait(act, ot_out[u], 16 * stored)
                    nc.scalar.activation(ot[u][:], ps_out[:], ACT.Copy).then_inc(ot_ready, 1)

                def copy_max_rows(n):
                    act.wait_ge(mt_ready, n + 1)
                    return nc.scalar.activation(mrow[:], ps_mt[0:12, 0:S], ACT.Copy).then_inc(mrow_ready, 1)

                def body(b, last=False):
                    for g in range(G):
                        n, u = b * G + g, g % 2
                        for h in range(4):
                            for j in range(3):
                                if h == 0:
                                    wait(act, pv_done, n - 1)
                                act.wait_ge(exp_scores, 12 * n + 3 * h + j + 1)
                                width = 256 if j == 2 else 512
                                nc.scalar.activation(probs[u][:, h, 512 * j:512 * j + width], ps_exp[j][:, 0:width],
                                                     ACT.Exp, scale=1.0 / D ** 0.5).then_inc(exp_read, 1)
                            if h == 1 and not (last and g == G - 1):
                                act.wait_ge(mrow_in[g], 48 * (b + 1))
                                copy_max_rows(n + 1)
                            if h == 0 and not (isinstance(n, int) and n < 2):
                                keep_sums(n - 2, u, 2 * b + g // 2 - 1)
                copy_max_rows(0)
                body(0)
                with act.Fori(1, B - 1) as b:
                    body(b)
                body(B - 1, last=True)
                keep_sums(B * G - 2, 0, 2 * B - 1)
                keep_sums(B * G - 1, 1, 2 * B - 1)

            @block.vector
            def _(dve):
                nc.vector.memset(ps_out[:], 0.0).then_inc(ones_ready, 1)
                for g in range(NB):
                    nc.vector.memset(k_st[g][KR:KR + 3, :, :], 1.0).then_inc(ones_ready, 1)
                LINKS = 4

                def maxima(n, h):
                    wait(dve, max_read, 12 * n + 3 * h)
                    for j in range(3):
                        dve.wait_ge(max_scores, 12 * n + 3 * h + j + 1)
                        hold(dve, K)
                        for i, col in MAX_JOBS[j]:
                            w = P * (i + 1)
                            last = nc.vector.tensor_tensor_reduce(
                                out=junk[:, i, 0:w], in0=ps_max[j][:, col:col + w], in1=K["causal"][:, S - w:S], scale=1.0,
                                scalar=LOW, op0=ALU.add, op1=ALU.max, accum_out=mx[:, i, h:h + 1])
                        last.then_inc(max_read, 1)

                def split_maxima(n, base):
                    ord_ = Order(dve, order, LINKS)
                    ord_.base = base
                    dve.wait_ge(max_read, 12 * n + 12)
                    wait(dve, mt_ready, n)
                    ord_.link(nc.vector.tensor_scalar(mparts[:, :, 0], mx[:], -1.0, None, ALU.mult))
                    ord_.link(nc.vector.scalar_tensor_tensor(mrest[:, 0], mx[:], -1.0, mparts[:, :, 0], ALU.mult, ALU.subtract))
                    ord_.link(nc.vector.tensor_copy(mparts[:, :, 1], mrest[:, 0]))
                    ord_.link(nc.vector.tensor_tensor(mrest[:, 1], mrest[:, 0], mparts[:, :, 1], ALU.subtract))
                    nc.vector.tensor_copy(mparts[:, :, 2], mrest[:, 1]).then_inc(mparts_ready, 1)

                def body(b, last=False):
                    for g in range(G):
                        n = b * G + g
                        for h in range(4):
                            if h == 0 and not (last and g == G - 1):
                                split_maxima(n + 1, (n + 1) * LINKS)
                            if not (last and g + 2 >= G):
                                maxima(n + 2, h)
                for h in range(4):
                    maxima(0, h)
                split_maxima(0, 0)
                for h in range(4):
                    maxima(1, h)
                body(0)
                with dve.Fori(1, B - 1) as b:
                    body(b)
                body(B - 1, last=True)

            @block.tensor
            def _(pe):
                def scores_for_max(n, b, g, h):
                    if h == 0:
                        pe.wait_ge(stack_in[g], 16 * LOADS * (b + 1))
                    for j in range(3):
                        wait(pe, max_read, 12 * n + 3 * h + j - 2)
                        for i, col in MAX_JOBS[j]:
                            last = nc.tensor.matmul(ps_max[j][:, col:col + P * (i + 1)], q_st[g][0:KR, h, P * i:P * (i + 1)],
                                                    k_st[g][0:KR, h, 0:P * (i + 1)], start=True, stop=True)
                        last.then_inc(max_scores, 1)

                def transpose_maxima(n):
                    pe.wait_ge(mparts_ready, n + 1)
                    wait(pe, mrow_ready, n)
                    for i in range(NT):
                        last = nc.tensor.transpose(ps_mt[0:12, i * P:(i + 1) * P],
                                                   mparts[:, i].rearrange("p a h -> p (a h)"), K["identb"][:])
                    last.then_inc(mt_ready, 1)

                def products_with_v(n, u, i):
                    if i == 0:
                        pe.wait_ge(masked, 4 * n + 4)
                        pe.wait_ge(v1_ready, n + 1)
                        wait(pe, ot_ready, n)
                    for h in range(4):
                        mm = nc.tensor.matmul(ps_out[32 * h:32 * h + HD + 1, P * i:S], v1[u][:, i, h, :],
                                              probs[u][:, h, EXP_AT[i]:EXP_AT[i] + S - P * i], start=(i == 0),
                                              stop=(i == NT - 1), skip_group_check=True)
                    if i == NT - 1:
                        mm.then_inc(pv_done, 1)

                def body(b, last=False):
                    for g in range(G):
                        n, u = b * G + g, g % 2
                        for h in range(4):
                            if not (last and g + 2 >= G):
                                scores_for_max(n + 2, b + (g + 2) // G, (g + 2) % G, h)
                            if h == 0:
                                pe.wait_ge(mrow_in[g], 48 * (b + 1))
                            for j in range(3):
                                wait(pe, exp_read, 12 * n + 3 * h + j - 2)
                                for i, col in EXP_JOBS[j]:
                                    last_mm = nc.tensor.matmul(ps_exp[j][:, col:col + S - P * i], k_st[g][:, h, P * i:P * (i + 1)],
                                                               q_st[g][:, h, P * i:S], start=True, stop=True)
                                last_mm.then_inc(exp_scores, 1)
                            if h == 0 and not (last and g == G - 1):
                                transpose_maxima(n + 1)
                            if not (isinstance(n, int) and n == 0):
                                for i in ((), (0,), (1,), (2, 3))[h]:
                                    products_with_v(n - 1, (u + 1) % 2, i)
                pe.wait_ge(ones_ready, NB + 3)
                for h in range(4):
                    scores_for_max(0, 0, 0, h)
                transpose_maxima(0)
                for h in range(4):
                    scores_for_max(1, 0, 1, h)
                body(0)
                with pe.Fori(1, B - 1) as b:
                    body(b)
                body(B - 1, last=True)
                for i in range(NT):
                    products_with_v(B * G - 1, 1, i)


TWO_PI = 2.0 * np.pi
PI_1 = 6.28125
PI_2 = float(np.float32(np.floor((TWO_PI - PI_1) * 2.0 ** 20) / 2.0 ** 20))
PI_3 = float(TWO_PI - PI_1 - PI_2)
ROUND = 12582912.0
PI_MAX = 3.1415925
KS = 64


def take_off_turns(nc, link, x, k, out):
    link(nc.vector.tensor_scalar(k, x, 1.0 / TWO_PI, ROUND, ALU.mult, ALU.add))
    link(nc.vector.tensor_scalar(k, k, ROUND, None, ALU.subtract))
    link(nc.vector.scalar_tensor_tensor(out, k, -PI_1, x, ALU.mult, ALU.add))
    link(nc.vector.scalar_tensor_tensor(out, k, -PI_2, out, ALU.mult, ALU.add))
    link(nc.vector.scalar_tensor_tensor(out, k, -PI_3, out, ALU.mult, ALU.add))


def prepare_middle(nc, K, W):
    with ExitStack() as ctx:
        sb = lambda name, shape, dt=F32: ctx.enter_context(nc.sbuf_tensor(name, shape, dt))
        sem = nc.alloc_semaphore
        den, inv = sb("m_den", [P, S]), sb("m_inv", [P, S])
        w0t, a1, a2, t1t = (sb(f"m_{n}", [P, NC, D]) for n in ("w0t", "a1", "a2", "t1t"))
        wc = sb("m_wc", [P, NC, D])
        opt = sb("m_opt", [P, D])
        bd, bds = sb("m_bd", [P, P]), sb("m_bds", [P, P])
        raw = {n: sb(f"m_raw_{n}", list(W[n + "_hi"].shape)) for n in ("win", "wins", "gate")}
        raw.update(w1=W["w1"], w2=W["w2"])
        freq, decay, e, k1 = (sb(f"m_{n}", [P, 1]) for n in ("freq", "decay", "e", "k1"))
        f_hi, f_lo = sb("m_f_hi", [P, 1], F32R), sb("m_f_lo", [P, 1])
        ni, nf, r, k, ang = sb("m_ni", [P, S], I32), sb("m_nf", [P, S]), sb("m_r", [P, S]), sb("m_k", [P, S]), sb("m_ang", [P, 2, S])
        ps = [ctx.enter_context(nc.psum_tensor(f"m_ps{j}", [P, 512], F32)) for j in range(6)]
        den_in, inv_ready, inv_out = sem("m_den_in"), sem("m_inv_ready"), sem("m_inv_out")
        chain_in, raw_in, small_in, cleared, bd_in = sem("m_chain_in"), sem("m_raw_in"), sem("m_small_in"), sem("m_cleared"), sem("m_bd_in")
        mm, copied, grid, order, angles, tables, wide_in = (
            sem("m_mm"), sem("m_copied"), sem("m_grid"), sem("m_order"), sem("m_angles"), sem("m_tables"), sem("m_wide_in"))
        exped = sem("m_exped")
        with nc.Block() as block:
            @block.sync
            def _(sp):
                for half in range(2):
                    sp.dma_start(freq[KS * half:KS * half + KS, :], K["freq"]).then_inc(small_in, 16)
                    sp.dma_start(decay[KS * half:KS * half + KS, :], K["decay"]).then_inc(small_in, 16)
                sp.dma_start(den[:], K["attended"].rearrange("(m r) s -> m r s", r=32)[:, HD, :]).then_inc(den_in, 16)
                for t, n in ((w0t, "w0t"), (a1, "a1"), (a2, "a2")):
                    sp.dma_start(t[:], K[n].rearrange("(c p) n -> p c n", p=P)).then_inc(chain_in, 16)
                sp.dma_start(opt[:], K["opt"]).then_inc(chain_in, 16)
                sp.wait_ge(cleared, 3)
                for half in range(2):
                    for h in range(4):
                        at_, col = KS * half + 16 * h, KS * half + 16 * h
                        other = KS * (1 - half) + 16 * h
                        sp.dma_start(bd[at_:at_ + 16, col:col + 16], K["coupling"][h]).then_inc(bd_in, 16)
                        sp.dma_start(bds[at_:at_ + 16, other:other + 16], K["coupling"][h]).then_inc(bd_in, 16)
                for h in range(4):
                    sp.dma_start(W["wo"][32 * h:32 * h + HD, :, :],
                                 K["wo"].rearrange("(g h d) n -> h d g n", h=4, d=HD)[h]).then_inc(wide_in, 16)
                sp.wait_ge(inv_ready, 1)
                sp.dma_start(K["inverse"], inv[:]).then_inc(inv_out, 16)
                sp.wait_ge(inv_out, 16)
                sp.wait_ge(wide_in, 16 * (4 + 9))

            @block.scalar
            def _(act):
                act.dma_start(raw["win"][:], K["win"].rearrange("(c p) n -> p c n", p=P)).then_inc(raw_in, 16)
                for half in range(2):
                    act.dma_start(raw["wins"][:, :, KS * half:KS * half + KS],
                                  K["win"].rearrange("(c p) n -> p c n", p=P)[:, :, KS - KS * half:2 * KS - KS * half]).then_inc(raw_in, 16)
                act.dma_start(raw["gate"][:], K["gate_wt"].rearrange("(c p) n -> p c n", p=P)).then_inc(raw_in, 16)
                act.dma_start(raw["w1"][:], K["w1t"].rearrange("(c p) n -> p c n", p=P)).then_inc(raw_in, 16)
                act.dma_start(raw["w2"][:], K["w2t"].rearrange("(c p) n -> p c n", p=P)).then_inc(raw_in, 16)
                for n in ("bias0", "gate_b", "b2"):
                    act.dma_start(W[n][:], K[n].rearrange("(o d) -> o d", o=1).partition_broadcast(P)
                                  .rearrange("p o d -> p (o d)")).then_inc(wide_in, 16)
                for n in ("n1g", "n1b", "n2g", "n2b", "b1"):
                    act.dma_start(W[n][:], K[n]).then_inc(wide_in, 16)
                act.dma_start(W["wr"][:], K["wr"].rearrange("(c p) e -> p c e", p=P)).then_inc(wide_in, 16)
                act.wait_ge(small_in, 64)
                nc.scalar.activation(e[:], decay[:], ACT.Exp, scale=-1.0).then_inc(exped, 1)
                act.wait_ge(angles, 1)
                nc.scalar.activation(W["sin"][:], ang[:, 0], ACT.Sin).then_inc(tables, 1)
                nc.scalar.activation(W["cos"][:], ang[:, 1], ACT.Sin).then_inc(tables, 1)

            @block.gpsimd
            def _(pool):
                nc.gpsimd.iota(ni[:], [[1, S]], base=0, channel_multiplier=0).then_inc(grid, 1)
                for t in (bd, bds, W["wo"]):
                    nc.gpsimd.memset(t[:], 0.0).then_inc(cleared, 1)

            @block.vector
            def _(dve):
                ord_ = Order(dve, order, 0)
                link = ord_.link
                dve.wait_ge(exped, 1)
                link(nc.vector.tensor_scalar(e[:], e[:], 1.0, None, ALU.add))
                link(nc.vector.reciprocal(k1[:], e[:]))
                link(nc.vector.memset(W["mag"][:], 0.0))
                link(nc.vector.tensor_scalar(W["mag"][:], W["mag"][:], k1[:, 0:1], None, ALU.add))
                dve.wait_ge(den_in, 16)
                nc.vector.reciprocal(inv[:], den[:]).then_inc(inv_ready, 1)
                take_off_turns(nc, link, freq[:], k1[:], freq[:])
                link(nc.vector.tensor_copy(f_hi[:], freq[:]))
                link(nc.vector.tensor_tensor(f_lo[:], freq[:], f_hi[:].bitcast(F32), ALU.subtract))
                dve.wait_ge(grid, 1)
                link(nc.vector.tensor_copy(nf[:], ni[:]))
                link(nc.vector.tensor_scalar(r[:], nf[:], f_hi[:, 0:1].bitcast(F32), None, ALU.mult))
                take_off_turns(nc, link, r[:], k[:], r[:])
                link(nc.vector.scalar_tensor_tensor(r[:], nf[:], f_lo[:, 0:1], r[:], ALU.mult, ALU.add))
                for j in range(2):
                    if j:
                        link(nc.vector.tensor_scalar(r[:], r[:], TWO_PI / 4, None, ALU.add))
                    take_off_turns(nc, link, r[:], k[:], ang[:, j])
                    link(nc.vector.tensor_scalar(ang[:, j], ang[:, j], -PI_MAX, PI_MAX, ALU.max, ALU.min))
                nc.vector.tensor_scalar(ang[KS:P, 0], ang[KS:P, 0], -1.0, None, ALU.mult).then_inc(angles, 1)
                dve.wait_ge(mm, 1)
                for m in range(NC):
                    last = nc.vector.tensor_copy(t1t[:, m], ps[m][:, 0:D])
                last.then_inc(copied, 1)
                dve.wait_ge(mm, 2)
                for m in range(NC):
                    last = nc.vector.tensor_copy(wc[:, m], ps[2 + m][:, 0:D])
                link(last)
                for m, t in enumerate((W["mt"], W["mts"])):
                    last = nc.vector.tensor_copy(t[:], ps[4 + m][:, 0:D])
                link(last)
                dve.wait_ge(raw_in, 96)
                for src, n in ((wc, "wc"), (raw["win"], "win"), (raw["wins"], "wins"), (raw["gate"], "gate")):
                    link(nc.vector.tensor_copy(W[n + "_hi"][:], src[:]))
                    last = nc.vector.tensor_tensor(W[n + "_lo"][:], src[:], W[n + "_hi"][:].bitcast(F32), ALU.subtract)
                link(last)

            @block.tensor
            def _(pe):
                pe.wait_ge(chain_in, 64)
                for m in range(NC):
                    for c in range(NC):
                        last = nc.tensor.matmul(ps[m][:, 0:D], a1[:, c, m * P:(m + 1) * P], w0t[:, c], start=(c == 0), stop=(c == 1))
                last.then_inc(mm, 1)
                pe.wait_ge(copied, 1)
                pe.wait_ge(bd_in, 16 * 16)
                for m in range(NC):
                    for c in range(NC):
                        nc.tensor.matmul(ps[2 + m][:, 0:D], t1t[:, c, m * P:(m + 1) * P], a2[:, c], start=(c == 0), stop=(c == 1))
                nc.tensor.matmul(ps[4][:, 0:D], bd[:], opt[:], start=True, stop=True)
                nc.tensor.matmul(ps[5][:, 0:D], bds[:], opt[:], start=True, stop=True).then_inc(mm, 1)


(ATTENDED, RESIDUAL1, CHAIN, TANH, RESIDUAL2, NORM, BETA, SCAN, RESIDUAL3, SPREAD, HIDDEN, OUTPUT, RESIDUAL4,
 EXPERT_ROWS, LOGITS) = STAGES = range(15)
MIDDLE = [x for s in STAGES for x in ((s + 12, 1, 1) if s < 3 else (s - 3, 0, 1), (s, 0, 0))]
NORM_LINKS = 2 + ROOT_LINKS


def middle(nc, K, W):
    with ExitStack() as ctx:
        sb = lambda name, shape, dt=F32: ctx.enter_context(nc.sbuf_tensor(name, shape, dt))
        two = range(2)
        A = [sb("c_a0", [P, 4, S]), W["a1"]]
        V = [sb("c_v0", [P, 4, S]), W["v1"]]
        xn = [sb(f"c_xn{u}", [P, NT, D]) for u in two]
        h = [sb(f"c_h{u}", [P, NC, S]) for u in two]
        h_hi = [sb(f"c_h_hi{u}", [P, NC, S], F32R) for u in two]
        h_lo = [sb(f"c_h_lo{u}", [P, NC, S], F32R) for u in two]
        rows = [sb(f"c_rows{u}", [P, 7, D]) for u in two]
        mod = [sb(f"c_mod{u}", [P, 4, 1]) for u in two]
        stats = sb("c_stats", [P, NT, 6])
        mv = [sb(f"c_mv{u}", [P, NT, 2]) for u in two]
        root = [sb(f"c_root{u}", [P, 3, NT]) for u in two]
        hid_hi, hid_lo = sb("c_hid_hi", [P, 8, S], F32R), sb("c_hid_lo", [P, 8, S], F32R)
        ps = [[ctx.enter_context(nc.psum_tensor(f"c_ps{u}{j}", [P, 512], F32)) for j in range(4)] for u in two]
        hres = [V[u][:, 0:2, :].rearrange("p a s -> p (a s)").rearrange("p (i d) -> p i d", d=D) for u in two]
        gate = [V[u][:, 2:4, :].rearrange("p a s -> p (a s)").rearrange("p (i d) -> p i d", d=D) for u in two]
        hidden = [[A[u][:, m] for m in range(4)] + [V[u][:, m] for m in (2, 3)] +
                  [xn[u][:, 2 * m:2 * m + 2].rearrange("p i d -> p (i d)") for m in two] for u in two]
        row = lambda u, j: rows[u][:, j:j + 1, :].to_broadcast([P, NT, D])
        tok = lambda u, j: [ps[u][j][:].rearrange("p (i d) -> p i d", i=2), ps[u][j + 1][:].rearrange("p (i d) -> p i d", i=2)]
        sem = nc.alloc_semaphore
        names = """att_in rows_in att_ready wo_ready x1_ready xn2 xt2 h2 lo2 z_ready zb_ready tanh_ready
                   xn3 xn4 xt4 h4 lo4 beta_ready gpre_ready gsum_ready gate_ready rot_ready o_ready x3_ready
                   xn5 xt5 h5 lo5 hid_ps hid_f hid_lo_ready y_ready b2_added x4_ready xn6 hrow_ready xt6 h6 h_out lg_ready lg_done
                   order""".split()
        PER_HALF = ("att_in", "rows_in", "h_out")
        Z = {n: sem("c_" + n) for n in names if n not in PER_HALF}
        for n in PER_HALF:
            Z[n] = [sem(f"c_{n}{u}") for u in two]

        def run(eng, stage, before_pass=None):
            def body(it):
                if before_pass:
                    before_pass(it)
                for s, lag, u in MIDDLE:
                    if not (lag and isinstance(it, int) and it == 0):
                        stage(s, it - lag, u)
            body(0)
            body(1)
            with eng.Fori(0, B // 2 - 2) as j:
                body(j + 2)
            if before_pass:
                before_pass(B // 2)
            for s, lag, u in MIDDLE:
                if lag:
                    stage(s, B // 2 - 1, u)

        with nc.Block() as block:
            @block.sync
            def _(sp):
                def stage(s, it, u):
                    b = 2 * it + u
                    if s == ATTENDED:
                        if u == 1 and isinstance(it, int) and it == 0:
                            sp.wait_ge(Z["order"], 4)
                        wait(sp, Z["x4_ready"], at(it - 1, u))
                        sp.dma_start(A[u][:], K["attended"][bass.ds(b * S, S), :].rearrange("(g p) s -> p g s", p=P)).then_inc(Z["att_in"][u], 16)
                        for h_ in range(4):
                            sp.dma_start(V[u][32 * h_:32 * h_ + 32, :, :],
                                         K["inverse"].rearrange("(n h) s -> h n s", h=4)[h_, bass.ds(b * G, G), :]
                                         .partition_broadcast(32)).then_inc(Z["att_in"][u], 16)
                        wait(sp, Z["hrow_ready"], 2 * at(it - 1, u))
                        for j, (l, m) in enumerate(((0, 2), (0, 5), (1, 1), (1, 0), (1, 2), (1, 4), (1, 3))):
                            sp.dma_start(rows[u][:, j, :], K["mod_rows"][bass.ds(b, 1), ROWS.index((l, m))]
                                         .partition_broadcast(P).rearrange("p o d -> p (o d)")).then_inc(Z["rows_in"][u], 16)
                    if s == LOGITS:
                        sp.wait_ge(Z["hrow_ready"], 2 * at(it, u))
                        sp.dma_start(K["h_rows"][bass.ds(b * S, S), :].rearrange("(i p) d -> p i d", p=P),
                                     xn[u][:]).then_inc(Z["h_out"][u], 16)
                run(sp, stage)
                for u in two:
                    sp.wait_ge(Z["h_out"][u], 16 * (B // 2))

            @block.gpsimd
            def _(pool):
                def stage(s, it, u):
                    if s == ATTENDED:
                        wait(pool, Z["h2"], at(it - 1, u))
                        hold(pool, K)
                        nc.gpsimd.tensor_copy(mod[u][:], K["mod_cols"][:, 6:10, bass.ds(2 * it + u, 1)])
                        pool.wait_ge(Z["att_in"][u], 80 * (it + 1))
                        for g in range(G):
                            last = nc.gpsimd.tensor_tensor(A[u][:, g], A[u][:, g], V[u][:, g], ALU.mult)
                        last.then_inc(Z["att_ready"], 1)
                    if s == HIDDEN:
                        pool.wait_ge(Z["xn5"], at(it, u))
                        hold(pool, K)
                        nc.gpsimd.tensor_tensor(hres[u], hres[u], W["b2"][:].rearrange("p (o d) -> p o d", o=1).to_broadcast([P, NT, D]),
                                                ALU.add).then_inc(Z["b2_added"], 1)
                    if s == EXPERT_ROWS:
                        pool.wait_ge(Z["xn6"], at(it, u))
                        hold(pool, K)
                        nc.gpsimd.tensor_tensor(xn[u][:], xn[u][:], row(u, 5), ALU.mult).then_inc(Z["hrow_ready"], 1)
                        pool.wait_ge(Z["hrow_ready"], 2 * at(it, u) - 1)
                        hold(pool, K)
                        nc.gpsimd.tensor_tensor(xn[u][:], xn[u][:], row(u, 6), ALU.add).then_inc(Z["hrow_ready"], 1)
                run(pool, stage)

            @block.scalar
            def _(act):
                cols = lambda t: [t[:, c:c + 1] for c in range(NC)]

                def spread(it, u, xt, done, scale, shift, used, bank):
                    act.wait_ge(Z[xt], at(it, u))
                    wait(act, *used)
                    for dst in (h, h_hi):
                        for c in range(NC):
                            last = nc.scalar.activation(dst[u][:, c], ps[u][bank + c][:], ACT.Identity, bias=shift[c], scale=scale[c])
                    last.then_inc(Z[done], 1)

                def stage(s, it, u):
                    if s == CHAIN:
                        act.wait_ge(Z["att_ready"], at(it, u))
                        spread(it, u, "xt2", "h2", [mod[u][:, 2 + c] for c in range(NC)], [mod[u][:, c] for c in range(NC)],
                               (Z["lg_ready"], at(it - 1, u)), 0)
                    if s == TANH:
                        act.wait_ge(Z["zb_ready"], at(it, u))
                        nc.scalar.activation(xn[u][:], xn[u][:], ACT.Tanh).then_inc(Z["tanh_ready"], 1)
                    if s == BETA:
                        spread(it, u, "xt4", "h4", cols(W["n1g"]), cols(W["n1b"]), (Z["z_ready"], at(it, u)), 0)
                    if s == SCAN:
                        act.wait_ge(Z["gsum_ready"], at(it, u))
                        nc.scalar.activation(gate[u], gate[u], ACT.Sigmoid).then_inc(Z["gate_ready"], 1)
                    if s == SPREAD:
                        spread(it, u, "xt5", "h5", cols(W["n2g"]), cols(W["n2b"]), (Z["gpre_ready"], at(it, u)), 2)
                    if s == HIDDEN:
                        wait(act, Z["y_ready"], 2 * it + u)
                        for m in range(8):
                            act.wait_ge(Z["hid_ps"], 8 * (2 * it + u) + (m + 1))
                            nc.scalar.activation(hidden[u][m], ps[u][m % 4][:], ACT.Silu, bias=W["b1"][:, m:m + 1])
                            nc.scalar.activation(hid_hi[:, m], ps[u][m % 4][:], ACT.Silu, bias=W["b1"][:, m:m + 1]).then_inc(Z["hid_f"], 1)
                    if s == LOGITS:
                        act.wait_ge(Z["xt6"], at(it, u))
                        for c in range(NC):
                            last = nc.scalar.activation(h[u][:, c], ps[u][2 + c][:], ACT.Copy)
                        last.then_inc(Z["h6"], 1)
                run(act, stage)

            @block.vector
            def _(dve):
                LINKS = {RESIDUAL1: 1 + NORM_LINKS, RESIDUAL2: 2 + NORM_LINKS, NORM: 2 + NORM_LINKS, SCAN: 3,
                         RESIDUAL3: 1 + NORM_LINKS, RESIDUAL4: 2 + NORM_LINKS}
                in_pass = sum(LINKS.get(s, 0) for s, lag, u in MIDDLE)
                lagging = sum(LINKS.get(s, 0) for s, lag, u in MIDDLE if lag)
                ord_ = Order(dve, Z["order"], in_pass)
                link = ord_.link
                whole = lambda t: t[:].rearrange("p (o d) -> p o d", o=1)

                def before_pass(it):
                    ord_.base, ord_.n = (4 if isinstance(it, int) and it == 0 else it * in_pass + (4 - lagging)), 0

                def norm(src, u, done):
                    link(means_and_variances(nc, K, dve, link, src, stats, mv[u]))
                    link(inverse_roots(nc, link, mv[u], root[u]))
                    for i in range(NT):
                        last = nc.vector.tensor_scalar(xn[u][:, i:i + 1], src[i], mv[u][:, i, 0:1], root[u][:, 1, i:i + 1], ALU.subtract, ALU.mult)
                    last.then_inc(Z[done], 1)

                def low(it, u, hs, lo):
                    dve.wait_ge(Z[hs], at(it, u))
                    nc.vector.tensor_tensor(h_lo[u][:], h[u][:], h_hi[u][:].bitcast(F32), ALU.subtract).then_inc(Z[lo], 1)

                def stage(s, it, u):
                    b = 2 * it + u
                    x = K["x_sb"][:, bass.ds(b * NT, NT), :]
                    xt = [K["x_sb"][:, bass.ds(b * NT + i, 1), :] for i in range(NT)]
                    ht = [hres[u][:, i:i + 1, :] for i in range(NT)]
                    if s == RESIDUAL1:
                        dve.wait_ge(Z["rows_in"][u], 16 * 7 * (it + 1))
                        wait(dve, Z["h_out"][u], 16 * it)
                        dve.wait_ge(Z["wo_ready"], at(it, u))
                        for j in two:
                            last = nc.vector.tensor_tensor(xn[u][:, 2 * j:2 * j + 2], tok(u, 2)[j], rows[u][:, 0:1, :].to_broadcast([P, 2, D]), ALU.mult)
                        link(last)
                        nc.vector.tensor_tensor(x, x, xn[u][:], ALU.add).then_inc(Z["x1_ready"], 1)
                        dve.wait_ge(Z["x1_ready"], at(it, u))
                        norm(xt, u, "xn2")
                    if s == CHAIN:
                        low(it, u, "h2", "lo2")
                    if s == TANH:
                        dve.wait_ge(Z["z_ready"], at(it, u))
                        for j in two:
                            last = nc.vector.tensor_tensor(xn[u][:, 2 * j:2 * j + 2], tok(u, 2)[j], whole(W["bias0"]).to_broadcast([P, 2, D]), ALU.add)
                        last.then_inc(Z["zb_ready"], 1)
                    if s == RESIDUAL2:
                        dve.wait_ge(Z["tanh_ready"], at(it, u))
                        link(nc.vector.tensor_tensor(xn[u][:], xn[u][:], row(u, 1), ALU.mult))
                        link(nc.vector.tensor_tensor(x, x, xn[u][:], ALU.add))
                        norm(xt, u, "xn3")
                    if s == NORM:
                        dve.wait_ge(Z["xn3"], at(it, u))
                        link(nc.vector.tensor_tensor(hres[u], xn[u][:], row(u, 2), ALU.mult))
                        link(nc.vector.tensor_tensor(hres[u], hres[u], row(u, 3), ALU.add))
                        norm(ht, u, "xn4")
                    if s == BETA:
                        low(it, u, "h4", "lo4")
                    if s == SCAN:
                        dve.wait_ge(Z["beta_ready"], at(it, u))
                        nc.vector.tensor_tensor(A[u][:, 0], ps[u][0][:], W["cos"][:], ALU.mult)
                        link(nc.vector.tensor_tensor(A[u][:, 1], ps[u][1][:], W["sin"][:], ALU.mult))
                        link(nc.vector.tensor_tensor(A[u][:, 0], A[u][:, 0], A[u][:, 1], ALU.add))
                        hold(dve, K)
                        link(nc.vector.tensor_tensor_scan(A[u][:, 1], W["mag"][:], A[u][:, 0], 0.0, ALU.mult, ALU.add))
                        nc.vector.tensor_tensor(A[u][:, 2], A[u][:, 1], W["cos"][:], ALU.mult)
                        nc.vector.tensor_tensor(A[u][:, 3], A[u][:, 1], W["sin"][:], ALU.mult).then_inc(Z["rot_ready"], 1)
                        dve.wait_ge(Z["gpre_ready"], at(it, u))
                        for j in two:
                            last = nc.vector.tensor_tensor(gate[u][:, 2 * j:2 * j + 2], tok(u, 2)[j], whole(W["gate_b"]).to_broadcast([P, 2, D]), ALU.add)
                        last.then_inc(Z["gsum_ready"], 1)
                    if s == RESIDUAL3:
                        dve.wait_ge(Z["gate_ready"], at(it, u))
                        dve.wait_ge(Z["o_ready"], at(it, u))
                        for j in two:
                            last = nc.vector.tensor_tensor(gate[u][:, 2 * j:2 * j + 2], gate[u][:, 2 * j:2 * j + 2], tok(u, 0)[j], ALU.mult)
                        link(last)
                        nc.vector.tensor_tensor(hres[u], hres[u], gate[u], ALU.add).then_inc(Z["x3_ready"], 1)
                        dve.wait_ge(Z["x3_ready"], at(it, u))
                        norm(ht, u, "xn5")
                    if s == SPREAD:
                        low(it, u, "h5", "lo5")
                    if s == OUTPUT:
                        for m in range(8):
                            dve.wait_ge(Z["hid_f"], 8 * (2 * it + u) + (m + 1))
                            nc.vector.tensor_tensor(hid_lo[:, m], hidden[u][m], hid_hi[:, m].bitcast(F32), ALU.subtract).then_inc(Z["hid_lo_ready"], 1)
                    if s == RESIDUAL4:
                        dve.wait_ge(Z["b2_added"], at(it, u))
                        dve.wait_ge(Z["y_ready"], at(it, u))
                        for j in two:
                            last = nc.vector.tensor_tensor(hres[u][:, 2 * j:2 * j + 2], hres[u][:, 2 * j:2 * j + 2], tok(u, 0)[j], ALU.add)
                        link(last)
                        link(nc.vector.tensor_tensor(hres[u], hres[u], row(u, 4), ALU.mult))
                        nc.vector.tensor_tensor(x, x, hres[u], ALU.add).then_inc(Z["x4_ready"], 1)
                        dve.wait_ge(Z["x4_ready"], at(it, u))
                        norm(xt, u, "xn6")
                    if s == LOGITS:
                        dve.wait_ge(Z["lg_ready"], at(it, u))
                        nc.vector.tensor_copy(K["logits"][:, bass.ds(b * NT, NT), :],
                                              ps[u][0][:, 0:NT * 8].rearrange("p (i e) -> p i e", e=8)).then_inc(Z["lg_done"], 1)
                for n in ("w1", "w2"):
                    link(nc.vector.tensor_copy(W[n + "_hi"][:], W[n][:]))
                    link(nc.vector.tensor_tensor(W[n + "_lo"][:], W[n][:], W[n + "_hi"][:].bitcast(F32), ALU.subtract))
                run(dve, stage, before_pass)

            @block.tensor
            def _(pe):
                def transposes(it, u, xns, xt, bank):
                    pe.wait_ge(Z[xns], at(it, u))
                    for c in range(NC):
                        for i in range(NT):
                            last = nc.tensor.transpose(ps[u][bank + c][:, i * P:(i + 1) * P], xn[u][:, i, c * P:(c + 1) * P], K["ident"][:])
                    last.then_inc(Z[xt], 1)

                def by_tokens(u, bank, x_hi, x_lo, w_hi, w_lo, done):
                    for i in range(NT):
                        out, n = ps[u][bank + i // 2][:, (i % 2) * D:(i % 2) * D + D], 0
                        t = slice(i * P, (i + 1) * P)
                        for c in range(NC):
                            for a, w in ((x_hi, w_hi), (x_lo, w_hi), (x_hi, w_lo)):
                                last = nc.tensor.matmul(out, a[:, c, t], w[:, c, :], start=(n == 0), stop=(n == 3 * NC - 1))
                                n += 1
                    last.then_inc(Z[done], 1)

                def by_features(out, w_hi, w_lo, cols, x_hi, x_lo):
                    n = 0
                    for c in range(NC):
                        for w, a in ((w_hi, x_hi), (w_hi, x_lo), (w_lo, x_hi)):
                            last = nc.tensor.matmul(out, w[:, c, cols], a[:, c], start=(n == 0), stop=(n == 3 * NC - 1))
                            n += 1
                    return last

                def stage(s, it, u):
                    if s == ATTENDED:
                        pe.wait_ge(Z["att_ready"], at(it, u))
                        wait(pe, Z["h6"], at(it - 1, u))
                        for i in range(NT):
                            for g in range(G):
                                last = nc.tensor.matmul(ps[u][2 + i // 2][:, (i % 2) * D:(i % 2) * D + D], A[u][:, g, i * P:(i + 1) * P],
                                                        W["wo"][:, g, :], start=(g == 0), stop=(g == G - 1))
                        last.then_inc(Z["wo_ready"], 1)
                    if s == RESIDUAL1:
                        wait(pe, Z["lg_done"], at(it - 1, u))
                        transposes(it, u, "xn2", "xt2", 0)
                    if s == CHAIN:
                        pe.wait_ge(Z["lo2"], at(it, u))
                        pe.wait_ge(Z["x1_ready"], at(it, u))
                        by_tokens(u, 2, h_hi[u], h_lo[u], W["wc_hi"], W["wc_lo"], "z_ready")
                    if s == NORM:
                        pe.wait_ge(Z["h2"], at(it, u))
                        transposes(it, u, "xn4", "xt4", 0)
                    if s == BETA:
                        pe.wait_ge(Z["lo4"], at(it, u))
                        by_features(ps[u][0][:], W["win_hi"], W["win_lo"], slice(0, P), h_hi[u], h_lo[u])
                        by_features(ps[u][1][:], W["wins_hi"], W["wins_lo"], slice(0, P), h_hi[u], h_lo[u]).then_inc(Z["beta_ready"], 1)
                        pe.wait_ge(Z["zb_ready"], at(it, u))
                        by_tokens(u, 2, h_hi[u], h_lo[u], W["gate_hi"], W["gate_lo"], "gpre_ready")
                    if s == SCAN:
                        pe.wait_ge(Z["rot_ready"], at(it, u))
                        for i in range(NT):
                            for n, m in enumerate(("mt", "mts")):
                                last = nc.tensor.matmul(ps[u][i // 2][:, (i % 2) * D:(i % 2) * D + D], A[u][:, 2 + n, i * P:(i + 1) * P],
                                                        W[m][:], start=(n == 0), stop=(n == 1))
                        last.then_inc(Z["o_ready"], 1)
                    if s == RESIDUAL3:
                        pe.wait_ge(Z["gsum_ready"], at(it, u))
                        transposes(it, u, "xn5", "xt5", 2)
                    if s == HIDDEN:
                        pe.wait_ge(Z["lo5"], at(it, u))
                        pe.wait_ge(Z["x3_ready"], at(it, u))
                        first = 8 * (2 * it + u)
                        for m in range(8):
                            if m >= 4:
                                pe.wait_ge(Z["hid_f"], first + (m - 3))
                            by_features(ps[u][m % 4][:], W["w1_hi"], W["w1_lo"], slice(m * P, (m + 1) * P), h_hi[u], h_lo[u]).then_inc(Z["hid_ps"], 1)
                    if s == OUTPUT:
                        first = 8 * (2 * it + u)
                        pe.wait_ge(Z["hid_f"], first + 6)
                        for m in range(8):
                            pe.wait_ge(Z["hid_lo_ready"], first + (m + 1))
                            for i in range(NT):
                                n = 0
                                for a, w in ((hid_hi, "w2_hi"), (hid_lo, "w2_hi"), (hid_hi, "w2_lo")):
                                    last = nc.tensor.matmul(ps[u][i // 2][:, (i % 2) * D:(i % 2) * D + D], a[:, m, i * P:(i + 1) * P], W[w][:, m, :],
                                                            start=(m == n == i % 2 == 0), stop=(m == 7 and n == 2 and i % 2 == 1), skip_group_check=True)
                                    n += 1
                        last.then_inc(Z["y_ready"], 1)
                    if s == LOGITS:
                        pe.wait_ge(Z["hid_f"], 8 * (2 * it + u) + 8)
                        pe.wait_ge(Z["hrow_ready"], 2 * at(it, u))
                        transposes(it, u, "xn6", "xt6", 2)
                        pe.wait_ge(Z["h6"], at(it, u))
                        pe.wait_ge(Z["x4_ready"], at(it, u))
                        for i in range(NT):
                            for c in range(NC):
                                last = nc.tensor.matmul(ps[u][0][:, 8 * i:8 * i + 8], h[u][:, c, i * P:(i + 1) * P], W["wr"][:, c, :],
                                                        start=(c == 0), stop=(c == NC - 1))
                        last.then_inc(Z["lg_ready"], 1)
                run(pe, stage)


E = 8
F = 4 * D
STEP = 2 * P
STEPS = B * S * E // STEP
TILES = 2 * (STEPS + 3)
NOWHERE = float(1 << 23)
SIDE = 8


def load_expert(eng, K, e):
    eng.dma_start(K["ew1f"][:], K["ew1"][bass.ds(e, 1)].rearrange("o (c p) n -> (o p) c n", p=P)).then_inc(K["raw_in"], 16)
    eng.dma_start(K["ew2f"][:], K["ew2"][bass.ds(e, 1)].rearrange("o (c p) n -> (o p) c n", p=P)).then_inc(K["raw_in"], 16)


def split_expert(nc, dve, K, e, p):
    dve.wait_ge(K["raw_in"], 32 * (e + 1))
    nc.vector.tensor_copy(K["ew1_hi"][p][:], K["ew1f"][:])
    nc.vector.tensor_copy(K["ew2_hi"][p][:], K["ew2f"][:]).then_inc(K["whi_ready"], 1)
    dve.wait_ge(K["whi_ready"], e + 1)
    nc.vector.tensor_tensor(K["ew1_lo"][p][:], K["ew1f"][:], K["ew1_hi"][p][:].bitcast(F32), ALU.subtract)
    nc.vector.tensor_tensor(K["ew2_lo"][p][:], K["ew2f"][:], K["ew2_hi"][p][:].bitcast(F32), ALU.subtract).then_inc(K["w_ready"], 1)


def route(nc, K):
    n = T * E
    with ExitStack() as ctx:
        sb = lambda name, shape, dt=F32: ctx.enter_context(nc.sbuf_tensor(name, shape, dt))
        sem = nc.alloc_semaphore
        lg, top, mask, ex, gate, rank = (sb(f"r_{x}", [P, T, E]) for x in ("lg", "top", "mask", "ex", "gate", "rank"))
        pos, sel, tmp = (sb(f"r_{x}", [P, T, E]) for x in ("pos", "sel", "tmp"))
        tot, run = sb("r_tot", [P, E, T]), sb("r_run", [P, E, T])
        same_token, same_expert = sb("r_same_token", [P, T, E]), sb("r_same_expert", [P, E, T])
        total, slot_f = sb("r_total", [P, T]), sb("r_slot_f", [P, E * T])
        tile_i, tile_f = sb("r_tile_i", [P, E * T], I32), sb("r_tile_f", [P, E * T])
        cnt, steps_f, base_f, ones_e = sb("r_cnt", [P, E]), sb("r_steps_f", [P, E]), sb("r_base_f", [P, E]), sb("r_ones_e", [P, E])
        cnt_i = sb("r_cnt_i", [P, E], I32)
        most, most_all = sb("r_most", [P, 1]), sb("r_most_all", [P, 1])
        before, ones = sb("r_before", [P, P]), sb("r_ones", [P, P])
        slots = sb("r_slots", [P, E * T], I32)
        entries = sb("r_entries", [P, E * T, 2], I32)
        token = sb("r_token", [P, T], I32)
        blank = sb("r_blank", [P, TILES, 2], I32)
        zeros = sb("r_zeros", [P, 17 * D])
        br = sb("r_br", [P, E])
        sl = [sb(f"r_sl{u}", [P, SIDE], I32) for u in range(2)]
        en = [sb(f"r_en{u}", [P, SIDE, 2], I32) for u in range(2)]
        ps_in, ps_tot = (ctx.enter_context(nc.psum_tensor(f"r_ps{j}", [P, 512], F32)) for j in range(2))
        cleared, filled, br_in, exped, order, mask_ready, counted, slots_ready, consts, most_ready, most_done, moved = (
            sem("r_" + x) for x in ("cleared", "filled", "br_in", "exped", "order", "mask_ready", "counted",
                                    "slots_ready", "consts", "most_ready", "most_done", "moved"))
        scattered = [sem(f"r_scattered{u}") for u in range(2)]
        with nc.Block() as block:
            @block.sync
            def _(sp):
                sp.dma_start(br[:], K["br"].rearrange("(o e) -> o e", o=1).partition_broadcast(P).rearrange("p o e -> p (o e)")).then_inc(br_in, 16)
                sp.wait_ge(cleared, 2)
                rows = K["mixed"].rearrange("(p a) d -> p (a d)", p=P)
                for j in range(2):
                    sp.dma_start(rows[:, 17 * D * j:17 * D * (j + 1)], zeros[:]).then_inc(filled, 16)
                sp.dma_start(K["h_rows"][B * S:B * S + STEP, :].rearrange("(a p) d -> p a d", p=P),
                             zeros[:, 0:2 * D].rearrange("p (a d) -> p a d", a=2)).then_inc(filled, 16)
                sp.dma_start(K["table"].rearrange("(p a) c -> p a c", p=P), blank[:]).then_inc(filled, 16)
                for e in range(2):
                    wait(sp, K["w_ready"], e)
                    load_expert(sp, K, e)
                sp.wait_ge(filled, 64)

            @block.scalar
            def _(act):
                act.wait_ge(mask_ready, 1)
                nc.scalar.activation(ex[:], ex[:], ACT.Exp).then_inc(exped, 1)

            @block.tensor
            def _(pe):
                pe.wait_ge(mask_ready, 1)
                pe.wait_ge(consts, 6)
                flat = mask[:].rearrange("p t e -> p (t e)")
                nc.tensor.matmul(ps_in[:, 0:n], before[:], flat, start=True, stop=True).then_inc(counted, 1)
                nc.tensor.matmul(ps_tot[:, 0:n], ones[:], flat, start=True, stop=True).then_inc(counted, 1)

            @block.gpsimd
            def _(pool):
                nc.gpsimd.memset(zeros[:], 0.0).then_inc(cleared, 1)
                nc.gpsimd.memset(blank[:], 0).then_inc(consts, 1)
                pool.wait_ge(consts, 1)
                nc.gpsimd.iota(blank[:, :, 0], [[P, TILES]], base=0, channel_multiplier=1).then_inc(consts, 1)
                nc.gpsimd.memset(before[:], 1.0).then_inc(consts, 1)
                nc.gpsimd.memset(ones[:], 1.0).then_inc(consts, 1)
                nc.gpsimd.iota(token[:], [[P, T]], base=0, channel_multiplier=1).then_inc(consts, 1)
                pool.wait_ge(consts, 5)
                nc.gpsimd.affine_select(out=before[:], in_=before[:], compare_op=ALU.is_gt, fill=0.0, base=0,
                                        pattern=[[1, P]], channel_multiplier=-1).then_inc(consts, 1)
                pool.wait_ge(most_ready, 1)
                pool.partition_all_reduce(most_all[:], most[:], P, bass.bass_isa.ReduceOp.max).then_inc(most_done, 1)
                pool.wait_ge(slots_ready, 1)
                pool.wait_ge(filled, 64)

                def body(j):
                    for u in range(2):
                        wait(pool, scattered[u], 16 * SIDE * j)
                        c0 = (2 * j + u) * SIDE
                        hold(pool, K)
                        nc.gpsimd.tensor_copy(sl[u][:], slots[:, bass.ds(c0, SIDE)]).then_inc(moved, 1)
                        nc.gpsimd.tensor_copy(en[u][:], entries[:, bass.ds(c0, SIDE), :]).then_inc(moved, 1)
                        pool.wait_ge(moved, 4 * j + 2 * u + 2)
                        hold(pool, K)
                        for i in range(SIDE):
                            pool.indirect_dma_start(K["table"], bass.IndirectOffsetOnAxis(ap=sl[u][:, i:i + 1], axis=0), en[u][:, i, :],
                                                    None, bounds_check=P * TILES - 1, oob_is_err=False).then_inc(scattered[u], 16)
                pairs = T // SIDE // 2
                body(0)
                with pool.Fori(1, 2 * pairs) as j:
                    body(j)
                pool.wait_ge(slots_ready, 2)
                ranks = pool.value_load(K["ranks"][0:1, 0:1], min_val=2, max_val=E)
                with pool.If(ranks > 2):
                    with pool.Fori(2 * pairs, ranks * pairs) as j:
                        body(j)
                for u in range(2):
                    pool.wait_ge(scattered[u], ranks * (16 * SIDE * pairs))
                hold(pool, K)

            @block.vector
            def _(dve):
                ord_ = Order(dve, order, 0)
                link = ord_.link
                fl = lambda t: t[:].rearrange("p a b -> p (a b)")
                nc.vector.memset(same_token[:], 1.0)
                nc.vector.memset(same_expert[:], 1.0)
                link(nc.vector.memset(ones_e[:], 1.0))
                nc.vector.memset(same_token[:, :, 0], 0.0)
                link(nc.vector.memset(same_expert[:, :, 0], 0.0))
                dve.wait_ge(consts, 2)
                link(nc.vector.tensor_scalar(blank[:, :, 0], blank[:, :, 0], STEP - 1, B * S, ALU.bitwise_and, ALU.bitwise_or))
                dve.sem_inc(cleared, 1)
                dve.wait_ge(br_in, 16)
                link(nc.vector.tensor_tensor(lg[:], K["logits"][:], br[:].rearrange("p (o e) -> p o e", o=1).to_broadcast([P, T, E]), ALU.add))
                for t in range(T):
                    last = nc.vector.max(top[:, t, :], lg[:, t, :])
                link(last)
                link(nc.vector.tensor_tensor(ex[:], lg[:], top[:, :, 0:1].to_broadcast([P, T, E]), ALU.subtract))
                nc.vector.tensor_tensor(mask[:], lg[:], top[:, :, 1:2].to_broadcast([P, T, E]), ALU.is_ge).then_inc(mask_ready, 1)
                dve.wait_ge(mask_ready, 1)
                link(nc.vector.tensor_tensor_scan(fl(rank), fl(same_token), fl(mask), 0.0, ALU.mult, ALU.add))
                link(nc.vector.tensor_reduce(most[:], rank[:, :, E - 1], AX.X, ALU.max))
                dve.sem_inc(most_ready, 1)
                dve.wait_ge(exped, 1)
                link(nc.vector.tensor_tensor(ex[:], ex[:], mask[:], ALU.mult))
                link(nc.vector.tensor_reduce(total[:], ex[:], AX.X, ALU.add))
                link(nc.vector.reciprocal(total[:], total[:]))
                link(nc.vector.tensor_tensor(gate[:], ex[:], total[:].rearrange("p (t o) -> p t o", o=1).to_broadcast([P, T, E]), ALU.mult))
                dve.wait_ge(counted, 2)
                link(nc.vector.tensor_copy(tot[:], ps_tot[:, 0:n].rearrange("p (t e) -> p e t", e=E)))
                link(nc.vector.tensor_tensor_scan(fl(run), fl(same_expert), fl(tot), 0.0, ALU.mult, ALU.add))
                link(nc.vector.tensor_scalar(cnt[:], run[:, :, T - 1], 1.0, float(STEP - 1), ALU.max, ALU.add))
                link(nc.vector.tensor_copy(cnt_i[:], cnt[:]))
                link(nc.vector.tensor_scalar(K["steps"][:], cnt_i[:], 8, None, ALU.logical_shift_right))
                link(nc.vector.tensor_copy(steps_f[:], K["steps"][:]))
                link(nc.vector.tensor_tensor_scan(base_f[:], ones_e[:], steps_f[:], 0.0, ALU.mult, ALU.add))
                link(nc.vector.tensor_tensor(base_f[:], base_f[:], steps_f[:], ALU.subtract))
                link(nc.vector.tensor_copy(K["base"][:], base_f[:]))
                link(nc.vector.scalar_tensor_tensor(steps_f[:], steps_f[:], -1.0, base_f[:], ALU.add, ALU.add))
                link(nc.vector.tensor_copy(K["final"][:], steps_f[:]))
                link(nc.vector.tensor_tensor(run[:], run[:], tot[:], ALU.subtract))
                link(nc.vector.tensor_scalar(base_f[:], base_f[:], float(STEP), -NOWHERE, ALU.mult, ALU.add))
                link(nc.vector.tensor_tensor(run[:], run[:], base_f[:].rearrange("p (e o) -> p e o", o=1).to_broadcast([P, E, T]), ALU.add))
                link(nc.vector.tensor_tensor(pos[:], ps_in[:, 0:n].rearrange("p (t e) -> p t e", e=E), run[:].rearrange("p e t -> p t e"), ALU.add))
                for first, last in ((0, 2), (2, E)):
                    for r in range(first, last):
                        cols = slice(T * r, T * r + T)
                        link(nc.vector.scalar_tensor_tensor(sel[:], rank[:], float(r + 1), mask[:], ALU.is_equal, ALU.mult))
                        link(nc.vector.tensor_tensor(tmp[:], sel[:], pos[:], ALU.mult))
                        link(nc.vector.tensor_reduce(slot_f[:, cols], tmp[:], AX.X, ALU.add))
                        link(nc.vector.tensor_tensor(tmp[:], sel[:], gate[:], ALU.mult))
                        link(nc.vector.tensor_reduce(entries[:, cols, 1].bitcast(F32), tmp[:], AX.X, ALU.add))
                        link(nc.vector.tensor_copy(entries[:, cols, 0], token[:]))
                    cols = slice(T * first, T * last)
                    s_f, s_i, t_f, t_i = (t[:, cols] for t in (slot_f, slots, tile_f, tile_i))
                    link(nc.vector.tensor_scalar(s_f, s_f, NOWHERE, None, ALU.add))
                    link(nc.vector.tensor_copy(s_i, s_f))
                    link(nc.vector.tensor_scalar(t_i, s_i, 7, None, ALU.logical_shift_right))
                    link(nc.vector.tensor_copy(t_f, t_i))
                    link(nc.vector.scalar_tensor_tensor(s_f, t_f, -float(P), s_f, ALU.mult, ALU.add))
                    link(nc.vector.scalar_tensor_tensor(s_f, s_f, float(TILES), t_f, ALU.mult, ALU.add))
                    link(nc.vector.tensor_copy(s_i, s_f))
                    if first == 0:
                        dve.sem_inc(slots_ready, 1)
                dve.wait_ge(most_done, 1)
                link(nc.vector.tensor_scalar(K["ranks"][:], most_all[:], 2.0, None, ALU.max))
                dve.sem_inc(slots_ready, 1)
                for e in range(2):
                    split_expert(nc, dve, K, e, e)


def experts(nc, K):
    with ExitStack() as ctx:
        sb = lambda name, shape, dt=F32: ctx.enter_context(nc.sbuf_tensor(name, shape, dt))
        sem = nc.alloc_semaphore
        two = range(2)
        table = sb("e_table", [P, TILES, 2], I32)
        w1_hi, w1_lo, w2_hi, w2_lo = K["ew1_hi"], K["ew1_lo"], K["ew2_hi"], K["ew2_lo"]
        b1 = [sb(f"e_b1{p}", [P, 8]) for p in two]
        b2 = [sb(f"e_b2{p}", [P, D]) for p in two]
        rows, cur = sb("e_rows", [P, 2, 2], I32), sb("e_cur", [P, 2, 2], I32)
        xg = sb("e_xg", [P, 2, D])
        xf = sb("e_xf", [P, NC, STEP])
        x_hi, x_lo = sb("e_x_hi", [P, NC, STEP], F32R), sb("e_x_lo", [P, NC, STEP], F32R)
        gf = sb("e_gf", [P, 8, STEP])
        g_hi, g_lo = sb("e_g_hi", [P, 8, STEP], F32R), sb("e_g_lo", [P, 8, STEP], F32R)
        yb, yv = sb("e_yb", [P, 2, D]), sb("e_yv", [P, 2, D])
        ps_t = ctx.enter_context(nc.psum_tensor("e_ps_t", [P, 512], F32))
        ps_y = ctx.enter_context(nc.psum_tensor("e_ps_y", [P, 512], F32))
        ps_h = [ctx.enter_context(nc.psum_tensor(f"e_ps_h{j}", [P, 512], F32)) for j in range(4)]
        names = """gathered picked transposed xf_ready x_hi_ready x_ready hid_ps gelu_ready g_hi_ready g_ready g_used yb_ready
                   yv_ready scattered weights_used""".split()
        Z = {n: sem("e_" + n) for n in names}
        Z["bias_in"] = [sem(f"e_bias_in{p}") for p in two]

        def step_range(eng, e):
            steps = eng.value_load(K["steps"][0:1, bass.ds(e, 1)], min_val=1, max_val=B * S // STEP)
            base = eng.value_load(K["base"][0:1, bass.ds(e, 1)], min_val=0, max_val=STEPS - B * S // STEP)
            final = eng.value_load(K["final"][0:1, bass.ds(e, 1)], min_val=0, max_val=STEPS - 1)
            return base, steps, final

        def slots_of(eng, e, p, slot, last=False, before_final=None):
            base, steps, final = step_range(eng, e)
            with eng.If(steps > 1):
                with eng.Fori(0, steps - 1) as i:
                    slot(base + i, p, p)
            if before_final:
                before_final()
            slot(final, p, None if last else 1 - p)

        with nc.Block() as block:
            @block.sync
            def _(sp):
                with sp.Fori(2, E) as e:
                    sp.wait_ge(K["w_ready"], e)
                    load_expert(sp, K, e)

            @block.gpsimd
            def _(pool):
                def gather(g, picked):
                    nc.gpsimd.tensor_copy(rows[:], table[:, bass.ds(2 * g, 2), :]).then_inc(Z["picked"], 1)
                    pool.wait_ge(Z["picked"], picked)
                    hold(pool, K)
                    for s in two:
                        pool.indirect_dma_start(xg[:, s, :], None, K["h_rows"], bass.IndirectOffsetOnAxis(ap=rows[:, s, 0:1], axis=0)
                                                ).then_inc(Z["gathered"], 16)

                for half in two:
                    pool.dma_start(table[:, half * (TILES // 2):(half + 1) * (TILES // 2), :],
                                   K["table"].rearrange("(p a) c -> p a c", p=P)[:, half * (TILES // 2):(half + 1) * (TILES // 2), :]
                                   ).then_inc(Z["scattered"], 16)
                pool.wait_ge(Z["scattered"], 32)
                gather(0, 1)
                pool.wait_ge(Z["transposed"], 1)
                gather(1, 2)
                pool.wait_ge(Z["transposed"], 2)
                gather(2, 3)

                def slot(g, p, q):
                    if q is not None:
                        pool.wait_ge(Z["transposed"], g + 3)
                        hold(pool, K)
                        gather(g + 3, 2 * g + 4)
                    pool.wait_ge(Z["scattered"], 32 * (g + 1))
                    hold(pool, K)
                    nc.gpsimd.tensor_copy(cur[:], table[:, bass.ds(2 * g, 2), :]).then_inc(Z["picked"], 1)
                    pool.wait_ge(Z["picked"], 2 * g + (4 if q is None else 5))
                    pool.wait_ge(Z["yv_ready"], g + 2)
                    hold(pool, K)
                    for s in two:
                        pool.indirect_dma_start(K["mixed"], bass.IndirectOffsetOnAxis(ap=cur[:, s, 0:1], axis=0), yv[:, s, :],
                                                None, compute_op=ALU.add).then_inc(Z["scattered"], 16)
                    if q is None:
                        pool.wait_ge(Z["scattered"], 32 * (g + 2))
                        hold(pool, K)

                def body(it, last=False):
                    for p in two:
                        slots_of(pool, 2 * it + p, p, slot, last and p == 1)
                body(0)
                with pool.Fori(1, E // 2 - 1) as it:
                    body(it)
                body(E // 2 - 1, last=True)

            @block.scalar
            def _(act):
                def biases(e, p):
                    act.dma_start(b1[p][:], K["eb1"][bass.ds(e, 1)].rearrange("o p m -> (o p) m")).then_inc(Z["bias_in"][p], 16)
                    act.dma_start(b2[p][:], K["eb2"][bass.ds(e, 1), :].partition_broadcast(P).rearrange("p o d -> p (o d)")).then_inc(Z["bias_in"][p], 16)

                def take_rows(g):
                    act.wait_ge(Z["transposed"], g + 1)
                    wait(act, Z["x_ready"], g)
                    nc.scalar.activation(xf[:], ps_t[:].rearrange("p (c n) -> p c n", c=NC), ACT.Copy).then_inc(Z["xf_ready"], 1)

                def gelu(g, q):
                    for k in range(4):
                        act.wait_ge(Z["hid_ps"], g * 4 + (k + 5))
                        wait(act, Z["g_ready"], g * 4 + (k + 1))
                        for m in (2 * k, 2 * k + 1):
                            ins = nc.scalar.activation(gf[:, m], ps_h[k][:, (m % 2) * STEP:(m % 2) * STEP + STEP],
                                                       ACT.Gelu, bias=b1[q][:, m:m + 1])
                        ins.then_inc(Z["gelu_ready"], 1)

                biases(0, 0)
                act.sem_inc(Z["yv_ready"], 1)
                take_rows(0)
                act.wait_ge(Z["bias_in"][0], 32)
                gelu(-1, 0)
                take_rows(1)

                def slot(g, p, q):
                    if q is not None:
                        gelu(g, q)
                        take_rows(g + 2)
                    act.wait_ge(Z["picked"], 2 * g + (4 if q is None else 5))
                    act.wait_ge(Z["yb_ready"], g + 2)
                    for s in two:
                        ins = nc.scalar.activation(yv[:, s], yb[:, s], ACT.Copy, scale=cur[:, s, 1:2].bitcast(F32))
                    ins.then_inc(Z["yv_ready"], 1)

                def body(it, last=False):
                    for p in two:
                        e = 2 * it + p
                        final = last and p == 1
                        if not final:
                            biases(e + 1, 1 - p)
                            act.wait_ge(Z["bias_in"][1 - p], 32 * (it + p + 1))
                            hold(act, K)
                        slots_of(act, e, p, slot, final)
                body(0)
                with act.Fori(1, E // 2 - 1) as it:
                    body(it)
                body(E // 2 - 1, last=True)

            @block.vector
            def _(dve):
                def split_rows(g):
                    dve.wait_ge(Z["xf_ready"], g + 1)
                    wait(dve, Z["hid_ps"], 4 * g)
                    nc.vector.tensor_copy(x_hi[:], xf[:]).then_inc(Z["x_hi_ready"], 1)
                    dve.wait_ge(Z["x_hi_ready"], g + 1)
                    nc.vector.tensor_tensor(x_lo[:], xf[:], x_hi[:].bitcast(F32), ALU.subtract).then_inc(Z["x_ready"], 1)

                def split_hidden(g, k):
                    n = g * 4 + (k + 5)
                    dve.wait_ge(Z["gelu_ready"], n)
                    wait(dve, Z["g_used"], g * 4 + (k + 1))
                    nc.vector.tensor_copy(g_hi[:, 2 * k:2 * k + 2], gf[:, 2 * k:2 * k + 2]).then_inc(Z["g_hi_ready"], 1)
                    dve.wait_ge(Z["g_hi_ready"], n)
                    nc.vector.tensor_tensor(g_lo[:, 2 * k:2 * k + 2], gf[:, 2 * k:2 * k + 2], g_hi[:, 2 * k:2 * k + 2].bitcast(F32),
                                            ALU.subtract).then_inc(Z["g_ready"], 1)

                dve.sem_inc(Z["yb_ready"], 1)
                split_rows(0)
                for k in range(4):
                    split_hidden(-1, k)
                split_rows(1)

                def slot(g, p, q):
                    for k in range(4):
                        if q is not None:
                            split_hidden(g, k)
                            if k == 1:
                                split_rows(g + 2)
                    dve.wait_ge(Z["g_used"], 4 * (g + 1))
                    dve.wait_ge(Z["yv_ready"], g + 1)
                    nc.vector.tensor_tensor(yb[:], ps_y[:].rearrange("p (s d) -> p s d", s=2),
                                            b2[p][:].rearrange("p (o d) -> p o d", o=1).to_broadcast([P, 2, D]), ALU.add
                                            ).then_inc(Z["yb_ready"], 1)

                def body(it, last=False):
                    for p in two:
                        e = 2 * it + p
                        final = last and p == 1
                        if not final and not (isinstance(e, int) and e == 0):
                            dve.wait_ge(Z["weights_used"], e)
                            split_expert(nc, dve, K, e + 1, 1 - p)
                        dve.wait_ge(Z["bias_in"][p], 32 * (it + 1))
                        hold(dve, K)
                        slots_of(dve, e, p, slot, final)
                body(0)
                with dve.Fori(1, E // 2 - 1) as it:
                    body(it)
                body(E // 2 - 1, last=True)

            @block.tensor
            def _(pe):
                def transposes(g):
                    pe.wait_ge(Z["gathered"], 32 * (g + 1))
                    wait(pe, Z["xf_ready"], g)
                    for c in range(NC):
                        for s in two:
                            last = nc.tensor.transpose(ps_t[:, c * STEP + s * P:c * STEP + (s + 1) * P], xg[:, s, c * P:(c + 1) * P], K["ident"][:])
                    last.then_inc(Z["transposed"], 1)

                def hidden(g, q):
                    pe.wait_ge(Z["x_ready"], g + 2)
                    for m in range(8):
                        if m % 2 == 0:
                            wait(pe, Z["gelu_ready"], g * 4 + (m // 2 + 1))
                        n = 0
                        for c in range(NC):
                            for w, a in ((w1_hi, x_hi), (w1_hi, x_lo), (w1_lo, x_hi)):
                                last = nc.tensor.matmul(ps_h[m // 2][:, (m % 2) * STEP:(m % 2) * STEP + STEP],
                                                        w[q][:, c, m * P:(m + 1) * P], a[:, c], start=(n == 0), stop=(n == 5))
                                n += 1
                        if m % 2:
                            last.then_inc(Z["hid_ps"], 1)

                transposes(0)
                pe.wait_ge(K["w_ready"], 1)
                hidden(-1, 0)
                transposes(1)

                def slot(g, p, q):
                    if q is not None:
                        hidden(g, q)
                    pe.wait_ge(Z["yb_ready"], g + 1)
                    for k in range(4):
                        pe.wait_ge(Z["g_ready"], g * 4 + (k + 1))
                        for s in two:
                            n = 0
                            for c in (2 * k, 2 * k + 1):
                                for a, w in ((g_hi, w2_hi), (g_lo, w2_hi), (g_hi, w2_lo)):
                                    last = nc.tensor.matmul(ps_y[:, s * D:(s + 1) * D], a[:, c, s * P:(s + 1) * P], w[p][:, c, :],
                                                            start=(k == s == n == 0), stop=(k == 3 and s == 1 and n == 5), skip_group_check=True)
                                    n += 1
                        last.then_inc(Z["g_used"], 1)
                        if k == 1 and q is not None:
                            transposes(g + 2)

                def body(it, last=False):
                    for p in two:
                        e = 2 * it + p
                        final = last and p == 1

                        def next_weights():
                            pe.wait_ge(K["w_ready"], e + 2)
                            hold(pe, K)
                        slots_of(pe, e, p, slot, final, None if final else next_weights)
                        pe.drain().then_inc(Z["weights_used"], 1)
                body(0)
                with pe.Fori(1, E // 2 - 1) as it:
                    body(it)
                body(E // 2 - 1, last=True)


def finish(nc, K):
    with ExitStack() as ctx:
        sb = lambda name, shape, dt=F32: ctx.enter_context(nc.sbuf_tensor(name, shape, dt))
        sem = nc.alloc_semaphore
        acc = sb("f_acc", [P, T, D])
        gb = sb("f_gb", [P, B, D])
        pairs = range(B // 2)
        loaded = [sem(f"f_loaded{k}") for k in pairs]
        summed, stored = sem("f_summed"), sem("f_stored")
        tiles = lambda b: slice(b * NT, (b + 1) * NT)
        rows = lambda t, k: t[2 * k * S:2 * (k + 1) * S, :].rearrange("(i p) d -> p i d", p=P)
        with nc.Block() as block:
            @block.sync
            def _(sp):
                sp.dma_start(gb[:], K["mod_rows"][:, ROWS.index((1, 5)), :].partition_broadcast(P)).then_inc(loaded[0], 16)
                for k in pairs:
                    sp.dma_start(acc[:, 2 * k * NT:2 * (k + 1) * NT, :], rows(K["mixed"], k)).then_inc(loaded[k], 16)

            @block.scalar
            def _(act):
                for b in range(B):
                    act.wait_ge(summed, 2 * (b + 1))
                    act.dma_start(K["out"][b].rearrange("(i p) d -> p i d", p=P), acc[:, tiles(b), :]).then_inc(stored, 16)
                act.wait_ge(stored, 16 * B)

            @block.vector
            def _(dve):
                for b in range(B):
                    if b % 2 == 0:
                        dve.wait_ge(loaded[b // 2], 32 if b == 0 else 16)
                    nc.vector.tensor_tensor(acc[:, tiles(b), :], acc[:, tiles(b), :], gb[:, b:b + 1, :].to_broadcast([P, NT, D]),
                                            ALU.mult).then_inc(summed, 1)
                    dve.wait_ge(summed, 2 * b + 1)
                    nc.vector.tensor_tensor(acc[:, tiles(b), :], acc[:, tiles(b), :], K["x_sb"][:, tiles(b), :], ALU.add).then_inc(summed, 1)


def lay_out(a):
    t = lambda x: np.ascontiguousarray(np.swapaxes(x, 0, 1))
    col = lambda x: np.ascontiguousarray(x.reshape(-1, P).T)
    cols = lambda c: np.ascontiguousarray(c.reshape(B, NC, P).transpose(2, 1, 0))
    return {
        "x": a["L0_attn_h"], "ct0": cols(a["L0_c"]), "ct1": cols(a["L1_c"]), "wmod0": a["L0_wmod"], "wmod1": a["L1_wmod"],
        "wqkv": a["L0_attn_Wqvk"], "wo": a["L0_attn_Wo"],
        "w0t": t(a["L0_ffn_weight"]), "a1": a["L0_ffn_aux_weight1"], "a2": a["L0_ffn_aux_weight2"], "bias0": a["L0_ffn_bias"],
        "win": t(a["L1_attn_in_proj_w"]), "opt": t(a["L1_attn_out_proj_w"]), "coupling": a["L1_attn_coupling"],
        "freq": a["L1_attn_frequency"].reshape(KS, 1), "decay": a["L1_attn_log_decay"].reshape(KS, 1),
        "gate_wt": t(a["L1_attn_gate_w"]), "gate_b": a["L1_attn_gate_b"], "w1t": t(a["L1_attn_mlp_w1"]), "w2t": t(a["L1_attn_mlp_w2"]),
        "b1": col(a["L1_attn_mlp_b1"]), "b2": a["L1_attn_mlp_b2"], "n1g": col(a["L1_attn_n1_g"]), "n1b": col(a["L1_attn_n1_b"]),
        "n2g": col(a["L1_attn_n2_g"]), "n2b": col(a["L1_attn_n2_b"]), "wr": a["L1_ffn_Wr"],
        "br": a["L1_ffn_br"], "ew1": a["L1_ffn_W1"], "ew2": a["L1_ffn_W2"], "eb2": a["L1_ffn_b2"],
        "eb1": np.ascontiguousarray(a["L1_ffn_b1"].reshape(E, 8, P).swapaxes(1, 2)),
    }
def adaln_two_layers(nc, I, out):
    with ExitStack() as ctx:
        sb = lambda name, shape, dt=F32: ctx.enter_context(nc.sbuf_tensor(name, shape, dt))
        dram = lambda name, shape, dt=F32: nc.dram_tensor(name, shape, dt, kind="Internal").ap()
        K = dict(I)
        K["x_sb"] = sb("x_sb", [P, T, D])
        K["logits"] = sb("logits", [P, T, 8])
        K["mod_cols"] = sb("mod_cols", [P, 12, B])
        K["ident"] = sb("ident", [P, P])
        K["identb"] = sb("identb", [P, P], BF16)
        K["mod_rows"] = dram("mod_rows", [B, len(ROWS), D])
        K["qk_parts"] = dram("qk_parts", [B * G * 2, 3, HD, 4, S], BF16)
        K["attended"] = dram("attended", [B * G * P, S])
        K["inverse"] = dram("inverse", [P, S])
        K["h_rows"] = dram("h_rows", [B * S + STEP, D])
        K["mixed"] = dram("mixed", [B * S + STEP, D])
        K["table"] = dram("table", [P * TILES, 2], I32)
        K["steps"] = sb("steps", [P, E], I32)
        K["base"] = sb("base", [P, E], I32)
        K["final"] = sb("final", [P, E], I32)
        K["ranks"] = sb("ranks", [P, 1], I32)
        K["out"] = out
        K["held"] = nc.alloc_semaphore("held")
        with ExitStack() as first:
            K["causal"] = first.enter_context(nc.sbuf_tensor("causal", [P, S], F32))
            K["v"] = first.enter_context(nc.sbuf_tensor("v_sb", [P, T, D], F32))
            with ExitStack() as projections:
                for part in ("w_hi", "w_lo"):
                    K[part] = projections.enter_context(nc.sbuf_tensor("qkv_" + part, [P, NC, 3 * D], F32R))
                setup_modulation(nc, K)
                project_qkv(nc, K)
            attend(nc, K)
        with ExitStack() as second:
            W = {}
            for name, shape, dt in (("wo", [P, G, D], F32), ("mt", [P, D], F32), ("mts", [P, D], F32), ("wr", [P, NC, 8], F32),
                                    ("sin", [P, S], F32), ("cos", [P, S], F32), ("mag", [P, S], F32), ("bias0", [P, D], F32),
                                    ("gate_b", [P, D], F32), ("b2", [P, D], F32), ("n1g", [P, NC], F32), ("n1b", [P, NC], F32),
                                    ("n2g", [P, NC], F32), ("n2b", [P, NC], F32), ("b1", [P, 8], F32)):
                W[name] = second.enter_context(nc.sbuf_tensor("w_" + name, shape, dt))
            for name, shape in (("wc", [P, NC, D]), ("win", [P, NC, P]), ("wins", [P, NC, P]), ("gate", [P, NC, D]),
                                ("w1", [P, NC, 4 * D]), ("w2", [P, 8, D])):
                for part in ("_hi", "_lo"):
                    W[name + part] = second.enter_context(nc.sbuf_tensor("w_" + name + part, shape, F32R))
            W["a1"], W["v1"] = (second.enter_context(nc.sbuf_tensor("c_" + n, [P, 4, S], F32)) for n in ("a1", "v1"))
            W["w1"] = W["a1"][:].rearrange("p (c m) s -> p c (m s)", c=NC)
            W["w2"] = W["v1"][:].rearrange("p c (m n) -> p (c m) n", n=D)
            prepare_middle(nc, K, W)
            middle(nc, K, W)
        with ExitStack() as third:
            part = lambda name, shape, dt: third.enter_context(nc.sbuf_tensor(name, shape, dt))
            K["ew1f"], K["ew2f"] = part("ew1f", [P, NC, F], F32), part("ew2f", [P, 8, D], F32)
            for x in ("hi", "lo"):
                K["ew1_" + x] = [part(f"ew1_{x}{p}", [P, NC, F], F32R) for p in range(2)]
                K["ew2_" + x] = [part(f"ew2_{x}{p}", [P, 8, D], F32R) for p in range(2)]
            for name in ("raw_in", "whi_ready", "w_ready"):
                K[name] = nc.alloc_semaphore("e_" + name)
            route(nc, K)
            experts(nc, K)
        finish(nc, K)


def kernel(**inputs):
    import concourse.bacc as bacc
    from concourse.bass_utils import run_bass_kernel_spmd

    arrays = lay_out({name: np.asarray(a) for name, a in inputs.items()})
    arrays = {f"in_{name}_dram": np.ascontiguousarray(a) for name, a in arrays.items()}
    nc = bacc.Bacc("TRN2", target_bir_lowering=False, num_devices=1)
    given = {name[3:-5]: nc.dram_tensor(name, a.shape, mybir.dt.from_np(a.dtype), kind="ExternalInput").ap()
             for name, a in arrays.items()}
    out = nc.dram_tensor("out_0_dram", (B, S, D), F32, kind="ExternalOutput").ap()
    adaln_two_layers(nc, given, out)
    nc.compile() if not nc.is_finalized() else None
    return run_bass_kernel_spmd(nc, [arrays], core_ids=[0]).results[0]["out_0_dram"]
```
